# Optimizing a Trainium2 kernel written in Bass

```python
import numpy as np
import jax
import jax.numpy as jnp

def _softmax(x, axis=-1):
    return jax.nn.softmax(x, axis=axis)

def _gelu(x):
    return jax.nn.gelu(x, approximate=True)

def _silu(x):
    return jax.nn.silu(x)

def _sigmoid(x):
    return jax.nn.sigmoid(x)

def _layernorm(x, axis=-1, eps=1e-05):
    m = jnp.mean(x, axis=axis, keepdims=True)
    v = jnp.var(x, axis=axis, keepdims=True)
    return (x - m) / jnp.sqrt(v + eps)

def _scatter_add(tgt, idx, src, axis=0):
    return tgt.at[idx].add(src)

def _segment_sum(src, seg, n):
    return jax.ops.segment_sum(src, seg, n)
kernel_name = 'mk_xattn_ffn_d4_seqx_r4_1091df'

def setup_inputs(seed: int=0):
    np.random.seed(seed)
    _w = jnp.asarray

    def _rec_inputs():
        import jax
        import jax.numpy as jnp
        _rk = jax.random.key(seed)
        x = -0.0002928 + 1 * jax.random.normal(jax.random.fold_in(_rk, 1), (16, 128, 256), jnp.float32)
        _lenS = 128 - jax.random.randint(jax.random.fold_in(_rk, 7), (16,), 0, max(1, 128 // 4) + 1, jnp.int32)
        _lenS2 = 128 - jax.random.randint(jax.random.fold_in(_rk, 8), (16,), 0, max(1, 128 // 4) + 1, jnp.int32)
        _ctx_1024P = jax.random.normal(jax.random.fold_in(_rk, 11), (16, 16, 256), jnp.float32)
        _ctx_1024c = jax.random.dirichlet(jax.random.fold_in(_rk, 511), 0.3 * jnp.ones((16,), jnp.float32), (16, 128))
        _ctx_1024t = jnp.einsum('bsk,bkd->bsd', _ctx_1024c, _ctx_1024P)
        _ctx_1024t = _ctx_1024t * jax.lax.rsqrt(jnp.mean(jnp.square(_ctx_1024t)) + 1e-12) * 0.953939
        ctx_1024 = -1.39393e-06 + 0.999914 * (_ctx_1024t + 0.3 * jax.random.normal(jax.random.fold_in(_rk, 611), (16, 128, 256), jnp.float32))
        _validS = jnp.arange(128)[None, :] < _lenS[:, None]
        _validS2 = jnp.arange(128)[None, :] < _lenS2[:, None]
        _causal = jnp.tril(jnp.ones((128, 128), dtype=bool))
        mask_1x1xSxS2_ik0 = jnp.where(jnp.broadcast_to(_validS2[0:1, None, None, :], (1, 1, 128, 128)), 0, 1).astype(jnp.int32)
        mask_BxS2_bk0 = jnp.logical_not(jnp.broadcast_to(_validS2[:, :], (16, 128)))
        return (x, ctx_1024, mask_1x1xSxS2_ik0, mask_BxS2_bk0)
    x, ctx_1024, mask_1x1xSxS2_ik0, mask_BxS2_bk0 = _rec_inputs()

    def _L0_xattn_setup():
        import math
        import jax, jax.numpy as jnp
        import numpy as np
        N_HEAD = 16

        def _slopes(n_head):
            cp2 = 2 ** int(math.floor(math.log2(n_head)))
            slopes = 0.5 ** np.arange(1, cp2 + 1)
            if cp2 < n_head:
                intra = 1.0 / math.sqrt(2.0)
                pair = intra ** np.arange(1, 1 + 2 * (n_head - cp2), 2)
                slopes = np.sort(np.concatenate([slopes, pair]))[::-1]
            return jnp.asarray(slopes, dtype=jnp.float32)

        def _alibi_bias(S):
            d = jnp.arange(S)[:, None] - jnp.arange(S)[None, :]
            return -jnp.maximum(d, 0).astype(jnp.float32)
        key = jax.random.key(seed)
        B, S, D = (2, 512, 256)
        ks = jax.random.split(key, 12)
        f = lambda k, sh: jax.random.normal(k, sh, dtype=jnp.float32)
        inp = {'q': f(ks[0], (B, S, D)), 'k': f(ks[1], (B, S, D)), 'v': f(ks[2], (B, S, D)), 'mask': jnp.tril(jnp.ones((S, S), dtype=jnp.int32))[None, None], 'wq_w': f(ks[3], (D, D)) * 0.02, 'wq_b': f(ks[4], (D,)) * 0.02, 'wk_w': f(ks[5], (D, D)) * 0.02, 'wk_b': f(ks[6], (D,)) * 0.02, 'wv_w': f(ks[7], (D, D)) * 0.02, 'wv_b': f(ks[8], (D,)) * 0.02, 'out_w': f(ks[9], (D, D)) * 0.02, 'out_b': f(ks[10], (D,)) * 0.02}
        return inp
    _L0_xattn_all = _L0_xattn_setup()
    _L0_xattn_in = {k: v for k, v in _L0_xattn_all.items() if k in ('wq_w', 'wq_b', 'wk_w', 'wk_b', 'wv_w', 'wv_b', 'out_w', 'out_b')}
    del _L0_xattn_all

    def _L0_ffn_setup():
        import jax, jax.numpy as jnp
        import numpy as np
        E = 8
        G = 4
        LG = 2
        TOPK = 2
        ROUTE_SCALE = 1.0

        def _grouped_mm(x, w, counts):
            counts = counts.astype(jnp.int32)
            if hasattr(jax.lax, 'ragged_dot'):
                return jax.lax.ragged_dot(x, w, counts)
            offs = jnp.cumsum(counts)
            eid = jnp.searchsorted(offs, jnp.arange(x.shape[0]), side='right')
            oh = jax.nn.one_hot(eid, w.shape[0], dtype=x.dtype)
            return jnp.einsum('nd,ne,edh->nh', x, oh, w)
        key = jax.random.key(seed)
        ks = jax.random.split(key, 8)
        bs, slen, dim, hid, shid = (2, 512, 256, 128, 256)
        std = 0.02
        return {'x': jax.random.normal(ks[0], (bs, slen, dim), jnp.float32), 'w_gate': jax.random.normal(ks[1], (E, dim), jnp.float32) * std, 'w1': jax.random.normal(ks[2], (E, dim, hid), jnp.float32) * std, 'w2': jax.random.normal(ks[3], (E, hid, dim), jnp.float32) * std, 'w3': jax.random.normal(ks[4], (E, dim, hid), jnp.float32) * std, 'sw1': jax.random.normal(ks[5], (shid, dim), jnp.float32) * std, 'sw2': jax.random.normal(ks[6], (dim, shid), jnp.float32) * std, 'sw3': jax.random.normal(ks[7], (shid, dim), jnp.float32) * std, 'expert_bias': jnp.zeros((E,), jnp.float32)}
    _L0_ffn_all = _L0_ffn_setup()
    _L0_ffn_in = {k: v for k, v in _L0_ffn_all.items() if k in ('w_gate', 'w1', 'w2', 'w3', 'sw1', 'sw2', 'sw3', 'expert_bias')}
    del _L0_ffn_all

    def _L1_xattn_setup():
        import jax, jax.numpy as jnp
        import numpy as np
        import math
        NHEADS = 16
        CAUSAL = True
        NEG_INF = -1e+18
        key = jax.random.key(seed)
        kq, kk, kv = jax.random.split(key, 3)
        B, S, D = (4, 2048, 256)
        q = jax.random.normal(kq, (B, S, D), dtype=jnp.float32)
        k = jax.random.normal(kk, (B, S, D), dtype=jnp.float32)
        v = jax.random.normal(kv, (B, S, D), dtype=jnp.float32)
        return {'q': q, 'k': k, 'v': v}
    _L1_xattn_all = _L1_xattn_setup()
    _L1_xattn_in = {k: v for k, v in _L1_xattn_all.items() if k in ()}
    del _L1_xattn_all

    def _L1_ffn_setup():
        import jax, jax.numpy as jnp
        import numpy as np
        TOP_K = 2
        key = jax.random.key(seed)
        k1, k2, k3, k4, k5 = jax.random.split(key, 5)
        B, S, D, F, E = (2, 256, 256, 512, 8)
        return {'x': jax.random.normal(k1, (B, S, D), dtype=jnp.float32), 'router_kernel_DE': jax.random.normal(k2, (D, E), dtype=jnp.float32) * 0.02, 'kernel_gating_EDF': jax.random.normal(k3, (E, D, F), dtype=jnp.float32) * 0.02, 'kernel_up_EDF': jax.random.normal(k4, (E, D, F), dtype=jnp.float32) * 0.02, 'kernel_down_EFD': jax.random.normal(k5, (E, F, D), dtype=jnp.float32) * 0.02}
    _L1_ffn_all = _L1_ffn_setup()
    _L1_ffn_in = {k: v for k, v in _L1_ffn_all.items() if k in ('router_kernel_DE', 'kernel_gating_EDF', 'kernel_up_EDF', 'kernel_down_EFD')}
    del _L1_ffn_all

    def _L2_xattn_setup():
        import jax, jax.numpy as jnp
        import numpy as np
        B, LQ, LKV = (8, 256, 512)
        QDIM, KDIM, HID = (256, 256, 256)
        key = jax.random.key(seed)
        ks = jax.random.split(key, 12)
        s = lambda d: 1.0 / np.sqrt(d)
        return {'query': jax.random.normal(ks[0], (B, LQ, QDIM), jnp.float32), 'key_value': jax.random.normal(ks[1], (B, LKV, KDIM), jnp.float32), 'key_mask': jax.random.randint(ks[2], (B, LKV), 0, 2).astype(bool), 'Wq': jax.random.uniform(ks[3], (QDIM, HID), jnp.float32, -s(QDIM), s(QDIM)), 'bq': jax.random.uniform(ks[4], (HID,), jnp.float32, -s(QDIM), s(QDIM)), 'Wk': jax.random.uniform(ks[5], (KDIM, HID), jnp.float32, -s(KDIM), s(KDIM)), 'bk': jax.random.uniform(ks[6], (HID,), jnp.float32, -s(KDIM), s(KDIM)), 'Wv': jax.random.uniform(ks[7], (KDIM, HID), jnp.float32, -s(KDIM), s(KDIM)), 'bv': jax.random.uniform(ks[8], (HID,), jnp.float32, -s(KDIM), s(KDIM)), 'Wo': jax.random.uniform(ks[9], (HID, QDIM), jnp.float32, -s(HID), s(HID)), 'bo': jax.random.uniform(ks[10], (QDIM,), jnp.float32, -s(HID), s(HID))}
    _L2_xattn_all = _L2_xattn_setup()
    _L2_xattn_in = {k: v for k, v in _L2_xattn_all.items() if k in ('Wq', 'bq', 'Wk', 'bk', 'Wv', 'bv', 'Wo', 'bo')}
    del _L2_xattn_all

    def _L2_ffn_setup():
        import jax, jax.numpy as jnp
        import numpy as np
        INT4_QMAX = 7.0

        def simulate_quantize_int4(w):
            scale = jnp.max(jnp.abs(w)) / INT4_QMAX
            q = jnp.clip(jnp.round(w / scale), -8.0, 7.0)
            return q * scale
        key = jax.random.key(seed)
        k_x, k_w, k_bias, k_a, k_b = jax.random.split(key, 5)
        d_in, features, rank = (256, 256, 16)
        x = jax.random.normal(k_x, (4, 2048, d_in), dtype=jnp.float32)
        kernel = jax.random.normal(k_w, (d_in, features), dtype=jnp.float32)
        bias = jax.random.normal(k_bias, (features,), dtype=jnp.float32)
        a = jax.random.normal(k_a, (d_in, rank), dtype=jnp.float32) * (1.0 / np.sqrt(d_in))
        b = jax.random.normal(k_b, (rank, features), dtype=jnp.float32) * 0.01
        return {'x': x, 'kernel': kernel, 'bias': bias, 'a': a, 'b': b}
    _L2_ffn_all = _L2_ffn_setup()
    _L2_ffn_in = {k: v for k, v in _L2_ffn_all.items() if k in ('kernel', 'bias', 'a', 'b')}
    del _L2_ffn_all

    def _L3_xattn_setup():
        import jax, jax.numpy as jnp
        import numpy as np
        EPS = 0.001
        LEAKY_ALPHA = 0.2

        def layer_norm(x, gamma, beta):
            mu = jnp.mean(x, axis=-1, keepdims=True)
            var = jnp.mean(jnp.square(x - mu), axis=-1, keepdims=True)
            return (x - mu) * jax.lax.rsqrt(var + EPS) * gamma + beta

        def attention_head(x_k, x_v, x_q, Wk, Wq, Wv, use_mask):
            K = x_k @ Wk
            V = x_v @ Wv
            Q = x_q @ Wq
            Lq, Lk = (Q.shape[1], K.shape[1])
            score = jnp.einsum('bqd,bkd->bqk', Q, K) / jnp.sqrt(jnp.float32(Lk))
            if use_mask:
                mask = jnp.triu(jnp.full((Lq, Lk), -jnp.inf, dtype=score.dtype), k=1)
                score = score + mask
            return jax.nn.softmax(score, axis=-1) @ V
        key = jax.random.key(seed)
        ks = jax.random.split(key, 12)
        B, S, D = (8, 512, 256)
        inp = {'inputs': jax.random.normal(ks[0], (B, S, D), jnp.float32), 'context_sequence': jax.random.normal(ks[1], (B, S, D), jnp.float32), 'Wk1': jax.random.normal(ks[2], (D, D), jnp.float32) * 0.01, 'Wq1': jax.random.normal(ks[3], (D, D), jnp.float32) * 0.01, 'Wv1': jax.random.normal(ks[4], (D, D), jnp.float32) * 0.01, 'Wk2': jax.random.normal(ks[5], (D, D), jnp.float32) * 0.01, 'Wq2': jax.random.normal(ks[6], (D, D), jnp.float32) * 0.01, 'Wv2': jax.random.normal(ks[7], (D, D), jnp.float32) * 0.01, 'W1': jax.random.normal(ks[8], (D, D), jnp.float32) * (1.0 / np.sqrt(D)), 'b1': jnp.zeros((D,), jnp.float32), 'W2': jax.random.normal(ks[9], (D, D), jnp.float32) * (1.0 / np.sqrt(D)), 'b2': jnp.zeros((D,), jnp.float32), 'gamma': jnp.ones((D,), jnp.float32), 'beta': jnp.zeros((D,), jnp.float32)}
        return inp
    _L3_xattn_all = _L3_xattn_setup()
    _L3_xattn_in = {k: v for k, v in _L3_xattn_all.items() if k in ('Wk1', 'Wq1', 'Wv1', 'Wk2', 'Wq2', 'Wv2', 'W1', 'b1', 'W2', 'b2', 'gamma', 'beta')}
    del _L3_xattn_all

    def _L3_ffn_setup():
        import jax, jax.numpy as jnp
        import numpy as np
        NUM_EXPERTS = 8
        TOP_K = 2
        DIM = 256
        HIDDEN = 1024
        B, S = (2, 256)
        key = jax.random.key(seed)
        k_x, k_g, k_1, k_2, k_3 = jax.random.split(key, 5)
        s_d = 1.0 / np.sqrt(DIM)
        s_h = 1.0 / np.sqrt(HIDDEN)
        return {'x': jax.random.normal(k_x, (B, S, DIM), dtype=jnp.float32), 'gate_w': jax.random.normal(k_g, (NUM_EXPERTS, DIM), dtype=jnp.float32) * s_d, 'w1': jax.random.normal(k_1, (NUM_EXPERTS, HIDDEN, DIM), dtype=jnp.float32) * s_d, 'w2': jax.random.normal(k_2, (NUM_EXPERTS, DIM, HIDDEN), dtype=jnp.float32) * s_h, 'w3': jax.random.normal(k_3, (NUM_EXPERTS, HIDDEN, DIM), dtype=jnp.float32) * s_d}
    _L3_ffn_all = _L3_ffn_setup()
    _L3_ffn_in = {k: v for k, v in _L3_ffn_all.items() if k in ('gate_w', 'w1', 'w2', 'w3')}
    del _L3_ffn_all
    return {'x': x, 'ctx_1024': ctx_1024, 'mask_1x1xSxS2_ik0': mask_1x1xSxS2_ik0, 'mask_BxS2_bk0': mask_BxS2_bk0, 'L0_xattn_wq_w': _L0_xattn_in['wq_w'], 'L0_xattn_wq_b': _L0_xattn_in['wq_b'], 'L0_xattn_wk_w': _L0_xattn_in['wk_w'], 'L0_xattn_wk_b': _L0_xattn_in['wk_b'], 'L0_xattn_wv_w': _L0_xattn_in['wv_w'], 'L0_xattn_wv_b': _L0_xattn_in['wv_b'], 'L0_xattn_out_w': _L0_xattn_in['out_w'], 'L0_xattn_out_b': _L0_xattn_in['out_b'], 'L0_ffn_w_gate': _L0_ffn_in['w_gate'], 'L0_ffn_w1': _L0_ffn_in['w1'], 'L0_ffn_w2': _L0_ffn_in['w2'], 'L0_ffn_w3': _L0_ffn_in['w3'], 'L0_ffn_sw1': _L0_ffn_in['sw1'], 'L0_ffn_sw2': _L0_ffn_in['sw2'], 'L0_ffn_sw3': _L0_ffn_in['sw3'], 'L0_ffn_expert_bias': _L0_ffn_in['expert_bias'], 'L1_ffn_router_kernel_DE': _L1_ffn_in['router_kernel_DE'], 'L1_ffn_kernel_gating_EDF': _L1_ffn_in['kernel_gating_EDF'], 'L1_ffn_kernel_up_EDF': _L1_ffn_in['kernel_up_EDF'], 'L1_ffn_kernel_down_EFD': _L1_ffn_in['kernel_down_EFD'], 'L2_xattn_Wq': _L2_xattn_in['Wq'], 'L2_xattn_bq': _L2_xattn_in['bq'], 'L2_xattn_Wk': _L2_xattn_in['Wk'], 'L2_xattn_bk': _L2_xattn_in['bk'], 'L2_xattn_Wv': _L2_xattn_in['Wv'], 'L2_xattn_bv': _L2_xattn_in['bv'], 'L2_xattn_Wo': _L2_xattn_in['Wo'], 'L2_xattn_bo': _L2_xattn_in['bo'], 'L2_ffn_kernel': _L2_ffn_in['kernel'], 'L2_ffn_bias': _L2_ffn_in['bias'], 'L2_ffn_a': _L2_ffn_in['a'], 'L2_ffn_b': _L2_ffn_in['b'], 'L3_xattn_Wk1': _L3_xattn_in['Wk1'], 'L3_xattn_Wq1': _L3_xattn_in['Wq1'], 'L3_xattn_Wv1': _L3_xattn_in['Wv1'], 'L3_xattn_Wk2': _L3_xattn_in['Wk2'], 'L3_xattn_Wq2': _L3_xattn_in['Wq2'], 'L3_xattn_Wv2': _L3_xattn_in['Wv2'], 'L3_xattn_W1': _L3_xattn_in['W1'], 'L3_xattn_b1': _L3_xattn_in['b1'], 'L3_xattn_W2': _L3_xattn_in['W2'], 'L3_xattn_b2': _L3_xattn_in['b2'], 'L3_xattn_gamma': _L3_xattn_in['gamma'], 'L3_xattn_beta': _L3_xattn_in['beta'], 'L3_ffn_gate_w': _L3_ffn_in['gate_w'], 'L3_ffn_w1': _L3_ffn_in['w1'], 'L3_ffn_w2': _L3_ffn_in['w2'], 'L3_ffn_w3': _L3_ffn_in['w3']}

def reference(x, ctx_1024, mask_1x1xSxS2_ik0, mask_BxS2_bk0, L0_xattn_wq_w, L0_xattn_wq_b, L0_xattn_wk_w, L0_xattn_wk_b, L0_xattn_wv_w, L0_xattn_wv_b, L0_xattn_out_w, L0_xattn_out_b, L0_ffn_w_gate, L0_ffn_w1, L0_ffn_w2, L0_ffn_w3, L0_ffn_sw1, L0_ffn_sw2, L0_ffn_sw3, L0_ffn_expert_bias, L1_ffn_router_kernel_DE, L1_ffn_kernel_gating_EDF, L1_ffn_kernel_up_EDF, L1_ffn_kernel_down_EFD, L2_xattn_Wq, L2_xattn_bq, L2_xattn_Wk, L2_xattn_bk, L2_xattn_Wv, L2_xattn_bv, L2_xattn_Wo, L2_xattn_bo, L2_ffn_kernel, L2_ffn_bias, L2_ffn_a, L2_ffn_b, L3_xattn_Wk1, L3_xattn_Wq1, L3_xattn_Wv1, L3_xattn_Wk2, L3_xattn_Wq2, L3_xattn_Wv2, L3_xattn_W1, L3_xattn_b1, L3_xattn_W2, L3_xattn_b2, L3_xattn_gamma, L3_xattn_beta, L3_ffn_gate_w, L3_ffn_w1, L3_ffn_w2, L3_ffn_w3):
    import jax
    import jax.numpy as jnp

    def _L0_xattn_ref(q, k, v, mask, wq_w, wq_b, wk_w, wk_b, wv_w, wv_b, out_w, out_b):
        import math
        import jax, jax.numpy as jnp
        import numpy as np
        N_HEAD = 16

        def _slopes(n_head):
            cp2 = 2 ** int(math.floor(math.log2(n_head)))
            slopes = 0.5 ** np.arange(1, cp2 + 1)
            if cp2 < n_head:
                intra = 1.0 / math.sqrt(2.0)
                pair = intra ** np.arange(1, 1 + 2 * (n_head - cp2), 2)
                slopes = np.sort(np.concatenate([slopes, pair]))[::-1]
            return jnp.asarray(slopes, dtype=jnp.float32)

        def _alibi_bias(S):
            d = jnp.arange(S)[:, None] - jnp.arange(S)[None, :]
            return -jnp.maximum(d, 0).astype(jnp.float32)
        B, S, D = q.shape
        H = N_HEAD
        hd = D // H
        lin = lambda x, w, b: x @ w.T + b
        split = lambda x: x.reshape(B, S, H, hd).transpose(0, 2, 1, 3)
        wq = split(lin(q, wq_w, wq_b))
        wk = split(lin(k, wk_w, wk_b))
        wv = split(lin(v, wv_w, wv_b))
        qk = jnp.einsum('bhsd,bhtd->bhst', wq, wk)
        alibi = _alibi_bias(S)[None, :, :] * _slopes(H)[:, None, None]
        attn = qk + alibi[None]
        attn = jnp.where(mask == 0, jnp.float32(-1000000000.0), attn)
        attn = jax.nn.softmax(attn, axis=-1)
        out = jnp.einsum('bhst,bhtd->bhsd', attn, wv)
        out = out.transpose(0, 2, 1, 3).reshape(B, S, D)
        return lin(out, out_w, out_b)

    def _L0_ffn_ref(x, w_gate, w1, w2, w3, sw1, sw2, sw3, expert_bias):
        import jax, jax.numpy as jnp
        import numpy as np
        E = 8
        G = 4
        LG = 2
        TOPK = 2
        ROUTE_SCALE = 1.0

        def _grouped_mm(x, w, counts):
            counts = counts.astype(jnp.int32)
            if hasattr(jax.lax, 'ragged_dot'):
                return jax.lax.ragged_dot(x, w, counts)
            offs = jnp.cumsum(counts)
            eid = jnp.searchsorted(offs, jnp.arange(x.shape[0]), side='right')
            oh = jax.nn.one_hot(eid, w.shape[0], dtype=x.dtype)
            return jnp.einsum('nd,ne,edh->nh', x, oh, w)
        bs, slen, dim = x.shape
        xf = x.reshape(-1, dim)
        N = xf.shape[0]
        logits = xf @ w_gate.T
        scores = jax.nn.softmax(logits.astype(jnp.float32), axis=-1)
        original = scores
        s = (scores + expert_bias).reshape(N, G, E // G)
        group_scores = jax.lax.top_k(s, 2)[0].sum(-1)
        top_groups = jax.lax.top_k(group_scores, LG)[1]
        keep = jnp.zeros((N, G), bool).at[jnp.arange(N)[:, None], top_groups].set(True)
        masked = jnp.where(keep[:, :, None], s, -jnp.inf).reshape(N, E)
        topk_idx = jax.lax.top_k(masked, TOPK)[1]
        weights = (jnp.take_along_axis(original, topk_idx, axis=1) * ROUTE_SCALE).astype(x.dtype)
        counts = jnp.bincount(topk_idx.reshape(-1), length=E)
        flat_idx = topk_idx.reshape(-1)
        routed_in = xf[flat_idx]
        routed_in = (routed_in.astype(jnp.float32) * weights.reshape(-1, 1)).astype(x.dtype)
        h = jax.nn.silu(_grouped_mm(routed_in, w1, counts)) * _grouped_mm(routed_in, w3, counts)
        routed_out = _grouped_mm(h, w2, counts)
        shared = jax.nn.silu(xf @ sw1.T) * (xf @ sw3.T) @ sw2.T
        out = shared.at[flat_idx].add(routed_out)
        return out.reshape(bs, slen, dim)

    def _L1_xattn_ref(q, k, v):
        import jax, jax.numpy as jnp
        import numpy as np
        import math
        NHEADS = 16
        CAUSAL = True
        NEG_INF = -1e+18
        B, S, D = q.shape
        hd = D // NHEADS
        qh = q.reshape(B, S, NHEADS, hd)
        kh = k.reshape(B, S, NHEADS, hd)
        vh = v.reshape(B, S, NHEADS, hd)
        scores = jnp.einsum('bsqd,bskd->bsqk', qh, kh) / math.sqrt(hd)
        if CAUSAL:
            mask = jnp.tril(jnp.ones((NHEADS, NHEADS), dtype=bool))
            scores = jnp.where(mask, scores, jnp.asarray(NEG_INF, scores.dtype))
        attn = jax.nn.softmax(scores, axis=-1)
        out = jnp.einsum('bsqk,bskd->bsqd', attn, vh)
        return out.reshape(B, S, D)

    def _L1_ffn_ref(x, router_kernel_DE, kernel_gating_EDF, kernel_up_EDF, kernel_down_EFD):
        import jax, jax.numpy as jnp
        import numpy as np
        TOP_K = 2
        E = router_kernel_DE.shape[-1]
        x = x.astype(jnp.float32)
        logits_BSE = jnp.einsum('BSD,DE->BSE', x, router_kernel_DE)
        probs_BSE = jax.nn.softmax(logits_BSE.astype(jnp.float32), axis=-1)
        weights_BSK, indices_BSK = jax.lax.top_k(probs_BSE, TOP_K)
        norm_weights_BSK = jax.nn.softmax(weights_BSK, axis=-1)
        one_hot_BSKE = jax.nn.one_hot(indices_BSK, num_classes=E, dtype=x.dtype)
        full_weights_BSE = jnp.sum(one_hot_BSKE * norm_weights_BSK[..., None], axis=2)
        gating_BSEF = jnp.einsum('BSD,EDF->BSEF', x, kernel_gating_EDF)
        act_BSEF = jax.nn.silu(gating_BSEF)
        up_BSEF = jnp.einsum('BSD,EDF->BSEF', x, kernel_up_EDF)
        fuse_BSEF = act_BSEF * up_BSEF
        down_BSED = jnp.einsum('BSEF,EFD->BSED', fuse_BSEF, kernel_down_EFD)
        out_BSD = jnp.einsum('BSED,BSE->BSD', down_BSED, full_weights_BSE)
        return out_BSD.astype(jnp.float32)

    def _L2_xattn_ref(query, key_value, key_mask, Wq, bq, Wk, bk, Wv, bv, Wo, bo):
        import jax, jax.numpy as jnp
        import numpy as np
        B, LQ, LKV = (8, 256, 512)
        QDIM, KDIM, HID = (256, 256, 256)
        Q = query @ Wq + bq
        K = key_value @ Wk + bk
        V = key_value @ Wv + bv
        hid = Q.shape[-1]
        scores = jnp.einsum('bqh,bkh->bqk', Q, K) / jnp.sqrt(jnp.float32(hid))
        scores = jnp.where(key_mask[:, None, :], scores, jnp.float32(-1000000000.0))
        attn = jax.nn.softmax(scores, axis=-1)
        context = jnp.einsum('bqk,bkh->bqh', attn, V)
        return context @ Wo + bo

    def _L2_ffn_ref(x, kernel, bias, a, b):
        import jax, jax.numpy as jnp
        import numpy as np
        INT4_QMAX = 7.0

        def simulate_quantize_int4(w):
            scale = jnp.max(jnp.abs(w)) / INT4_QMAX
            q = jnp.clip(jnp.round(w / scale), -8.0, 7.0)
            return q * scale
        w = simulate_quantize_int4(kernel)
        y = jnp.einsum('bsd,df->bsf', x, w) + bias
        lora = jnp.einsum('bsr,rf->bsf', jnp.einsum('bsd,dr->bsr', x, a), b)
        return y + lora

    def _L3_xattn_ref(inputs, context_sequence, Wk1, Wq1, Wv1, Wk2, Wq2, Wv2, W1, b1, W2, b2, gamma, beta):
        import jax, jax.numpy as jnp
        import numpy as np
        EPS = 0.001
        LEAKY_ALPHA = 0.2

        def layer_norm(x, gamma, beta):
            mu = jnp.mean(x, axis=-1, keepdims=True)
            var = jnp.mean(jnp.square(x - mu), axis=-1, keepdims=True)
            return (x - mu) * jax.lax.rsqrt(var + EPS) * gamma + beta

        def attention_head(x_k, x_v, x_q, Wk, Wq, Wv, use_mask):
            K = x_k @ Wk
            V = x_v @ Wv
            Q = x_q @ Wq
            Lq, Lk = (Q.shape[1], K.shape[1])
            score = jnp.einsum('bqd,bkd->bqk', Q, K) / jnp.sqrt(jnp.float32(Lk))
            if use_mask:
                mask = jnp.triu(jnp.full((Lq, Lk), -jnp.inf, dtype=score.dtype), k=1)
                score = score + mask
            return jax.nn.softmax(score, axis=-1) @ V
        att = attention_head(inputs, inputs, inputs, Wk1, Wq1, Wv1, use_mask=True)
        norm = layer_norm(att + inputs, gamma, beta)
        att2 = attention_head(context_sequence, context_sequence, att, Wk2, Wq2, Wv2, use_mask=False)
        norm2 = layer_norm(att2 + norm, gamma, beta)
        h = jax.nn.leaky_relu(norm2 @ W1 + b1, negative_slope=LEAKY_ALPHA)
        ff = h @ W2 + b2
        norm3 = layer_norm(ff + norm2, gamma, beta)
        return jax.nn.relu(norm3)

    def _L3_ffn_ref(x, gate_w, w1, w2, w3):
        import jax, jax.numpy as jnp
        import numpy as np
        NUM_EXPERTS = 8
        TOP_K = 2
        DIM = 256
        HIDDEN = 1024
        B, S = (2, 256)
        orig_shape = x.shape
        xt = x.reshape(-1, orig_shape[-1])
        scores = xt @ gate_w.T
        top_vals, top_idx = jax.lax.top_k(scores, TOP_K)
        top_w = jax.nn.softmax(top_vals, axis=-1)
        combine = jnp.einsum('tke,tk->te', jax.nn.one_hot(top_idx, NUM_EXPERTS, dtype=xt.dtype), top_w)
        h = jax.nn.silu(jnp.einsum('td,ehd->eth', xt, w1)) * jnp.einsum('td,ehd->eth', xt, w3)
        ye = jnp.einsum('eth,edh->etd', h, w2)
        y = jnp.einsum('te,etd->td', combine, ye)
        return y.reshape(orig_shape)
    x = x + _L0_xattn_ref(_layernorm(x, axis=-1), ctx_1024, ctx_1024, mask_1x1xSxS2_ik0, L0_xattn_wq_w, L0_xattn_wq_b, L0_xattn_wk_w, L0_xattn_wk_b, L0_xattn_wv_w, L0_xattn_wv_b, L0_xattn_out_w, L0_xattn_out_b)
    x = x + _L0_ffn_ref(_layernorm(x, axis=-1), L0_ffn_w_gate, L0_ffn_w1, L0_ffn_w2, L0_ffn_w3, L0_ffn_sw1, L0_ffn_sw2, L0_ffn_sw3, L0_ffn_expert_bias)
    x = x + _L1_xattn_ref(_layernorm(x, axis=-1), ctx_1024, ctx_1024)
    x = x + _L1_ffn_ref(_layernorm(x, axis=-1), L1_ffn_router_kernel_DE, L1_ffn_kernel_gating_EDF, L1_ffn_kernel_up_EDF, L1_ffn_kernel_down_EFD)
    x = x + _L2_xattn_ref(_layernorm(x, axis=-1), ctx_1024, mask_BxS2_bk0, L2_xattn_Wq, L2_xattn_bq, L2_xattn_Wk, L2_xattn_bk, L2_xattn_Wv, L2_xattn_bv, L2_xattn_Wo, L2_xattn_bo)
    x = x + _L2_ffn_ref(_layernorm(x, axis=-1), L2_ffn_kernel, L2_ffn_bias, L2_ffn_a, L2_ffn_b)
    x = x + _L3_xattn_ref(_layernorm(x, axis=-1), ctx_1024, L3_xattn_Wk1, L3_xattn_Wq1, L3_xattn_Wv1, L3_xattn_Wk2, L3_xattn_Wq2, L3_xattn_Wv2, L3_xattn_W1, L3_xattn_b1, L3_xattn_W2, L3_xattn_b2, L3_xattn_gamma, L3_xattn_beta)
    x = x + _L3_ffn_ref(_layernorm(x, axis=-1), L3_ffn_gate_w, L3_ffn_w1, L3_ffn_w2, L3_ffn_w3)
    return x

_drawn_inputs = setup_inputs


def setup_inputs(seed=0):
    import zlib

    import numpy as np

    out = dict(_drawn_inputs(seed))
    spreads = {'L0_ffn_expert_bias': (0.0, 0.8),
     'L3_xattn_b1': (0.0, 2.0),
     'L3_xattn_b2': (0.0, 2.0),
     'L3_xattn_gamma': (1.0, 0.6),
     'L3_xattn_beta': (0.0, 0.744)}
    factors = {'L0_xattn_wv_b': 8.0,
     'L0_xattn_out_b': 2.935,
     'L0_ffn_w_gate': 8.0,
     'L0_ffn_w1': 7.31,
     'L0_ffn_w2': 6.825,
     'L0_ffn_w3': 7.265,
     'L0_ffn_sw1': 3.567,
     'L0_ffn_sw2': 3.558,
     'L0_ffn_sw3': 3.53,
     'L1_ffn_router_kernel_DE': 5.004,
     'L1_ffn_kernel_gating_EDF': 4.351,
     'L1_ffn_kernel_up_EDF': 4.308,
     'L1_ffn_kernel_down_EFD': 4.307,
     'L2_xattn_bq': 64.0,
     'L2_xattn_bk': 64.0,
     'L2_xattn_bv': 3.931,
     'L2_ffn_a': 8.0,
     'L2_ffn_b': 8.0,
     'L3_xattn_Wk1': 8.0,
     'L3_xattn_Wq1': 8.0,
     'L3_xattn_Wv1': 8.0,
     'L3_xattn_Wk2': 61.124,
     'L3_xattn_Wq2': 62.62,
     'L3_xattn_Wv2': 32.577,
     'L3_xattn_W1': 2.711,
     'L2_xattn_Wq': 5.937,
     'L2_xattn_Wk': 5.549,
     'L2_xattn_bo': 4.686,
     'L3_ffn_gate_w': 3.164,
     'L3_ffn_w1': 2.97,
     'L3_ffn_w2': 2.791,
     'L3_ffn_w3': 2.795}
    for name, (base, spread) in spreads.items():
        noise = np.random.default_rng([zlib.crc32(name.encode()), seed]).standard_normal(out[name].shape)
        drawn = base * np.exp(spread * noise) if base else spread * noise
        out[name] = jnp.asarray(drawn.astype(out[name].dtype))
    for name, factor in factors.items():
        out[name] = (out[name] * factor).astype(out[name].dtype)
    return out
```

```python
from contextlib import ExitStack

import concourse.bass as bass
from concourse import mybir

P = 128
TILES = 16
T = 4
GROUPS = TILES // T
D = 256
KC = D // P
H = 16
HD = D // H
E = 8
NTOK = TILES * P
CAP = NTOK
SLOT = 256
REGION = CAP // SLOT
MOE_TILES = 2 * NTOK // SLOT + E - 1
SPARE = E * REGION
HID0 = 128
E0 = 10
PAIR = E0 // 2 - 1
VW = HD + 1
HIDS = {1: 512, 3: 1024}
PAIRBLK = [4 * (b + 1) for b in range(4)]
PRW = sum(4 * n * HD for n in PAIRBLK)

F32 = mybir.dt.float32
BF16 = mybir.dt.bfloat16
I32 = mybir.dt.int32
U32 = mybir.dt.uint32
U8 = mybir.dt.uint8
ALU = mybir.AluOpType
ACT = mybir.ActivationFunctionType
AX = mybir.AxisListType.X
RMAX = bass.bass_isa.ReduceOp.max
ds = bass.ds

PRIMED = 1
PRIMED_SEMS = ["norm_rows_free", "result_free0", "result_free1", "combined", "x_final"]

RING = [0, 1, 2, 3, 4, 5]
ACC = [6, 7]


class BankPlan:

    def __init__(self):
        self.done = [0] * 8
        self.ring = 0
        self.acc = 0

    def phase(self, keys, turns):
        per, table = [0] * 8, {}
        for key in keys:
            if key[0] == "acc":
                b = ACC[self.acc % len(ACC)]
                self.acc += 1
            else:
                b = RING[self.ring % len(RING)]
                self.ring += 1
            table[key] = (b, self.done[b], per[b])
            per[b] += 1
        plan = {key: (b, base, per[b], k) for key, (b, base, k) in table.items()}
        for b in range(8):
            self.done[b] += turns * per[b]
        return plan


def job(plan, key, turn):
    b, base, per, k = plan[key]
    return b, turn * per + (base + k + 1)


class Waits:

    def __init__(self, engine):
        self.engine = engine
        self.plan = None

    def at_least(self, sem, plan, key, turn, more):
        b, n = job(plan, key, turn)
        _, base, _, k = plan[key]
        if self.plan is not plan:
            self.plan, self.had = plan, {}
        if self.had.get(b, -1) < base + k + more:
            self.had[b] = base + k + more
            self.engine.wait_ge(sem[b], n + more)
        return b


STEPS = {"phase1": 64, "routed": 1, "layer1": 96, "phase3": 121, "last": 8}


def build(nc, ins, out):
    x_in, ctx_in, mask_qk, mask_bk = ins["x"], ins["ctx"], ins["mask_qk"], ins["mask_bk"]

    bp = BankPlan()
    pre = bp.phase([("wab", 0), ("wab", 1)], 1)
    k1 = [("cT", 0), ("cT", 1), ("kT", 0), ("kT", 1)] + [("v", t) for t in range(T)]
    k1 += [("xT0", 0), ("xT0", 1), ("qT", 0), ("qT", 1)]
    UNITS = 2 * T
    att_order = []
    for n in range(UNITS + 3):
        att_order += [(a, n - lag) for a, lag in (("s", 0), ("p", 2), ("o", 3)) if 0 <= n - lag < UNITS]
    for a, i in att_order:
        if a != "o":
            k1 += [(a, i, 0), (a, i, 1)]
        elif i % 2 == 0:
            k1.append(("acc", "o", i // 2))
    k1 += [("aT", 0), ("aT", 1)] + [("xo", t) for t in range(T)] + [("xT1", 0), ("xT1", 1), ("lg",)]
    ffn_steps = []
    for i in range(T + 3):
        if i < T:
            ffn_steps.append(("up", i))
        if 2 <= i < T + 2:
            ffn_steps.append(("hT", i - 2))
        if i >= 3:
            ffn_steps.append(("down", i - 3))
    for s, i in ffn_steps:
        k1.append(("acc", "y", i) if s == "down" else (s, i))
    j1 = bp.phase(k1, GROUPS)
    jr0 = bp.phase([("cnt",), ("gt",)], 1)
    jr = bp.phase([("ow",)] + [("gu", t) for t in range(T)] + [("hs",)], GROUPS)
    jr1 = bp.phase([("dn",)], 1)
    j2 = bp.phase([("xT3", 0), ("xT3", 1), ("lg1",), ("rk",)], GROUPS)

    def moe_steps(hc, second):
        seq = [(u, c) for u in range(2 if second else 1) for c in range(hc)]
        steps = [("xsT", 0)]
        for i in range(len(seq) + 2):
            if i < len(seq):
                steps.append(("up",) + seq[i])
                if seq[i][0] == 0 and seq[i][1] == hc - 3 and second:
                    steps.append(("xsT", 1))
            if i >= 2:
                steps.append(("down",) + seq[i - 2])
        return steps

    def moe_keys(steps):
        keys = []
        for s in steps:
            if s[0] == "down":
                if s[2] == 0:
                    keys += [("acc", "y", s[1], 0), ("acc", "y", s[1], 1)]
            else:
                keys.append(s)
        return keys

    moe = {}
    LOOPS = MOE_TILES // 2
    moe[1] = [(moe_steps(4, True), bp.phase(moe_keys(moe_steps(4, True)), LOOPS)),
              (moe_steps(4, False), bp.phase(moe_keys(moe_steps(4, False)), 1))]
    k3 = [("cT", 0), ("cT", 1), ("k2", 0), ("k2", 1), ("v2", 0), ("v2", 1), ("xT4", 0), ("xT4", 1),
          ("q2", 0), ("q2", 1), ("s2",), ("k4", 0), ("k4", 1), ("v4", 0), ("v4", 1), ("p2",), ("o2", 0), ("o2", 1),
          ("oT2", 0), ("oT2", 1), ("x2", 0), ("x2", 1), ("xT5", 0), ("xT5", 1), ("f2", 0), ("f2", 1),
          ("xT6", 0), ("xT6", 1), ("q3", 0), ("q3", 1), ("k3", 0), ("k3", 1), ("s3",), ("v3", 0), ("v3", 1),
          ("p3",), ("o3", 0), ("o3", 1), ("aT", 0), ("aT", 1), ("q4", 0), ("q4", 1), ("s4",), ("p4",),
          ("o4", 0), ("o4", 1), ("nT", 0), ("nT", 1), ("h", 0), ("h", 1), ("ff", 0), ("ff", 1),
          ("xT7", 0), ("xT7", 1), ("lg1",), ("rk",)]
    j3 = bp.phase(k3, GROUPS)
    moe[3] = [(moe_steps(8, True), bp.phase(moe_keys(moe_steps(8, True)), LOOPS)),
              (moe_steps(8, False), bp.phase(moe_keys(moe_steps(8, False)), 1))]

    tiles_before = {1: (0, 0), 3: (LOOPS + 1, LOOPS)}

    ctx = ExitStack()
    with ctx:
        def sb(name, shape, dt=F32):
            return ctx.enter_context(nc.sbuf_tensor(name, shape, dt))

        sems = {}

        def sem(name):
            if name not in sems:
                sems[name] = ctx.enter_context(nc.semaphore(name))
            return sems[name]

        bank = [ctx.enter_context(nc.psum_tensor(f"bank{b}", [P, 512], F32)) for b in range(8)]
        bank_full = [sem(f"bank_full{b}") for b in range(8)]
        bank_empty = [sem(f"bank_empty{b}") for b in range(8)]

        xs_dram = nc.dram_tensor("expert_rows_in", ((SPARE + 1) * SLOT, D), F32, kind="Internal").ap()
        ys_dram = nc.dram_tensor("expert_rows_out", ((SPARE + 1) * SLOT, D), F32, kind="Internal").ap()

        X = sb("x_stream", [P, TILES * D])
        ident = sb("ident", [P, P])
        tri = sb("tri", [P, P], BF16)
        ones = sb("ones", [P, P], BF16)
        neg_half = sb("neg_half", [P, T])
        lower8 = sb("lower8", [P, E, E])
        lower4 = sb("lower4", [P, 4, 4])
        head_of = sb("head_of_row", [P, 8])
        region0 = sb("region_start", [P, E])
        causal = sb("causal", [P, P])
        causal16 = sb("causal16", [P, H, H])
        row_bias = sb("row_bias", [P, 8, D])
        BV0, BO0, BV2, BO2, BF2, GAM, BET, BB2 = range(8)
        col_bias = sb("col_bias", [P, 5, KC])
        CQ0, CK0, CQ2, CK2, CB1 = range(5)
        ebias = sb("expert_bias", [P, E])
        keymask = sb("keymask", [P, TILES * P])
        keymask8 = sb("keymask8", [P, TILES * P // 4], I32)
        mask01 = sb("mask01", [P, P])
        maski = sb("maski", [P, P], I32)
        Wr0 = sb("w_router0", [P, KC, E])
        Wr = {1: sb("w_router1", [P, KC, E]), 3: sb("w_router3", [P, KC, E])}
        IDX = sb("slot_index", [P, TILES * 2], U32)
        IDXG = sb("slot_index_group", [P, T * 2], U32)
        IDXP = sb("slot_index_gather", [P, T * 2], U32)
        CW = sb("combine_weight", [P, TILES * 2])
        CWP = sb("combine_weight_group", [P, T * 2])
        WREG = sb("weights", [P, 9984])
        BIG = sb("work", [P, 12288])
        Kb = BIG[:, 0:4096].rearrange("p (b h k) -> p b h k", b=4, h=8)
        SC = BIG[:, 4096:8192].rearrange("p (b h k) -> p b h k", b=4, h=8)
        PT = BIG[:, 8192:12288].rearrange("p (b h q) -> p b h q", b=4, h=8)
        PR = BIG[:, 7168:7168 + PRW]
        PRD = BIG[:, 7168 + PRW:7168 + 2 * PRW]
        ZERO = sb("zero", [P, D])
        NBG = sb("key_penalty", [P, T * P])
        CG = sb("ctx_rows", [P, T, D])
        cT = sb("ctx_cols", [P, KC, T * P])
        kT = sb("k_cols", [P, KC, T * P])
        qT = sb("q_cols", [P, KC, T * P])
        XN = sb("norm_rows", [P, T, D])
        xT = sb("norm_cols", [P, KC, T * P])
        AO = sb("att_rows", [P, T, D])
        aT = sb("att_cols", [P, KC, T * P])
        V0 = sb("v_rows", [P, T, H, VW])
        SCORE_BIAS = sb("score_bias", [P, H, P])
        EXTRA = sb("extra", [P, 3072])
        ST = sb("stats", [P, T, 6])
        MV = sb("mean_var", [P, T, 2])
        VE = sb("var_eps", [P, T])
        RS = sb("rstd", [P, T])
        MX = sb("row_max", [P, 64])
        RC = sb("row_rec", [P, 64])
        small = sb("small", [P, 16, T * E])
        cmpa = sb("cmpa", [P, T * E * E])
        cmpb = sb("cmpb", [P, T * E * E])
        SRC = sb("source_row", [P, TILES * 2 * E])
        WV = sb("choice_weight", [P, TILES * 2])
        FLAT = sb("flat_place", [P, TILES * 2])
        X8 = sb("first_rows_cols", [P, GROUPS * KC * E])
        RANK = sb("rank", [P, T, E])
        OH = sb("onehot", [P, T, 2, E])
        OHT = sb("onehot_t", [P, T, 2, E])
        SEL = sb("selected", [P, T, E], BF16)
        base = sb("list_len", [P, E])
        wide = sb("tile_math", [1, 6, MOE_TILES * E])
        lens_i = sb("lens_i", [1, E], I32)
        t8 = sb("tile8", [1, 6, E])
        jrow_i = sb("jrow_i", [1, MOE_TILES * E], I32)
        LAB = sb("lora_product", [P, KC, D])
        jrow = sb("jrow", [1, MOE_TILES * E])
        tile_e = sb("tile_expert", [1, MOE_TILES], I32)
        tile_r = sb("tile_region", [1, MOE_TILES], I32)

        def wview(off, k):
            return WREG[:, off:off + KC * k].rearrange("p (c n) -> p c n", c=KC)

        W0 = {n: wview(i * 512, D) for i, n in enumerate(("q", "k", "v", "o"))}
        W13 = wview(2048, E0 * 2 * HID0)
        W2 = WREG[:, 2048 + KC * E0 * 256:2048 + KC * E0 * 256 + E0 * D].rearrange("p (e n) -> p e n", e=E0)
        L3N = ("q2", "k2", "v2", "o2", "k3", "q3", "v3", "k4", "q4", "v4", "h", "ff")
        W3 = {n: wview(i * 512, D) for i, n in enumerate(L3N)}
        WEFF = wview(12 * 512, D)
        KER = wview(13 * 512, D)
        QTMP = wview(14 * 512, D)
        LORA_A = sb("lora_a", [16, D])
        LORA_B = sb("lora_b", [16, D])
        WB = [BIG[:, 6144 * u:6144 * (u + 1)] for u in range(2)]

        SG0 = EXTRA[:, 0:1536].rearrange("p (b n) -> p b n", b=len(RING))
        HB0 = EXTRA[:, 1536:2304].rearrange("p (b n) -> p b n", b=3)
        HT0 = EXTRA[:, 2304:3072].rearrange("p (b n) -> p b n", b=3)
        S16 = EXTRA[:, 0:1024].rearrange("p (t h k) -> p t h k", t=T, h=H)
        S16b = EXTRA[:, 1024:2048].rearrange("p (t h k) -> p t h k", t=T, h=H)
        O16 = EXTRA[:, 2048:3072].rearrange("p (t n) -> p t n", t=T)
        DIAG = 2 * E * E + E
        XE = BIG[:, 0:KC * E * DIAG].rearrange("p (c n) -> p c n", c=KC)
        OHS = BIG[:, 2176:2688].rearrange("p (a n) -> p a n", a=2 * T)
        OWS = BIG[:, 2688:3200].rearrange("p (t n) -> p t n", t=T)
        OWT = BIG[:, 3200:3712].rearrange("p (t n) -> p t n", t=T)
        GT = BIG[:, 3712:4224]
        SGR = BIG[:, 4224:5248].rearrange("p (t k n) -> p t k n", t=T, k=2)
        HR = BIG[:, 5248:6272].rearrange("p (a n) -> p a n", a=2 * T)
        HS = BIG[:, 6272:6336]
        EO = BIG[:, 6336:6592]
        XS = aT[:, :, :].rearrange("p c (h n) -> p c h n", h=2)
        xsT = xT[:, :, :].rearrange("p c (u n) -> p u c n", u=2)
        SG = SCORE_BIAS[:, 0:12, :].rearrange("p (b a) k -> p b (a k)", b=len(RING))
        HT = EXTRA[:, 0:2048].rearrange("p (c n) -> p c n", c=8)
        YS = AO[:, :, :].rearrange("p (u h) n -> p u h n", u=2)
        SC2 = BIG[:, 0:512].rearrange("p (t k) -> p t k", t=T)
        PT2 = BIG[:, 512:1024].rearrange("p (t k) -> p t k", t=T)
        V2 = BIG[:, 1024:2048].rearrange("p (t n) -> p t n", t=T)
        V4 = BIG[:, 2048:3072].rearrange("p (t n) -> p t n", t=T)
        V3 = BIG[:, 3072:4096].rearrange("p (t n) -> p t n", t=T)
        k4T = BIG[:, 4096:5120].rearrange("p (c n) -> p c n", c=KC)
        IN3 = BIG[:, 5120:6144].rearrange("p (t n) -> p t n", t=T)
        N1 = BIG[:, 6144:7168].rearrange("p (t n) -> p t n", t=T)
        N2 = BIG[:, 7168:8192].rearrange("p (t n) -> p t n", t=T)
        R3 = BIG[:, 8192:9216].rearrange("p (t n) -> p t n", t=T)
        hT3 = BIG[:, 9216:10240].rearrange("p (c n) -> p c n", c=KC)
        hTt = BIG[:, 10240:11264].rearrange("p (c n) -> p c n", c=KC)
        N2B = BIG[:, 11264:12288].rearrange("p (t n) -> p t n", t=T)
        YA = EXTRA[:, 0:2048].rearrange("p (a n) -> p a n", n=D)
        dist_i = AO[:, 2, 0:P].bitcast(I32)
        flat_i = AO[:, 3, 0:2 * TILES].bitcast(I32)
        DIST = AO[:, 0, 0:P]
        NEG = AO[:, 1, 0:P]

        xg = lambda g, t: X[:, ds((T * g + t) * D, D)]
        xgroup = lambda g: X[:, ds(g * T * D, T * D)].rearrange("p (t n) -> p t n", t=T)

        def bc(ap, n):
            return ap.unsqueeze(len(ap.shape)).to_broadcast(list(ap.shape) + [n])

        def rep(ap, n, at=1):
            s = list(ap.shape)
            return ap.unsqueeze(at).to_broadcast(s[:at] + [n] + s[at:])

        consts = [(maski[:, :], mask_qk), (keymask8[:, :].bitcast(U8), mask_bk.partition_broadcast(P)),
                  (ebias[:, :], ins["ebias"].partition_broadcast(P)),
                  (Wr0[:, :, :], ins["wr0"]), (Wr[1][:, :, :], ins["wr1"]), (Wr[3][:, :, :], ins["wr3"]),
                  (LORA_A[:, :], ins["lora_a"]), (LORA_B[:, :], ins["lora_b"]),
                  (row_bias[:, :, :].rearrange("p a n -> p (a n)"), ins["row_bias"].partition_broadcast(P)),
                  (col_bias[:, :, :], ins["col_bias"])]
        w1loads = [(W0["q"], ins["w0q"]), (W0["k"], ins["w0k"]), (W0["v"], ins["w0v"]), (W0["o"], ins["w0o"]),
                   (W13, ins["w13"]), (W2, ins["w2"])]
        w3loads = [(W3[n], ins["w3" + n]) for n in L3N] + [(KER, ins["kernel"])]
        ZCHUNK = 10
        zrows = xs_dram.rearrange("(a p r) d -> a p (r d)", p=P, r=ZCHUNK)

        yrows = ys_dram.rearrange("(a p r) d -> a p (r d)", p=P, r=ZCHUNK)

        def score_products(tt, dst, t):
            q = AO[:, t, :].rearrange("p (h d) -> p h d", h=H)
            kv = CG[:, t, :].rearrange("p (k d) -> p k d", k=H)
            off = 0
            for k, nk in enumerate(PAIRBLK):
                part = dst[:, off:off + 4 * nk * HD].rearrange("p (h k d) -> p h k d", h=4, d=HD)
                off += 4 * nk * HD
                yield tt(part, rep(q[:, 4 * k:4 * k + 4, :], nk, 2), rep(kv[:, 0:nk, :], 4), ALU.mult)

        def value_products(tt, dst, t):
            vt = CG[:, t, :].rearrange("p (k d) -> p d k", k=H)
            off = 0
            for k, nk in enumerate(PAIRBLK):
                part = dst[:, off:off + 4 * nk * HD].rearrange("p (h d k) -> p h d k", h=4, d=HD)
                off += 4 * nk * HD
                yield tt(part, rep(S16b[:, t, 4 * k:4 * k + 4, 0:nk], HD, 2), rep(vt[:, :, 0:nk], 4), ALU.mult)

        block = ctx.enter_context(nc.Block())

        @block.sync
        def _(sp):
            sp.dma_start(X[:, :].rearrange("p (t n) -> p t n", t=TILES), x_in.rearrange("t p n -> p t n")).then_inc(sem("x_loaded"), 16)
            for dst, src in consts:
                sp.dma_start(dst, src).then_inc(sem("const_loaded"), 16)
            for dst, src in w1loads:
                sp.dma_start(dst, src).then_inc(sem("w1_loaded"), 16)

            def ctx_loads():
                sp.dma_start(CG[:, :, :], ctx_in[0:T, :, :].rearrange("t p n -> p t n")).then_inc(sem("ctx_loaded"), 16)
                with sp.Fori(1, GROUPS) as g:
                    b, n = job(j1, ("cT", 1), g)
                    sp.wait_ge(bank_full[b], n)
                    sp.dma_start(CG[:, :, :], ctx_in[ds(g * T, T), :, :].rearrange("t p n -> p t n")).then_inc(sem("ctx_loaded"), 16)
                b, n = job(j1, ("cT", 1), GROUPS)
                sp.wait_ge(bank_full[b], n)
                sp.dma_start(CG[:, :, :], ctx_in[0:T, :, :].rearrange("t p n -> p t n")).then_inc(sem("ctx_loaded"), 16)
                with sp.Fori(1, GROUPS) as g:
                    sp.wait_ge(sem("normed"), 2 * g + 2 * GROUPS)
                    sp.dma_start(CG[:, :, :], ctx_in[ds(g * T, T), :, :].rearrange("t p n -> p t n")).then_inc(sem("ctx_loaded"), 16)
                    sp.wait_ge(sem("rows_sent"), 16 * 2 * T * g)
                    sp.sem_inc(sem("norm_rows_free"), 1)

            def experts(layer):
                wsrc = ins[f"moe{layer}"]
                width = wsrc.shape[2]

                def load(u, j):
                    e = sp.value_load(tile_e[0:1, ds(j, 1)], min_val=0, max_val=E - 1)
                    r = sp.value_load(tile_r[0:1, ds(j, 1)], min_val=0, max_val=SPARE)
                    sp.dma_start(XS[:, u, :, :], xs_dram[ds(r * SLOT, SLOT), :].rearrange("(h p) d -> p h d", p=P)).then_inc(sem(f"rows_loaded{u}"), 16)
                    sp.dma_start(WB[u][:, 0:width], wsrc[ds(e, 1), :, :].rearrange("a p n -> p (a n)")).then_inc(sem(f"w_loaded{u}"), 16)

                def buffers_free(plan, turn, u):
                    b, n = job(plan, ("acc", "y", u, 1), turn)
                    sp.wait_ge(bank_full[b], n + 1)

                def store(plan, turn, pair, u, j):
                    for h in range(2):
                        b, n = job(plan, ("acc", "y", u, h), turn)
                        sp.wait_ge(bank_empty[b], n + 1)
                    r = sp.value_load(tile_r[0:1, ds(j, 1)], min_val=0, max_val=SPARE)
                    sp.dma_start(ys_dram[ds(r * SLOT, SLOT), :].rearrange("(h p) d -> p h d", p=P), YS[:, u, :, :]).then_inc(sem(f"y_stored{u}"), 16)
                    sp.wait_ge(sem(f"y_stored{u}"), (pair + tiles_before[layer][u] + 1) * 16)
                    sp.sem_inc(sem(f"result_free{u}"), 1)

                loop, tail = moe[layer][0][1], moe[layer][1][1]
                load(0, 0)
                load(1, 1)
                if layer == 1:
                    for dst, src in w3loads:
                        sp.dma_start(dst, src).then_inc(sem("w3_loaded"), 16)
                    sp.dma_start(CG[:, :, :], ctx_in[0:T, :, :].rearrange("t p n -> p t n")).then_inc(sem("ctx_loaded"), 16)
                with sp.Fori(0, LOOPS - 1) as i:
                    for u in range(2):
                        buffers_free(loop, i, u)
                        load(u, 2 * i + (2 + u))
                        store(loop, i, i, u, 2 * i + u)
                i = LOOPS - 1
                buffers_free(loop, i, 0)
                load(0, 2 * LOOPS)
                for u in range(2):
                    store(loop, i, i, u, 2 * i + u)
                store(tail, 0, LOOPS, 0, 2 * LOOPS)

            ctx_loads()
            sp.wait_ge(sem("rows_sent"), 16 * 2 * TILES)
            sp.sem_inc(sem("norm_rows_free"), 1)
            sp.wait_ge(sem("tiles_planned"), 1)
            sp.wait_ge(sem("results_zeroed"), 16 * yrows.shape[0])
            experts(1)
            with sp.Fori(1, GROUPS) as g:
                b, n = job(j3, ("cT", 1), g)
                sp.wait_ge(bank_full[b], n)
                sp.dma_start(CG[:, :, :], ctx_in[ds(g * T, T), :, :].rearrange("t p n -> p t n")).then_inc(sem("ctx_loaded"), 16)
                sp.wait_ge(sem("rows_sent"), 16 * 2 * T * (g + GROUPS))
                sp.sem_inc(sem("norm_rows_free"), 1)
            sp.wait_ge(sem("rows_sent"), 16 * 2 * TILES * 2)
            sp.wait_ge(sem("tiles_planned"), 2)
            experts(3)
            with sp.Fori(0, GROUPS) as g:
                sp.wait_ge(sem("x_final"), PRIMED + g + 1)
                sp.dma_start(out[ds(g * T, T), :, :].rearrange("t p n -> p t n"), xgroup(g)).then_inc(sem("out_stored"), 16)
            sp.wait_ge(sem("out_stored"), 16 * GROUPS)

        @block.tensor
        def _(pe):
            empties = Waits(pe)

            def fill(plan, g, key):
                b = empties.at_least(bank_empty, plan, key, g, 0)
                return bank[b], b

            def ready(plan, g, key):
                empties.at_least(bank_empty, plan, key, g, 1)

            def mm(o, l, r, a=True, z=True):
                return pe.matmul(o, l, r, start=a, stop=z)

            def turn_rows(plan, g, name, rows):
                for c in range(KC):
                    ps, b = fill(plan, g, (name, c))
                    for t in range(T):
                        m = pe.transpose(ps[:, t * P:(t + 1) * P], rows[:, t, c * P:(c + 1) * P], ident[:, :])
                    m.then_inc(bank_full[b], 1)

            def cols(plan, g, name, w, src):
                for m in range(KC):
                    ps, b = fill(plan, g, (name, m))
                    for c in range(KC):
                        last = mm(ps[:, :], w[:, c, m * P:(m + 1) * P], src[:, c, :], c == 0, c == KC - 1)
                    last.then_inc(bank_full[b], 1)

            def rows2(plan, g, name, w, src):
                for a in range(2):
                    ps, b = fill(plan, g, (name, a))
                    for i in range(2):
                        t = 2 * a + i
                        for c in range(KC):
                            last = mm(ps[:, i * D:(i + 1) * D], src[:, c, t * P:(t + 1) * P], w[:, c, :], c == 0, c == KC - 1)
                    last.then_inc(bank_full[b], 1)

            def rows1(plan, g, name, w, src):
                for t in range(T):
                    ps, b = fill(plan, g, (name, t))
                    for c in range(KC):
                        last = mm(ps[:, 0:D], src[:, c, t * P:(t + 1) * P], w[:, c, :], c == 0, c == KC - 1)
                    last.then_inc(bank_full[b], 1)

            def logits(plan, g, name, w):
                ps, b = fill(plan, g, (name,))
                for t in range(T):
                    for c in range(KC):
                        last = mm(ps[:, t * E:(t + 1) * E], xT[:, c, t * P:(t + 1) * P], w[:, c, :], c == 0, c == KC - 1)
                last.then_inc(bank_full[b], 1)

            def list_ranks(plan, g, turn):
                ps, b = fill(plan, g, ("rk",))
                pe.wait_ge(sem("selected"), turn + 1)
                for t in range(T):
                    for s in range(t + 1):
                        mm(ps[:, t * E:(t + 1) * E], tri[:, :] if s == t else ones[:, :], SEL[:, s, :], s == 0, s == t)
                for s in range(T):
                    last = mm(ps[:, T * E:(T + 1) * E], ones[:, :], SEL[:, s, :], s == 0, s == T - 1)
                last.then_inc(bank_full[b], 1)

            def phase1(g):
                pe.wait_ge(sem("ctx_loaded"), 16 * (g + 1))
                turn_rows(j1, g, "cT", CG)
                ready(j1, g, ("cT", 0))
                ready(j1, g, ("cT", 1))
                cols(j1, g, "kT", W0["k"], cT)
                rows1(j1, g, "v", W0["v"], cT)
                pe.wait_ge(sem("normed"), 2 * g + 1)
                turn_rows(j1, g, "xT0", XN)
                ready(j1, g, ("xT0", 0))
                ready(j1, g, ("xT0", 1))
                cols(j1, g, "qT", W0["q"], xT)
                ready(j1, g, ("qT", 0))
                ready(j1, g, ("qT", 1))
                for a, i in att_order:
                    t, m, u = i // 2, i % 2, i % 4
                    if a == "s":
                        pe.wait_ge(sem("k_heads"), UNITS * g + (i + 1))
                        for j in range(2):
                            ps, b = fill(j1, g, ("s", i, j))
                            mm(ps[:, :].rearrange("p (h k) -> p h k", h=4), qT[:, m, t * P:(t + 1) * P],
                               Kb[:, u, 4 * j:4 * j + 4, :]).then_inc(bank_full[b], 1)
                    elif a == "p":
                        pe.wait_ge(sem("probs"), UNITS * g + (i + 1))
                        for j in range(2):
                            ps, b = fill(j1, g, ("p", i, j))
                            for h in range(4):
                                last = pe.transpose(ps[:, h * P:(h + 1) * P], SC[:, u, 4 * j + h, :], ident[:, :])
                            last.then_inc(bank_full[b], 1)
                    else:
                        if m == 0:
                            ready(j1, g, ("v", t))
                            ps_o, b_o = fill(j1, g, ("acc", "o", t))
                        for j in range(2):
                            ready(j1, g, ("p", i, j))
                        for h in range(8):
                            last = mm(ps_o[:, (8 * m + h) * VW:(8 * m + h + 1) * VW], PT[:, u, h, :], V0[:, t, 8 * m + h, :])
                        if m == 1:
                            last.then_inc(bank_full[b_o], 1)
                for t in range(T):
                    ready(j1, g, ("acc", "o", t))
                turn_rows(j1, g, "aT", AO)
                ready(j1, g, ("aT", 0))
                ready(j1, g, ("aT", 1))
                rows1(j1, g, "xo", W0["o"], aT)
                pe.wait_ge(sem("normed"), 2 * g + 2)
                turn_rows(j1, g, "xT1", XN)
                ready(j1, g, ("xT1", 0))
                ready(j1, g, ("xT1", 1))
                logits(j1, g, "lg", Wr0)
                for s, i in ffn_steps:
                    t, p = i, PAIR
                    if s == "up":
                        ps, b = fill(j1, g, ("up", i))
                        for c in range(KC):
                            last = mm(ps[:, :], xT[:, c, t * P:(t + 1) * P], W13[:, c, p * 512:(p + 1) * 512], c == 0, c == KC - 1)
                        last.then_inc(bank_full[b], 1)
                    elif s == "hT":
                        ready(j1, g, ("up", i))
                        ps, b = fill(j1, g, ("hT", i))
                        for a in range(2):
                            last = pe.transpose(ps[:, a * P:(a + 1) * P], HB0[:, i % 3, a * P:(a + 1) * P], ident[:, :])
                        last.then_inc(bank_full[b], 1)
                    else:
                        ps, b = fill(j1, g, ("acc", "y", t))
                        ready(j1, g, ("hT", i))
                        for a in range(2):
                            last = mm(ps[:, 0:D], HT0[:, i % 3, a * P:(a + 1) * P], W2[:, 2 * p + a, :],
                                      a == 0, a == 1)
                        last.then_inc(bank_full[b], 1)

            def routed_start():
                pe.wait_ge(sem("choices_counted"), 1)
                ps, b = fill(jr0, 0, ("cnt",))
                mm(ps[:, 0:E], ones[:, :], SEL[:, 0, :]).then_inc(bank_full[b], 1)
                pe.wait_ge(sem("first_rows_spread"), 2)
                ps, b = fill(jr0, 0, ("gt",))
                for e in range(E):
                    for c in range(KC):
                        last = mm(ps[:, 0:256], XE[:, c, P * e:P * e + P], W13[:, c, 256 * e:256 * e + 256],
                                  e == 0 and c == 0, e == E - 1 and c == KC - 1)
                last.then_inc(bank_full[b], 1)
                ready(jr0, 0, ("gt",))

            def routed(g):
                pe.wait_ge(sem("pairs_built"), g + 1)
                ps, b = fill(jr, g, ("ow",))
                for t in range(T):
                    last = pe.transpose(ps[:, t * P:(t + 1) * P], OWS[:, t, :], ident[:, :])
                last.then_inc(bank_full[b], 1)
                ready(jr, g, ("ow",))
                for t in range(T):
                    ps, b = fill(jr, g, ("gu", t))
                    mm(ps[:, :], OWT[:, t, :], GT).then_inc(bank_full[b], 1)
                ps, b = fill(jr, g, ("hs",))
                for t in range(T):
                    ready(jr, g, ("gu", t))
                    for k in range(2):
                        last = mm(ps[:, 0:64], HR[:, 2 * t + k, :], OHS[:, 2 * t + k, :], t == 0 and k == 0, t == T - 1 and k == 1)
                last.then_inc(bank_full[b], 1)

            def routed_end():
                ready(jr, GROUPS - 1, ("hs",))
                ps, b = fill(jr1, 0, ("dn",))
                for e in range(E):
                    last = mm(ps[0:E, 0:D], HS[:, E * e:E * e + E], W2[:, e, :], e == 0, e == E - 1)
                last.then_inc(bank_full[b], 1)

            def layer1(g):
                pe.wait_ge(sem("normed"), 2 * g + (2 * GROUPS + 2))
                turn_rows(j2, g, "xT3", XN)
                ready(j2, g, ("xT3", 0))
                ready(j2, g, ("xT3", 1))
                logits(j2, g, "lg1", Wr[1])
                list_ranks(j2, g, g)

            def experts(layer, turn, pair, steps, plan):
                hc = HIDS[layer] // P
                before = [pair + n for n in tiles_before[layer]]
                ybank = {}
                up = {u: WB[u][:, 0:KC * 2 * hc * P].rearrange("p (c n) -> p c n", c=KC) for u in range(2)}
                dn = {u: WB[u][:, KC * 2 * hc * P:KC * 2 * hc * P + hc * D].rearrange("p (c n) -> p c n", c=hc) for u in range(2)}
                for s in steps:
                    u = s[1]
                    if s[0] == "xsT":
                        pe.wait_ge(sem(f"rows_loaded{u}"), 16 * (before[u] + 1))
                        ps, b = fill(plan, turn, s)
                        for c in range(KC):
                            for h in range(2):
                                last = pe.transpose(ps[:, (2 * c + h) * P:(2 * c + h + 1) * P], XS[:, u, h, c * P:(c + 1) * P], ident[:, :])
                        last.then_inc(bank_full[b], 1)
                    elif s[0] == "up":
                        c = s[2]
                        if c == 0:
                            pe.wait_ge(sem(f"w_loaded{u}"), 16 * (before[u] + 1))
                            ready(plan, turn, ("xsT", u))
                        ps, b = fill(plan, turn, s)
                        for a in range(2):
                            for k in range(KC):
                                last = mm(ps[:, a * 256:(a + 1) * 256], up[u][:, k, (a * hc + c) * P:(a * hc + c + 1) * P],
                                          xsT[:, u, k, :], k == 0, k == KC - 1)
                        last.then_inc(bank_full[b], 1)
                    else:
                        c = s[2]
                        if c == 0:
                            ybank[u] = [fill(plan, turn, ("acc", "y", u, h)) for h in range(2)]
                        ready(plan, turn, ("up", u, c))
                        for h in range(2):
                            ps, b = ybank[u][h]
                            last = mm(ps[:, 0:D], HT[:, c, h * P:(h + 1) * P], dn[u][:, c, :], c == 0, c == hc - 1)
                            if c == hc - 1:
                                last.then_inc(bank_full[b], 1)

            def phase3(g):
                pe.wait_ge(sem("ctx_loaded"), 16 * (g + (2 * GROUPS + 1)))
                turn_rows(j3, g, "cT", CG)
                ready(j3, g, ("cT", 0))
                ready(j3, g, ("cT", 1))
                cols(j3, g, "k2", W3["k2"], cT)
                rows2(j3, g, "v2", W3["v2"], cT)

                def norm_cols(i, name, rows):
                    pe.wait_ge(sem("normed"), 4 * GROUPS + 5 * g + (i + 1))
                    turn_rows(j3, g, name, rows)
                    ready(j3, g, (name, 0))
                    ready(j3, g, (name, 1))

                def scores(name, q, k, kname=None):
                    ps, b = fill(j3, g, (name,))
                    for t in range(T):
                        for m in range(KC):
                            last = mm(ps[:, t * P:(t + 1) * P], q[:, m, t * P:(t + 1) * P], k[:, m, t * P:(t + 1) * P], m == 0, m == KC - 1)
                    last.then_inc(bank_full[b], 1)

                def probs_v(i, pname, oname, v, vname):
                    pe.wait_ge(sem("probs"), 2 * TILES + 3 * g + (i + 1))
                    ps, b = fill(j3, g, (pname,))
                    for t in range(T):
                        last = pe.transpose(ps[:, t * P:(t + 1) * P], SC2[:, t, :], ident[:, :])
                    last.then_inc(bank_full[b], 1)
                    ready(j3, g, (vname, 0))
                    ready(j3, g, (vname, 1))
                    ready(j3, g, (pname,))
                    for a in range(2):
                        ps, b = fill(j3, g, (oname, a))
                        for i2 in range(2):
                            last = mm(ps[:, i2 * D:(i2 + 1) * D], PT2[:, 2 * a + i2, :], v[:, 2 * a + i2, :])
                        last.then_inc(bank_full[b], 1)

                norm_cols(0, "xT4", XN)
                cols(j3, g, "q2", W3["q2"], xT)
                for n in ("k2", "q2"):
                    for m in range(KC):
                        ready(j3, g, (n, m))
                scores("s2", qT, kT)
                cols(j3, g, "k4", W3["k4"], cT)
                rows2(j3, g, "v4", W3["v4"], cT)
                probs_v(0, "p2", "o2", V2, "v2")
                ready(j3, g, ("o2", 0))
                ready(j3, g, ("o2", 1))
                turn_rows(j3, g, "oT2", AO)
                ready(j3, g, ("oT2", 0))
                ready(j3, g, ("oT2", 1))
                rows2(j3, g, "x2", W3["o2"], aT)
                ready(j3, g, ("k4", 0))
                ready(j3, g, ("k4", 1))
                norm_cols(1, "xT5", XN)
                pe.wait_ge(sem("weff_ready"), 2)
                rows2(j3, g, "f2", WEFF, xT)
                norm_cols(2, "xT6", IN3)
                cols(j3, g, "q3", W3["q3"], xT)
                cols(j3, g, "k3", W3["k3"], xT)
                for n in ("k3", "q3"):
                    for m in range(KC):
                        ready(j3, g, (n, m))
                scores("s3", qT, kT)
                rows2(j3, g, "v3", W3["v3"], xT)
                probs_v(1, "p3", "o3", V3, "v3")
                ready(j3, g, ("o3", 0))
                ready(j3, g, ("o3", 1))
                turn_rows(j3, g, "aT", AO)
                ready(j3, g, ("aT", 0))
                ready(j3, g, ("aT", 1))
                cols(j3, g, "q4", W3["q4"], aT)
                ready(j3, g, ("q4", 0))
                ready(j3, g, ("q4", 1))
                scores("s4", qT, k4T)
                probs_v(2, "p4", "o4", V4, "v4")
                norm_cols(3, "nT", N2)
                cols(j3, g, "h", W3["h"], xT)
                pe.wait_ge(sem("leaky"), g + 1)
                rows2(j3, g, "ff", W3["ff"], hT3)
                norm_cols(4, "xT7", XN)
                logits(j3, g, "lg1", Wr[3])
                list_ranks(j3, g, g + GROUPS)

            pe.wait_ge(sem("masks_built"), 1)
            pe.wait_ge(sem("const_loaded"), 16 * len(consts))
            for m in range(KC):
                ps, b = fill(pre, 0, ("wab", m))
                mm(ps[:, 0:D], LORA_A[:, m * P:(m + 1) * P], LORA_B[:, :]).then_inc(bank_full[b], 1)
            pe.wait_ge(sem("w1_loaded"), 16 * len(w1loads))
            with pe.Fori(0, GROUPS) as g:
                phase1(g)
            routed_start()
            with pe.Fori(0, GROUPS) as g:
                routed(g)
            routed_end()
            with pe.Fori(0, GROUPS) as g:
                layer1(g)

            def all_experts(layer):
                with pe.Fori(0, LOOPS) as i:
                    experts(layer, i, i, *moe[layer][0])
                experts(layer, 0, LOOPS, *moe[layer][1])

            all_experts(1)
            pe.wait_ge(sem("w3_loaded"), 16 * len(w3loads))
            with pe.Fori(0, GROUPS) as g:
                phase3(g)
            all_experts(3)

        @block.scalar
        def _(act):
            fulls = Waits(act)

            def full(plan, g, key):
                b = fulls.at_least(bank_full, plan, key, g, 1)
                return bank[b], b

            def copy_cols(plan, g, name, dst, bias=None):
                for m in range(KC):
                    ps, b = full(plan, g, (name, m))
                    if bias is None:
                        act.activation(dst[:, m, :], ps[:, :], ACT.Copy).then_inc(bank_empty[b], 1)
                    else:
                        act.activation(dst[:, m, :], ps[:, :], ACT.Identity, bias=col_bias[:, bias, m:m + 1]).then_inc(bank_empty[b], 1)

            def phase1(g):
                copy_cols(j1, g, "cT", cT)
                copy_cols(j1, g, "kT", kT, CK0)
                copy_cols(j1, g, "xT0", xT)
                copy_cols(j1, g, "qT", qT, CQ0)
                for n in range(UNITS + 1):
                    if n < UNITS:
                        u = n % 4
                        act.wait_ge(sem("maxima"), UNITS * g + (n + 1))
                        for h in range(8):
                            last = act.activation(SC[:, u, h, :], SC[:, u, h, :], ACT.Exp, bias=MX[:, 32 + 8 * u + h:33 + 8 * u + h])
                        last.then_inc(sem("probs"), 1)
                    if n >= 1:
                        i = n - 1
                        for j in range(2):
                            ps, b = full(j1, g, ("p", i, j))
                            act.activation(PT[:, i % 4, 4 * j:4 * j + 4, :], ps[:, :].rearrange("p (h k) -> p h k", h=4), ACT.Copy).then_inc(bank_empty[b], 1)
                copy_cols(j1, g, "aT", aT)
                copy_cols(j1, g, "xT1", xT)
                b, n = job(j1, ("lg",), g)
                act.wait_ge(bank_empty[b], n + 1)
                act.activation(small[:, 0, :], small[:, 0, :], ACT.Exp).then_inc(sem("logits_exp"), 1)
                for i in range(T + 2):
                    if i < T:
                        t, p = i, PAIR
                        ps, b = full(j1, g, ("up", i))
                        for a in range(2):
                            last = act.activation(SG0[:, b, a * P:(a + 1) * P], ps[:, a * 256:a * 256 + P], ACT.Silu)
                        last.then_inc(sem("silu_rows"), 1)
                    if i >= 2:
                        ps, b = full(j1, g, ("hT", i - 2))
                        act.activation(HT0[:, (i - 2) % 3, :], ps[:, 0:256], ACT.Copy).then_inc(bank_empty[b], 1)

            def routed(g):
                ps, b = full(jr, g, ("ow",))
                act.activation(OWT, ps[:, :].rearrange("p (t n) -> p t n", t=T), ACT.Copy).then_inc(bank_empty[b], 1)
                for t in range(T):
                    ps, b = full(jr, g, ("gu", t))
                    act.activation(SGR[:, t, :, :], ps[:, :].rearrange("p (k n) -> p k n", k=2)[:, :, 0:HID0], ACT.Silu).then_inc(sem("routed_silu"), 1)

            def layer1(g):
                act.wait_ge(sem("shifted16"), g + 1)
                act.activation(EXTRA[:, 1024:2048], EXTRA[:, 1024:2048], ACT.Exp).then_inc(sem("probs16"), 1)
                copy_cols(j2, g, "xT3", xT)
                router_exps(g)

            def router_exps(turn):
                act.wait_ge(sem("router_in"), 2 * turn + 1)
                act.activation(small[:, 1, :], small[:, 1, :], ACT.Exp).then_inc(sem("router_exp"), 1)
                act.wait_ge(sem("router_in"), 2 * turn + 2)
                act.activation(small[:, 8, 0:T], small[:, 8, 0:T], ACT.Exp).then_inc(sem("router_exp"), 1)

            def experts(layer, turn, pair, steps, plan):
                hc = HIDS[layer] // P
                for s in steps:
                    if s[0] == "up":
                        ps, b = full(plan, turn, s)
                        act.activation(SG[:, b, :], ps[:, 0:256], ACT.Silu).then_inc(sem("silu_slots"), 1)
                    elif s[0] == "down" and s[2] == hc - 1:
                        u = s[1]
                        ps, b = full(plan, turn, ("acc", "y", u, 0))
                        act.wait_ge(sem(f"result_free{u}"), pair + (PRIMED + tiles_before[layer][u]))
                        act.activation(YS[:, u, 0, :], ps[:, 0:D], ACT.Copy).then_inc(bank_empty[b], 1)

            def phase3(g):
                copy_cols(j3, g, "cT", cT)
                copy_cols(j3, g, "k2", kT, CK2)
                copy_cols(j3, g, "xT4", xT)
                copy_cols(j3, g, "q2", qT, CQ2)
                copy_cols(j3, g, "k4", k4T)

                def soft(i, name):
                    act.wait_ge(sem("shifted"), 3 * g + (i + 1))
                    act.activation(SC2, SC2, ACT.Exp).then_inc(sem("probs"), 1)
                    ps, b = full(j3, g, (name,))
                    act.activation(PT2, ps[:, :].rearrange("p (t k) -> p t k", t=T), ACT.Copy).then_inc(bank_empty[b], 1)

                soft(0, "p2")
                copy_cols(j3, g, "oT2", aT)
                copy_cols(j3, g, "xT5", xT)
                copy_cols(j3, g, "xT6", xT)
                copy_cols(j3, g, "q3", qT)
                copy_cols(j3, g, "k3", kT)
                for a in range(2):
                    ps, b = full(j3, g, ("v3", a))
                    act.activation(V3[:, 2 * a:2 * a + 2, :], ps[:, :].rearrange("p (t n) -> p t n", t=2), ACT.Copy).then_inc(bank_empty[b], 1)
                soft(1, "p3")
                copy_cols(j3, g, "aT", aT)
                copy_cols(j3, g, "q4", qT)
                soft(2, "p4")
                copy_cols(j3, g, "nT", xT)
                copy_cols(j3, g, "xT7", xT)
                router_exps(g + GROUPS)

            act.wait_ge(sem("zero_set"), 1)
            for i in range(zrows.shape[0]):
                act.dma_start(zrows[i, :, :].rearrange("p (r d) -> p r d", d=D), rep(ZERO[:, :], ZCHUNK)).then_inc(sem("lists_zeroed"), 16)
            for i in range(yrows.shape[0]):
                act.dma_start(yrows[i, :, :].rearrange("p (r d) -> p r d", d=D), rep(ZERO[:, :], ZCHUNK)).then_inc(sem("results_zeroed"), 16)
            act.wait_ge(sem("const_loaded"), 16 * len(consts))
            with act.Fori(0, GROUPS) as g:
                phase1(g)
            with act.Fori(0, GROUPS) as g:
                routed(g)
            with act.Fori(0, GROUPS) as g:
                layer1(g)

            def all_experts(layer):
                with act.Fori(0, LOOPS) as i:
                    experts(layer, i, i, *moe[layer][0])
                experts(layer, 0, LOOPS, *moe[layer][1])

            all_experts(1)
            with act.Fori(0, GROUPS) as g:
                phase3(g)
            all_experts(3)

        @block.vector
        def _(dve):
            step = [0, 0, 0]
            turn_of = [0]

            def d(ins):
                ins.then_inc(sem("dve_step"), 1)
                step[2] += 1
                return ins

            def settle():
                dve.wait_ge(sem("dve_step"), turn_of[0] * step[1] + (step[0] + step[2]))

            def alone():
                dve.sem_inc(sem("dve_passed"), 1)

            def enter(turn, per):
                turn_of[0], step[1], step[2] = turn, per, 0

            def leave(turns):
                assert step[2] == step[1], f"steps of a turn: {step[2]}"
                step[0] += step[1] * turns
                turn_of[0], step[1], step[2] = 0, 0, 0

            fulls, empties = Waits(dve), Waits(dve)

            def full(plan, g, key):
                b = fulls.at_least(bank_full, plan, key, g, 1)
                return bank[b], b

            def evacuated(plan, g, key):
                empties.at_least(bank_empty, plan, key, g, 1)

            def tt(o, a, b, op):
                return dve.tensor_tensor(o, a, b, op)

            def norm(src, dst, eps, count, last=None):
                for t in range(T):
                    d(dve.bn_stats(ST[:, t, :], src(t)))
                settle()
                alone()
                for t in range(T):
                    d(dve.bn_aggr(MV[:, t, :], ST[:, t, :]))
                settle()
                dve.tensor_scalar(VE[:, :], MV[:, :, 1], eps, None, ALU.add).then_inc(sem("variance"), 1)
                dve.wait_ge(sem("rstd"), count)
                for t in range(T):
                    i = dve.tensor_scalar(dst(t), src(t), MV[:, t, 0:1], RS[:, t:t + 1], ALU.subtract, ALU.mult)
                    if t < T - 1 or last is None:
                        d(i)
                    else:
                        i.then_inc(sem(last), 1)

            def rank(v, n, lower, o):
                gt = cmpa[:, 0:T * n * n].rearrange("p (t i j) -> p t i j", t=T, i=n)
                eq = cmpb[:, 0:T * n * n].rearrange("p (t i j) -> p t i j", t=T, i=n)
                settle()
                d(tt(gt, rep(v, n, 2), bc(v, n), ALU.is_gt))
                d(tt(eq, rep(v, n, 2), bc(v, n), ALU.is_equal))
                settle()
                d(tt(eq, eq, rep(lower[:, :, :], T), ALU.mult))
                settle()
                d(tt(gt, gt, eq, ALU.add))
                settle()
                d(dve.tensor_reduce(o, gt, AX, ALU.add))
                settle()

            sm = lambda i, n=E: small[:, i, 0:T * n].rearrange("p (t e) -> p t e", t=T)

            def phase1(g):
                norm(lambda t: xg(g, t), lambda t: XN[:, t, :], 1e-5, 2 * g + 1, "normed")
                for t in range(T):
                    ps, b = full(j1, g, ("v", t))
                    tt(V0[:, t, :, 0:HD], ps[:, 0:D].rearrange("p (h d) -> p h d", h=H),
                       row_bias[:, BV0, :].rearrange("p (h d) -> p h d", h=H), ALU.add).then_inc(bank_empty[b], 1)

                def evac_scores(i):
                    for j in range(2):
                        ps, b = full(j1, g, ("s", i, j))
                        tt(SC[:, i % 4, 4 * j:4 * j + 4, :], ps[:, :].rearrange("p (h k) -> p h k", h=4),
                           rep(mask01[:, :], 4), ALU.mult).then_inc(bank_empty[b], 1)

                def maxima(i):
                    u = i % 4
                    if i % 2:
                        dve.wait_ge(sem("biased"), T * g + (i // 2 + 1))
                    else:
                        for j in range(2):
                            evacuated(j1, g, ("s", i, j))
                        d(tt(SC[:, u, :, :], SC[:, u, :, :], SCORE_BIAS[:, 0:8, :], ALU.add))
                        settle()
                    m = MX[:, 8 * u:8 * u + 8]
                    d(dve.tensor_reduce(m, SC[:, u, :, :], AX, ALU.max))
                    settle()
                    dve.tensor_scalar(MX[:, 32 + 8 * u:40 + 8 * u], m, -1.0, None, ALU.mult).then_inc(sem("maxima"), 1)

                def norm_out(t):
                    ps, b = full(j1, g, ("acc", "o", t))
                    o = ps[:, 0:H * VW].rearrange("p (h d) -> p h d", h=H)
                    r = RC[:, H * (t % 2):H * (t % 2) + H]
                    d(dve.reciprocal(r, o[:, :, HD]))
                    settle()
                    tt(AO[:, t, :].rearrange("p (h d) -> p h d", h=H), o[:, :, 0:HD], bc(r, HD), ALU.mult).then_inc(bank_empty[b], 1)

                for n in range(UNITS + 4):
                    if n < UNITS:
                        evac_scores(n)
                    if 1 <= n <= UNITS:
                        maxima(n - 1)
                    if n >= 5 and n % 2:
                        norm_out((n - 5) // 2)
                dve.wait_ge(sem("x_biased"), g + 1)
                for t in range(T):
                    ps, b = full(j1, g, ("xo", t))
                    tt(xg(g, t), xg(g, t), ps[:, 0:D], ALU.add).then_inc(bank_empty[b], 1)
                for t in range(T):
                    evacuated(j1, g, ("xo", t))
                alone()
                norm(lambda t: xg(g, t), lambda t: XN[:, t, :], 1e-5, 2 * g + 2, "normed")

                ps, b = full(j1, g, ("lg",))
                l = ps[:, 0:T * E].rearrange("p (t e) -> p t e", t=T)
                d(dve.tensor_reduce(MX[:, 0:T], l, AX, ALU.max))
                settle()
                tt(sm(0), l, bc(MX[:, 0:T], E), ALU.subtract).then_inc(bank_empty[b], 1)
                dve.wait_ge(sem("logits_exp"), g + 1)
                d(dve.tensor_reduce(MX[:, T:2 * T], sm(0), AX, ALU.add))
                settle()
                d(dve.reciprocal(RC[:, 0:T], MX[:, T:2 * T]))
                settle()
                d(tt(sm(1), sm(0), bc(RC[:, 0:T], E), ALU.mult))
                settle()
                d(tt(sm(2), sm(1), rep(ebias[:, :], T), ALU.add))
                settle()
                d(dve.tensor_reduce(small[:, 3, 0:4 * T], small[:, 2, :].rearrange("p (a b) -> p a b", b=2), AX, ALU.add))
                rank(sm(3, 4), 4, lower4, small[:, 4, 0:4 * T].rearrange("p (t e) -> p t e", t=T))
                d(dve.tensor_scalar(small[:, 5, 0:4 * T], small[:, 4, 0:4 * T], 2.0, None, ALU.is_lt))
                settle()
                d(dve.tensor_scalar(small[:, 6, 0:4 * T], small[:, 5, 0:4 * T], 1e30, -1e30, ALU.mult, ALU.add))
                pairs = lambda i: small[:, i, :].rearrange("p (a b) -> p a b", b=2)
                d(tt(pairs(7), pairs(2), bc(small[:, 5, 0:4 * T], 2), ALU.mult))
                settle()
                d(tt(pairs(7), pairs(7), bc(small[:, 6, 0:4 * T], 2), ALU.add))
                rank(sm(7), E, lower8, RANK[:, :, :])
                for k in range(2):
                    d(dve.tensor_scalar(OH[:, :, k, :], RANK[:, :, :], float(k), None, ALU.is_equal))
                settle()
                d(dve.tensor_copy(SRC[:, ds(g * 2 * T * E, 2 * T * E)], OH[:, :, :, :].rearrange("p t k e -> p (t k e)")))
                d(tt(OHT[:, :, :, :], OH[:, :, :, :], rep(sm(1), 2, 2), ALU.mult))
                d(dve.tensor_copy(X8[:, ds(g * KC * E, KC * E)].rearrange("p (c s) -> p c s", c=KC), xT[:, :, 0:E]))
                settle()
                d(dve.tensor_reduce(WV[:, ds(g * 2 * T, 2 * T)], OHT[:, :, :, :].rearrange("p t k e -> p (t k) e"), AX, ALU.add))

                def add_y(t):
                    ps, b = full(j1, g, ("acc", "y", t))
                    tt(xg(g, t), xg(g, t), ps[:, 0:D], ALU.add).then_inc(bank_empty[b], 1)

                for i in range(T):
                    ps, b = full(j1, g, ("up", i))
                    dve.wait_ge(sem("silu_rows"), T * g + (i + 1))
                    pair = ps[:, :].rearrange("p (a n) -> p a n", a=2)
                    tt(HB0[:, i % 3, :].rearrange("p (a n) -> p a n", a=2), pair[:, :, P:2 * P],
                       SG0[:, b, :].rearrange("p (a n) -> p a n", a=2), ALU.mult).then_inc(bank_empty[b], 1)
                    if i > 0:
                        add_y(i - 1)
                add_y(T - 1)
                for t in reversed(range(T)):
                    evacuated(j1, g, ("acc", "y", t))
                settle()

            def routed_start():
                flat3 = lambda ap: ap.rearrange("p (a e) -> p a e", e=E)
                d(dve.memset(XE, 0.0))
                d(dve.memset(HS, 0.0))
                d(dve.memset(GT, 0.0))
                d(dve.tensor_reduce(small[:, 0, 0:E], SRC[:, :].rearrange("p (a e) -> p e a", e=E), AX, ALU.add))
                settle()
                dve.tensor_copy(SEL[:, 0, :], small[:, 0, 0:E]).then_inc(sem("choices_counted"), 1)
                for half in range(2):
                    i = dve.tensor_copy(XE.rearrange("p c (e n) -> p c e n", n=DIAG)[:, :, :, E * E * half:E * E * half + E],
                                        rep(X8[:, 0:KC * E].rearrange("p (c s) -> p c s", c=KC), E, 2))
                    i.then_inc(sem("first_rows_spread"), 1)
                ps, b = full(jr0, 0, ("cnt",))
                dve.tensor_copy(small[:, 1, 0:E], ps[:, 0:E]).then_inc(bank_empty[b], 1)
                evacuated(jr0, 0, ("cnt",))
                count, begin, end = small[:, 1, 0:E], small[:, 2, 0:E], small[:, 3, 0:E]
                before = cmpa[:, 0:E * E].rearrange("p (i j) -> p i j", i=E)
                d(tt(before, lower8[:, :, :], rep(count, E), ALU.mult))
                settle()
                d(dve.tensor_reduce(begin, before, AX, ALU.add))
                settle()
                d(tt(end, begin, count, ALU.add))
                place = bc(FLAT[:, :], E)
                d(tt(flat3(EO), place, rep(begin, 2 * TILES), ALU.is_ge))
                settle()
                d(tt(flat3(cmpb[:, :]), place, rep(end, 2 * TILES), ALU.is_lt))
                settle()
                d(tt(EO, EO, cmpb[:, :], ALU.mult))
                ps, b = full(jr0, 0, ("gt",))
                d(dve.tensor_copy(GT[0:64, 0:256], ps[0:64, 0:256]))
                dve.tensor_copy(GT[64:P, 256:512], ps[64:P, 0:256]).then_inc(bank_empty[b], 1)
                settle()

            def routed(g):
                eo = EO[:, ds(g * 2 * T * E, 2 * T * E)].rearrange("p (a e) -> p a e", e=E)
                src = SRC[:, ds(g * 2 * T * E, 2 * T * E)].rearrange("p (a e) -> p a e", e=E)
                d(tt(OHS.rearrange("p a (e s) -> p a e s", e=E), bc(eo, E), rep(src, E, 2), ALU.mult))
                settle()
                tt(OWS.rearrange("p t (k n) -> p (t k) n", k=2), OHS, bc(WV[:, ds(g * 2 * T, 2 * T)], E * E), ALU.mult).then_inc(sem("pairs_built"), 1)
                for t in range(T):
                    ps, b = full(jr, g, ("gu", t))
                    dve.wait_ge(sem("routed_silu"), T * g + (t + 1))
                    tt(HR[:, 2 * t:2 * t + 2, :], ps[:, :].rearrange("p (k n) -> p k n", k=2)[:, :, HID0:2 * HID0],
                       SGR[:, t, :, :], ALU.mult).then_inc(bank_empty[b], 1)
                ps, b = full(jr, g, ("hs",))
                tt(HS, HS, ps[:, 0:64], ALU.add).then_inc(bank_empty[b], 1)
                evacuated(jr, g, ("hs",))
                alone()

            def routed_end():
                ps, b = full(jr1, 0, ("dn",))
                tt(X[0:E, 0:D], X[0:E, 0:D], ps[0:E, 0:D], ALU.add).then_inc(bank_empty[b], 1)
                evacuated(jr1, 0, ("dn",))

            def layer1(g):
                alone()
                norm(lambda t: xg(g, t), lambda t: AO[:, t, :], 1e-5, 2 * g + (2 * GROUPS + 1), "normed")

                d(dve.memset(S16, 0.0))
                settle()

                def sums(pr, dst, signal):
                    off = 0
                    for k in range(4):
                        last = dst(k, pr[:, off:off + 4 * PAIRBLK[k] * HD])
                        off += 4 * PAIRBLK[k] * HD
                        if k < 3 or not signal:
                            d(last)
                    if signal:
                        last.then_inc(sem("products_used"), 1)

                def score_sums(t, pr, signal):
                    sums(pr, lambda k, part: dve.tensor_reduce(S16[:, t, 4 * k:4 * k + 4, 0:PAIRBLK[k]],
                                                               part.rearrange("p (h k d) -> p h k d", h=4, d=HD), AX, ALU.add), signal)

                def value_sums(t, pr, signal):
                    sums(pr, lambda k, part: dve.tensor_reduce(O16[:, t, 64 * k:64 * k + 64].rearrange("p (h d) -> p h d", h=4),
                                                               part.rearrange("p (h d k) -> p h d k", h=4, d=HD), AX, ALU.add), signal)

                def both(products, total, first):
                    for i in range(2):
                        for part in products(tt, PRD, 2 * i + 1):
                            d(part)
                        settle()
                        total(2 * i + 1, PRD, False)
                        dve.wait_ge(sem("products"), 4 * g + (first + i + 1))
                        total(2 * i, PR, True)
                        settle()

                dve.wait_ge(sem("ctx_loaded"), 16 * (g + (GROUPS + 1)))
                dve.wait_ge(sem("normed"), 2 * g + (2 * GROUPS + 1))
                both(score_products, score_sums, 0)
                dve.wait_ge(sem("products_used"), 4 * g + 2)
                settle()
                sv, sbv = EXTRA[:, 0:1024].rearrange("p (t n) -> p t n", t=T), EXTRA[:, 1024:2048].rearrange("p (t n) -> p t n", t=T)
                d(dve.scalar_tensor_tensor(sbv, sv, float(HD) ** -0.5, rep(causal16[:, :, :].rearrange("p h k -> p (h k)"), T), ALU.mult, ALU.add))
                settle()
                rows = EXTRA[:, 1024:2048].rearrange("p (a k) -> p a k", k=H)
                d(dve.tensor_reduce(MX[:, :], rows, AX, ALU.max))
                settle()
                tt(rows, rows, bc(MX[:, :], H), ALU.subtract).then_inc(sem("shifted16"), 1)
                dve.wait_ge(sem("probs16"), g + 1)
                d(dve.tensor_reduce(MX[:, :], rows, AX, ALU.add))
                settle()
                d(dve.reciprocal(RC[:, :], MX[:, :]))
                both(value_products, value_sums, 2)
                dve.wait_ge(sem("products_used"), 4 * g + 4)
                settle()
                o = EXTRA[:, 2048:3072].rearrange("p (a d) -> p a d", d=HD)
                d(tt(o, o, bc(RC[:, :], HD), ALU.mult))
                settle()
                d(tt(X[:, ds(g * T * D, T * D)], X[:, ds(g * T * D, T * D)], EXTRA[:, 2048:3072], ALU.add))
                settle()
                dve.wait_ge(sem("norm_rows_free"), g + PRIMED)
                alone()
                norm(lambda t: xg(g, t), lambda t: XN[:, t, :], 1e-5, 2 * g + (2 * GROUPS + 2), "normed")
                lists(j2, g, g, True)

            def lists(plan, g, turn, of_probs):
                ps, b = full(plan, g, ("lg1",))
                dve.tensor_copy(sm(2), ps[:, 0:T * E].rearrange("p (t e) -> p t e", t=T)).then_inc(bank_empty[b], 1)
                evacuated(plan, g, ("lg1",))
                d(dve.tensor_reduce(MX[:, 0:T], sm(2), AX, ALU.max))
                settle()
                tt(sm(1), sm(2), bc(MX[:, 0:T], E), ALU.subtract).then_inc(sem("router_in"), 1)
                rank(sm(2), E, lower8, RANK[:, :, :])
                dve.tensor_scalar(SEL[:, :, :], RANK[:, :, :], 2.0, None, ALU.is_lt).then_inc(sem("selected"), 1)
                d(dve.tensor_scalar(OH[:, :, 0, :], RANK[:, :, :], 0.0, None, ALU.is_equal))
                d(dve.tensor_scalar(OH[:, :, 1, :], RANK[:, :, :], 1.0, None, ALU.is_equal))
                dve.wait_ge(sem("router_exp"), 2 * turn + 1)
                v = sm(2)
                if of_probs:
                    d(dve.tensor_reduce(MX[:, T:2 * T], sm(1), AX, ALU.add))
                    settle()
                    d(dve.reciprocal(RC[:, 0:T], MX[:, T:2 * T]))
                    settle()
                    d(tt(sm(3), sm(1), bc(RC[:, 0:T], E), ALU.mult))
                    v = sm(3)
                settle()
                d(tt(OHT[:, :, :, :], OH[:, :, :, :], rep(v, 2, 2), ALU.mult))
                settle()
                d(dve.tensor_reduce(sm(4, 2), OHT[:, :, :, :], AX, ALU.add))
                settle()
                two = sm(4, 2)
                tt(small[:, 8, 0:T], two[:, :, 1], two[:, :, 0], ALU.subtract).then_inc(sem("router_in"), 1)
                dve.wait_ge(sem("router_exp"), 2 * turn + 2)
                d(dve.tensor_scalar(small[:, 5, 0:T], small[:, 8, 0:T], 1.0, None, ALU.add))
                settle()
                d(dve.reciprocal(small[:, 6, 0:T], small[:, 5, 0:T]))
                settle()
                d(tt(small[:, 7, 0:T], small[:, 6, 0:T], small[:, 8, 0:T], ALU.mult))
                cw = CW[:, ds(g * 2 * T, 2 * T)].rearrange("p (t k) -> p t k", k=2)
                d(dve.tensor_copy(cw[:, :, 0], small[:, 6, 0:T]))
                settle()
                d(dve.tensor_copy(cw[:, :, 1], small[:, 7, 0:T]))
                ps, b = full(plan, g, ("rk",))
                d(tt(sm(10), ps[:, 0:T * E].rearrange("p (t e) -> p t e", t=T), rep(base[:, :], T), ALU.add))
                settle()
                tt(base[:, :], base[:, :], ps[:, T * E:(T + 1) * E], ALU.add).then_inc(bank_empty[b], 1)
                d(tt(sm(11), sm(10), rep(region0[:, :], T), ALU.add))
                settle()
                d(tt(OHT[:, :, :, :], OH[:, :, :, :], rep(sm(11), 2, 2), ALU.mult))
                settle()
                d(dve.tensor_reduce(sm(12, 2), OHT[:, :, :, :], AX, ALU.add))
                settle()
                d(dve.tensor_copy(IDX[:, ds(g * 2 * T, 2 * T)], small[:, 12, 0:2 * T]))
                dve.tensor_copy(IDXG[:, :], small[:, 12, 0:2 * T]).then_inc(sem("slots_found"), 1)
                evacuated(plan, g, ("rk",))
                settle()

            def plan_tiles():
                J = MOE_TILES
                w = lambda i: wide[0:1, i, :].rearrange("p (j e) -> p j e", e=E)
                r = lambda i: t8[0:1, i, :]
                d(dve.tensor_scalar(r(0), base[0:1, :], float(SLOT - 1), None, ALU.add))
                settle()
                d(dve.tensor_copy(lens_i[0:1, :], r(0)))
                settle()
                d(dve.tensor_scalar(lens_i[0:1, :], lens_i[0:1, :], SLOT.bit_length() - 1, None, ALU.logical_shift_right))
                settle()
                d(dve.tensor_copy(r(1), lens_i[0:1, :]))
                settle()
                d(dve.tensor_copy(r(2), r(1)))
                for e in range(1, E):
                    settle()
                    d(tt(t8[0:1, 2, e:e + 1], t8[0:1, 2, e - 1:e], t8[0:1, 1, e:e + 1], ALU.add))
                settle()
                d(tt(r(3), r(2), r(1), ALU.subtract))
                j = jrow[0:1, :].rearrange("p (j e) -> p j e", e=E)
                d(tt(w(0), j, rep(r(2), J), ALU.is_ge))
                settle()
                d(tt(w(1), j, rep(r(3), J), ALU.is_ge))
                d(tt(w(2), j, rep(r(3), J), ALU.subtract))
                settle()
                d(tt(w(1), w(1), w(0), ALU.subtract))
                d(tt(w(2), w(2), rep(r(5), J), ALU.add))
                settle()
                d(tt(w(2), w(2), w(1), ALU.mult))
                d(dve.tensor_reduce(wide[0:1, 3, 0:J], w(0), AX, ALU.add))
                settle()
                d(dve.tensor_reduce(wide[0:1, 4, 0:J], w(2), AX, ALU.add))
                d(dve.tensor_scalar(wide[0:1, 3, 0:J], wide[0:1, 3, 0:J], float(E - 1), None, ALU.min))
                settle()
                d(dve.scalar_tensor_tensor(wide[0:1, 5, 0:J], w(0)[:, :, E - 1], float(SPARE), wide[0:1, 4, 0:J], ALU.mult, ALU.add))
                d(dve.tensor_copy(tile_e[0:1, :], wide[0:1, 3, 0:J]))
                settle()
                dve.tensor_copy(tile_r[0:1, :], wide[0:1, 5, 0:J]).then_inc(sem("tiles_planned"), 1)
                d(dve.memset(base[:, :], 0.0))
                settle()

            def experts(layer, turn, pair, steps, plan):
                hc = HIDS[layer] // P
                first = 0 if layer == 1 else MOE_TILES * (HIDS[1] // P)
                n = 0
                for s in steps:
                    if s[0] == "xsT":
                        ps, b = full(plan, turn, s)
                        dve.tensor_copy(xsT[:, s[1], :, :], ps[:, :].rearrange("p (c n) -> p c n", c=KC)).then_inc(bank_empty[b], 1)
                    elif s[0] == "up":
                        _, u, c = s
                        n += 1
                        ps, b = full(plan, turn, s)
                        dve.wait_ge(sem("silu_slots"), pair * (2 * hc) + (first + n))
                        tt(HT[:, c, :], ps[:, 256:512], SG[:, b, :], ALU.mult).then_inc(bank_empty[b], 1)
                    elif s[2] == hc - 1:
                        u = s[1]
                        ps, b = full(plan, turn, ("acc", "y", u, 1))
                        dve.wait_ge(sem(f"result_free{u}"), pair + (PRIMED + tiles_before[layer][u]))
                        dve.tensor_copy(YS[:, u, 1, :], ps[:, 0:D]).then_inc(bank_empty[b], 1)

            def all_experts(layer):
                with dve.Fori(0, LOOPS) as i:
                    experts(layer, i, i, *moe[layer][0])
                experts(layer, 0, LOOPS, *moe[layer][1])

            def combine(g, turn):
                d(dve.tensor_copy(CWP[:, :], CW[:, ds(g * 2 * T, 2 * T)]))
                dve.wait_ge(sem("rows_gathered"), 16 * 2 * T * (turn + 1))
                settle()
                for t in range(T):
                    d(dve.scalar_tensor_tensor(xg(g, t), YA[:, 2 * t, :], CWP[:, 2 * t:2 * t + 1], xg(g, t), ALU.mult, ALU.add))
                settle()

            def phase3(g):
                combine(g, g)
                for t in range(T):
                    i = dve.scalar_tensor_tensor(xg(g, t), YA[:, 2 * t + 1, :], CWP[:, 2 * t + 1:2 * t + 2], xg(g, t), ALU.mult, ALU.add)
                    i.then_inc(sem("combined"), 1)
                dve.wait_ge(sem("combined"), PRIMED + T * (g + 1))
                dve.wait_ge(sem("norm_rows_free"), g + (PRIMED + GROUPS))
                alone()
                n0 = 4 * GROUPS + 7 * g
                xrows, xn = (lambda t: xg(g, t)), (lambda t: XN[:, t, :])
                norm(xrows, xn, 1e-5, n0 + 1, "normed")
                two = lambda ps: ps[:, :].rearrange("p (t n) -> p t n", t=2)
                four = lambda ps: ps[:, :].rearrange("p (t n) -> p t n", t=T)
                xhalf = lambda a: X[:, ds((T * g + 2 * a) * D, 2 * D)]

                for a in range(2):
                    ps, b = full(j3, g, ("v2", a))
                    tt(V2[:, 2 * a:2 * a + 2, :], two(ps), rep(row_bias[:, BV2, :], 2), ALU.add).then_inc(bank_empty[b], 1)

                def softmax_rows(i, name):
                    d(dve.tensor_reduce(MX[:, 0:T], SC2, AX, ALU.max))
                    settle()
                    tt(SC2, SC2, bc(MX[:, 0:T], P), ALU.subtract).then_inc(sem("shifted"), 1)
                    dve.wait_ge(sem("probs"), 2 * TILES + 3 * g + (i + 1))
                    d(dve.tensor_reduce(MX[:, T:2 * T], SC2, AX, ALU.add))
                    settle()
                    d(dve.reciprocal(RC[:, 0:T], MX[:, T:2 * T]))
                    settle()

                ps, b = full(j3, g, ("s2",))
                km = keymask[:, ds(g * T * P, T * P)]
                dve.scalar_tensor_tensor(BIG[:, 0:512], ps[:, :], float(D) ** -0.5, km, ALU.mult, ALU.mult).then_inc(bank_empty[b], 1)
                evacuated(j3, g, ("s2",))
                d(dve.tensor_scalar(NBG[:, :], km, 1e9, -1e9, ALU.mult, ALU.add))
                settle()
                d(tt(BIG[:, 0:512], BIG[:, 0:512], NBG[:, :], ALU.add))
                settle()
                softmax_rows(0, "s2")
                for a in range(2):
                    ps, b = full(j3, g, ("v4", a))
                    dve.tensor_copy(V4[:, 2 * a:2 * a + 2, :], two(ps)).then_inc(bank_empty[b], 1)
                for a in range(2):
                    ps, b = full(j3, g, ("o2", a))
                    tt(AO[:, 2 * a:2 * a + 2, :], two(ps), bc(RC[:, 2 * a:2 * a + 2], D), ALU.mult).then_inc(bank_empty[b], 1)

                def add_to_x(name, n):
                    dve.wait_ge(sem("x_biased"), GROUPS + 2 * g + n)
                    for a in range(2):
                        ps, b = full(j3, g, (name, a))
                        tt(xhalf(a), xhalf(a), ps[:, :], ALU.add).then_inc(bank_empty[b], 1)
                    for a in range(2):
                        evacuated(j3, g, (name, a))
                    alone()

                add_to_x("x2", 1)
                norm(xrows, xn, 1e-5, n0 + 2, "normed")
                add_to_x("f2", 2)
                norm(xrows, lambda t: IN3[:, t, :], 1e-5, n0 + 3, "normed")
                ps, b = full(j3, g, ("s3",))
                dve.scalar_tensor_tensor(SC2, four(ps), float(P) ** -0.5, rep(causal[:, :], T), ALU.mult, ALU.add).then_inc(bank_empty[b], 1)
                evacuated(j3, g, ("s3",))
                softmax_rows(1, "s3")
                for a in range(2):
                    ps, b = full(j3, g, ("o3", a))
                    tt(AO[:, 2 * a:2 * a + 2, :], two(ps), bc(RC[:, 2 * a:2 * a + 2], D), ALU.mult).then_inc(bank_empty[b], 1)
                for a in range(2):
                    evacuated(j3, g, ("o3", a))
                d(tt(R3, AO[:, :, :], IN3, ALU.add))
                settle()
                r3 = lambda t: R3[:, t, :]
                norm(r3, lambda t: N1[:, t, :], 1e-3, n0 + 4, "n1_raw")
                ps, b = full(j3, g, ("s4",))
                dve.tensor_scalar(BIG[:, 0:512], ps[:, :], float(P) ** -0.5, None, ALU.mult).then_inc(bank_empty[b], 1)
                evacuated(j3, g, ("s4",))
                softmax_rows(2, "s4")
                for a in range(2):
                    ps, b = full(j3, g, ("o4", a))
                    tt(R3[:, 2 * a:2 * a + 2, :], two(ps), bc(RC[:, 2 * a:2 * a + 2], D), ALU.mult).then_inc(bank_empty[b], 1)
                for a in range(2):
                    evacuated(j3, g, ("o4", a))
                dve.wait_ge(sem("n1_ready"), g + 1)
                d(tt(R3, R3, N1, ALU.add))
                settle()
                norm(r3, lambda t: N2[:, t, :], 1e-3, n0 + 5)
                settle()
                d(tt(N2, N2, rep(row_bias[:, GAM, :], T), ALU.mult))
                settle()
                tt(N2, N2, rep(row_bias[:, BET, :], T), ALU.add).then_inc(sem("normed"), 1)
                for m in range(KC):
                    ps, b = full(j3, g, ("h", m))
                    dve.tensor_scalar(hTt[:, m, :], ps[:, :], col_bias[:, CB1, m:m + 1], None, ALU.add).then_inc(bank_empty[b], 1)
                for m in range(KC):
                    evacuated(j3, g, ("h", m))
                dve.scalar_tensor_tensor(hT3, hTt, 0.2, hTt, ALU.mult, ALU.max).then_inc(sem("leaky"), 1)
                dve.wait_ge(sem("n2_biased"), g + 1)
                for a in range(2):
                    ps, b = full(j3, g, ("ff", a))
                    tt(R3[:, 2 * a:2 * a + 2, :], two(ps), N2B[:, 2 * a:2 * a + 2, :], ALU.add).then_inc(bank_empty[b], 1)
                for a in range(2):
                    evacuated(j3, g, ("ff", a))
                norm(r3, lambda t: N1[:, t, :], 1e-3, n0 + 6)
                settle()
                d(tt(N1, N1, rep(row_bias[:, GAM, :], T), ALU.mult))
                settle()
                d(tt(N1, N1, rep(row_bias[:, BET, :], T), ALU.add))
                settle()
                x4 = X[:, ds(g * T * D, T * D)]
                d(dve.scalar_tensor_tensor(x4, BIG[:, 6144:7168], 0.0, x4, ALU.max, ALU.add))
                settle()
                alone()
                norm(xrows, xn, 1e-5, n0 + 7, "normed")
                lists(j3, g, g + GROUPS, False)

            def quantized_weight():
                d(dve.tensor_reduce(MX[:, 0:1], KER, mybir.AxisListType.XY, ALU.max, apply_absolute_value=True))
                settle()
                dve.tensor_copy(MX[:, 1:2], MX[:, 0:1]).then_inc(sem("absmax"), 1)
                dve.wait_ge(sem("absmax_all"), 1)
                d(dve.tensor_scalar(MX[:, 4:5], MX[:, 2:3], 1.0 / 7.0, None, ALU.mult))
                settle()
                d(dve.reciprocal(MX[:, 3:4], MX[:, 4:5]))
                settle()
                q = QTMP
                d(dve.tensor_scalar(q, KER, MX[:, 3:4], None, ALU.mult))
                settle()
                half = 1.5 * 2.0 ** 23
                d(dve.tensor_scalar(q, q, half, -half, ALU.add, ALU.add))
                settle()
                d(dve.tensor_scalar(q, q, -8.0, 7.0, ALU.max, ALU.min))
                settle()
                for m in range(KC):
                    dve.scalar_tensor_tensor(WEFF[:, m, :], q[:, m, :], MX[:, 4:5], LAB[:, m, :], ALU.mult, ALU.add).then_inc(sem("weff_ready"), 1)

            dve.wait_ge(sem("const_loaded"), 16 * len(consts))
            dve.wait_ge(sem("masks_built"), 1)
            d(dve.tensor_copy(mask01[:, :], maski[:, :]))
            d(dve.tensor_copy(keymask[:, :], keymask8[:, :].bitcast(U8)))
            settle()
            d(dve.tensor_scalar(mask01[:, :], mask01[:, :], 0.0, None, ALU.not_equal))
            d(dve.tensor_scalar(DIST, DIST, 0.0, None, ALU.max))
            settle()
            d(tt(DIST, DIST, mask01[:, :], ALU.mult))
            d(dve.tensor_scalar(NEG, mask01[:, :], 1e9, -1e9, ALU.mult, ALU.add))
            settle()
            for h in range(H):
                i = dve.scalar_tensor_tensor(SCORE_BIAS[:, h, :], DIST, -(0.5 ** (h + 1)), NEG, ALU.mult, ALU.add)
                if h < H - 1:
                    d(i)
            i.then_inc(sem("score_bias_ready"), 1)
            for m in range(KC):
                ps, b = full(pre, 0, ("wab", m))
                dve.tensor_copy(LAB[:, m, :], ps[:, 0:D]).then_inc(bank_empty[b], 1)
            dve.wait_ge(sem("x_loaded"), 16)
            step[0], step[2] = step[2], 0
            enter_loop = dve.Fori(0, GROUPS)
            with enter_loop as g:
                enter(g, STEPS["phase1"])
                phase1(g)
            leave(GROUPS)

            def straight(body):
                step[1] = 0
                body()
                step[0], step[2] = step[0] + step[2], 0

            straight(routed_start)
            with dve.Fori(0, GROUPS) as g:
                enter(g, STEPS["routed"])
                routed(g)
            leave(GROUPS)
            routed_end()
            with dve.Fori(0, GROUPS) as g:
                enter(g, STEPS["layer1"])
                layer1(g)
            leave(GROUPS)

            straight(plan_tiles)
            all_experts(1)
            dve.wait_ge(sem("w3_loaded"), 16 * len(w3loads))
            straight(quantized_weight)
            with dve.Fori(0, GROUPS) as g:
                enter(g, STEPS["phase3"])
                phase3(g)
            leave(GROUPS)
            straight(plan_tiles)
            all_experts(3)
            with dve.Fori(0, GROUPS) as g:
                enter(g, STEPS["last"])
                dve.wait_ge(sem("x_final"), g + PRIMED)
                alone()
                combine(g, g + GROUPS)
                for t in range(T):
                    i = dve.scalar_tensor_tensor(xg(g, t), YA[:, 2 * t + 1, :], CWP[:, 2 * t + 1:2 * t + 2], xg(g, t), ALU.mult, ALU.add)
                    if t < T - 1:
                        d(i)
                i.then_inc(sem("x_final"), 1)
            leave(GROUPS)

        @block.gpsimd
        def _(pool):
            def alone():
                pool.sem_inc(sem("pool_passed"), 1)

            def power(count):
                pool.wait_ge(sem("variance"), count)
                pool.tensor_tensor(RS[:, :], VE[:, :], neg_half[:, :], ALU.pow).then_inc(sem("rstd"), 1)

            def x_bias(g, normed, which):
                pool.wait_ge(sem("normed"), normed)
                alone()
                xx = xgroup(g)
                pool.tensor_tensor(xx, xx, rep(row_bias[:, which, :], T), ALU.add).then_inc(sem("x_biased"), 1)

            def scatter(turn):
                pool.wait_ge(sem("slots_found"), turn + 1)
                alone()
                for t in range(T):
                    for k in range(2):
                        pool.indirect_dma_start(out=xs_dram, out_offset=bass.IndirectOffsetOnAxis(ap=IDXG[:, 2 * t + k:2 * t + k + 1], axis=0),
                                                in_=XN[:, t, :], in_offset=None).then_inc(sem("rows_sent"), 16)

            def gather(g, turn):
                pool.tensor_copy(IDXP[:, :], IDX[:, ds(g * 2 * T, 2 * T)]).then_inc(sem("gather_index"), 1)
                pool.wait_ge(sem("gather_index"), turn + 1)
                alone()
                for t in range(T):
                    for k in range(2):
                        pool.indirect_dma_start(out=YA[:, 2 * t + k, :], out_offset=None, in_=ys_dram,
                                                in_offset=bass.IndirectOffsetOnAxis(ap=IDXP[:, 2 * t + k:2 * t + k + 1], axis=0)).then_inc(sem("rows_gathered"), 16)

            def phase1(g):
                power(2 * g + 1)

                def spread(i):
                    t, m = i // 2, i % 2
                    b, n = job(j1, ("kT", m), g)
                    if t == 0:
                        pool.wait_ge(bank_empty[b], n + 1)
                    if i >= 4:
                        b, n = job(j1, ("s", i - 4, 1), g)
                        pool.wait_ge(bank_full[b], n + 1)
                    pool.tensor_tensor(Kb[:, i % 4, :, :], rep(kT[:, m, t * P:(t + 1) * P], 8), bc(head_of[:, :], P), ALU.mult).then_inc(sem("k_heads"), 1)

                def bias(i):
                    for j in range(2):
                        b, n = job(j1, ("s", i, j), g)
                        pool.wait_ge(bank_empty[b], n + 1)
                    pool.tensor_tensor(SC[:, i % 4, :, :], SC[:, i % 4, :, :], SCORE_BIAS[:, 8:16, :], ALU.add).then_inc(sem("biased"), 1)

                for i in range(4):
                    spread(i)
                x_bias(g, 2 * g + 1, BO0)
                for i in range(UNITS):
                    if i % 2:
                        bias(i)
                    if i + 4 < UNITS:
                        spread(i + 4)
                power(2 * g + 2)

            def layer1(g):
                power(2 * g + (2 * GROUPS + 1))
                pool.wait_ge(sem("normed"), 2 * g + (2 * GROUPS + 1))
                pool.wait_ge(sem("ctx_loaded"), 16 * (g + (GROUPS + 1)))
                for n in range(4):
                    if n == 2:
                        pool.wait_ge(sem("probs16"), g + 1)
                    if n >= 1:
                        pool.wait_ge(sem("products_used"), 4 * g + n)
                    for last in (score_products if n < 2 else value_products)(pool.tensor_tensor, PR, 2 * (n % 2)):
                        pass
                    last.then_inc(sem("products"), 1)
                power(2 * g + (2 * GROUPS + 2))
                scatter(g)

            def phase3(g):
                pool.wait_ge(sem("combined"), PRIMED + T * g)
                gather(g, g)
                n0 = 4 * GROUPS + 7 * g
                m0 = 4 * GROUPS + 5 * g
                power(n0 + 1)
                x_bias(g, m0 + 1, BO2)
                power(n0 + 2)
                x_bias(g, m0 + 2, BF2)
                power(n0 + 3)
                power(n0 + 4)
                pool.wait_ge(sem("n1_raw"), g + 1)
                pool.tensor_tensor(N1, N1, rep(row_bias[:, GAM, :], T), ALU.mult).then_inc(sem("n1_scaled"), 1)
                pool.wait_ge(sem("n1_scaled"), g + 1)
                pool.tensor_tensor(N1, N1, rep(row_bias[:, BET, :], T), ALU.add).then_inc(sem("n1_ready"), 1)
                power(n0 + 5)
                pool.wait_ge(sem("normed"), m0 + 4)
                pool.tensor_tensor(N2B, N2, rep(row_bias[:, BB2, :], T), ALU.add).then_inc(sem("n2_biased"), 1)
                power(n0 + 6)
                power(n0 + 7)
                scatter(g + GROUPS)

            c = sem("pool_const")
            cn = [0]

            def k(ins):
                ins.then_inc(c, 1)
                cn[0] += 1

            def kwait():
                pool.wait_ge(c, cn[0])

            for b in range(8):
                pool.sem_inc(bank_full[b], 1)
                pool.sem_inc(bank_empty[b], 1)
            for n in PRIMED_SEMS:
                pool.sem_inc(sem(n), PRIMED)
            pool.memset(ZERO[:, :], 0.0).then_inc(sem("zero_set"), 1)
            k(pool.memset(ident[:, :], 0.0))
            k(pool.memset(tri[:, :], 1.0))
            k(pool.memset(ones[:, :], 1.0))
            k(pool.memset(neg_half[:, :], -0.5))
            k(pool.memset(lower8[:, :, :], 1.0))
            k(pool.memset(lower4[:, :, :], 1.0))
            k(pool.memset(head_of[:, :], 1.0))
            k(pool.memset(causal[:, :], 0.0))
            k(pool.memset(causal16[:, :, :], 0.0))
            k(pool.memset(V0[:, :, :, :], 1.0))
            k(pool.memset(base[:, :], 0.0))
            for e in range(E):
                k(pool.memset(region0[:, e:e + 1], float(e * CAP)))
                k(pool.memset(t8[0:1, 5, e:e + 1], float(e * REGION)))
            k(pool.iota(jrow_i[0:1, :], [[1, MOE_TILES], [0, E]], base=0, channel_multiplier=0))
            k(pool.iota(flat_i, [[2 * P, TILES], [1, 2]], base=0, channel_multiplier=2))
            k(pool.iota(dist_i, [[-1, P]], base=0, channel_multiplier=1))
            kwait()
            sel = lambda o, pat, b, cm, fill, op=ALU.is_ge: k(pool.affine_select(out=o, in_=o, pattern=pat, compare_op=op, fill=fill, base=b, channel_multiplier=cm))
            sel(ident[:, :], [[-1, P]], 0, 1, 1.0, ALU.not_equal)
            sel(tri[:, :], [[1, P]], -1, -1, 0.0)
            sel(lower8[:, :, :], [[1, E], [-1, E]], -1, 0, 0.0)
            sel(lower4[:, :, :], [[1, 4], [-1, 4]], -1, 0, 0.0)
            sel(head_of[:, :], [[-HD, 8]], 0, 1, 0.0)
            sel(causal[:, :], [[-1, P]], 0, 1, -1e30)
            sel(causal16[:, :, :], [[1, H], [-1, H]], 0, 0, -1e30)
            k(pool.tensor_copy(jrow[0:1, :], jrow_i[0:1, :]))
            k(pool.tensor_copy(DIST, dist_i))
            k(pool.tensor_copy(FLAT[:, :], flat_i))
            kwait()
            pool.affine_select(out=head_of[:, :], in_=head_of[:, :], pattern=[[HD, 8]], compare_op=ALU.is_ge, fill=0.0,
                               base=HD - 1, channel_multiplier=-1).then_inc(sem("masks_built"), 1)
            pool.wait_ge(sem("masks_built"), 1)
            pool.wait_ge(sem("score_bias_ready"), 1)
            with pool.Fori(0, GROUPS) as g:
                phase1(g)
            pool.wait_ge(sem("lists_zeroed"), 16 * zrows.shape[0])
            with pool.Fori(0, GROUPS) as g:
                layer1(g)
            pool.wait_ge(sem("absmax"), 1)
            pool.partition_all_reduce(MX[:, 2:3], MX[:, 1:2], P, RMAX).then_inc(sem("absmax_all"), 1)
            for u in range(2):
                pool.wait_ge(sem(f"y_stored{u}"), 16 * (LOOPS + 1 - u))
            with pool.Fori(0, GROUPS) as g:
                phase3(g)
            for u in range(2):
                pool.wait_ge(sem(f"y_stored{u}"), 32 * (LOOPS + 1 - u))
            with pool.Fori(0, GROUPS) as g:
                b = g + GROUPS
                pool.wait_ge(sem("x_final"), PRIMED + g)
                gather(g, g + GROUPS)


_OUT_SHAPE = (TILES, P, D)


def kernel(**inputs):
    import numpy as np
    import concourse.bacc as bacc
    from concourse.bass_utils import run_bass_kernel_spmd

    A = {k: np.asarray(v) for k, v in inputs.items()}
    kc = lambda w: np.ascontiguousarray(w.reshape(w.shape[0] // P, P, w.shape[1]).transpose(1, 0, 2))
    L0, L1, L2, L3 = "L0_xattn_", "L1_ffn_", "L2_xattn_", "L3_xattn_"
    arrays = {
        "x": A["x"], "ctx": A["ctx_1024"], "mask_qk": A["mask_1x1xSxS2_ik0"].reshape(P, P),
        "mask_bk": A["mask_BxS2_bk0"].reshape(-1),
        "ebias": A["L0_ffn_expert_bias"],
        "wr0": kc(A["L0_ffn_w_gate"].T), "wr1": kc(A["L1_ffn_router_kernel_DE"]), "wr3": kc(A["L3_ffn_gate_w"].T),
        "lora_a": A["L2_ffn_a"].T, "lora_b": A["L2_ffn_b"], "kernel": kc(A["L2_ffn_kernel"]),
        "row_bias": np.concatenate([A[L0 + "wv_b"], A[L0 + "out_b"], A[L2 + "bv"], A[L2 + "bo"], A["L2_ffn_bias"],
                                    A[L3 + "gamma"], A[L3 + "beta"], A[L3 + "b2"]]),
        "col_bias": np.stack([A[n].reshape(KC, P) for n in (L0 + "wq_b", L0 + "wk_b", L2 + "bq", L2 + "bk", L3 + "b1")]).transpose(2, 0, 1),
        "w0q": kc(A[L0 + "wq_w"].T), "w0k": kc(A[L0 + "wk_w"].T), "w0v": kc(A[L0 + "wv_w"].T), "w0o": kc(A[L0 + "out_w"].T),
        "w3q2": kc(A[L2 + "Wq"]), "w3k2": kc(A[L2 + "Wk"]), "w3v2": kc(A[L2 + "Wv"]), "w3o2": kc(A[L2 + "Wo"]),
        "w3k3": kc(A[L3 + "Wk1"]), "w3q3": kc(A[L3 + "Wq1"]), "w3v3": kc(A[L3 + "Wv1"]),
        "w3k4": kc(A[L3 + "Wk2"]), "w3q4": kc(A[L3 + "Wq2"]), "w3v4": kc(A[L3 + "Wv2"]),
        "w3h": kc(A[L3 + "W1"]), "w3ff": kc(A[L3 + "W2"]),
    }
    F = "L0_ffn_"
    gate = np.concatenate([A[F + "w1"], A[F + "sw1"].T.reshape(D, 2, HID0).transpose(1, 0, 2)])
    up = np.concatenate([A[F + "w3"], A[F + "sw3"].T.reshape(D, 2, HID0).transpose(1, 0, 2)])
    down = np.concatenate([A[F + "w2"], A[F + "sw2"].T.reshape(2, HID0, D)])
    w13 = np.stack([gate, up], axis=1).transpose(2, 0, 1, 3).reshape(D, E0 * 2 * HID0)
    arrays["w13"] = kc(w13)
    arrays["w2"] = down.transpose(1, 0, 2)

    def experts(gate, up, down):
        hid = gate.shape[2]
        gu = np.concatenate([gate, up], axis=2).reshape(E, KC, P, 2 * hid).transpose(0, 2, 1, 3).reshape(E, P, -1)
        dn = down.reshape(E, hid // P, P, D).transpose(0, 2, 1, 3).reshape(E, P, -1)
        return np.concatenate([gu, dn], axis=2)

    tr = lambda a: a.transpose(0, 2, 1)
    arrays["moe1"] = experts(A[L1 + "kernel_gating_EDF"], A[L1 + "kernel_up_EDF"], A[L1 + "kernel_down_EFD"])
    arrays["moe3"] = experts(tr(A["L3_ffn_w1"]), tr(A["L3_ffn_w3"]), tr(A["L3_ffn_w2"]))
    arrays = {n: np.ascontiguousarray(a) for n, a in arrays.items()}
    nc = bacc.Bacc("TRN2", target_bir_lowering=False, num_devices=1)
    ins = {n: nc.dram_tensor(f"in_{n}", a.shape, mybir.dt.from_np(a.dtype), kind="ExternalInput").ap() for n, a in arrays.items()}
    out = nc.dram_tensor("out_x", _OUT_SHAPE, F32, kind="ExternalOutput").ap()
    build(nc, ins, out)
    r = run_bass_kernel_spmd(nc, [{f"in_{n}": a for n, a in arrays.items()}], core_ids=[0])
    return r.results[0]["out_x"]
```

```python
from contextlib import ExitStack

import concourse.bass as bass
from concourse import mybir

P = 128
TILES = 16
T = 4
GROUPS = TILES // T
STREAMS = 2
TS = T // STREAMS
D = 256
KC = D // P
H = 16
HD = D // H
E = 8
NTOK = TILES * P
CAP = NTOK
SLOT = 256
REGION = CAP // SLOT
MOE_TILES = 2 * NTOK // SLOT + E - 1
SPARE = E * REGION
HID0 = 128
E0 = 10
PAIR = E0 // 2 - 1
VW = HD + 1
HIDS = {1: 512, 3: 1024}
PAIRBLK = [4 * (b + 1) for b in range(4)]
PRW = sum(4 * n * HD for n in PAIRBLK)

F32 = mybir.dt.float32
BF16 = mybir.dt.bfloat16
I32 = mybir.dt.int32
U32 = mybir.dt.uint32
U8 = mybir.dt.uint8
ALU = mybir.AluOpType
ACT = mybir.ActivationFunctionType
AX = mybir.AxisListType.X
RMAX = bass.bass_isa.ReduceOp.max
ds = bass.ds

PRIMED = 2
PRIMED_SEMS = ["norm_rows_free", "result_free0", "result_free1", "x_final"]

RING = [0, 1, 2, 3, 4, 5]
ACC = [6, 7]


class BankPlan:

    def __init__(self):
        self.done = [0] * 8
        self.ring = 0
        self.acc = 0

    def phase(self, keys, turns):
        per, table = [0] * 8, {}
        for key in keys:
            if key[0] == "acc":
                b = ACC[self.acc % len(ACC)]
                self.acc += 1
            else:
                b = RING[self.ring % len(RING)]
                self.ring += 1
            table[key] = (b, self.done[b], per[b])
            per[b] += 1
        plan = {key: (b, base, per[b], k) for key, (b, base, k) in table.items()}
        for b in range(8):
            self.done[b] += turns * per[b]
        return plan


def job(plan, key, turn):
    b, base, per, k = plan[key]
    return b, turn * per + (base + k + 1)


class Waits:

    def __init__(self, engine):
        self.engine = engine
        self.plan = None

    def at_least(self, sem, plan, key, turn, more):
        b, n = job(plan, key, turn)
        _, base, _, k = plan[key]
        if self.plan is not plan:
            self.plan, self.had = plan, {}
        if self.had.get(b, -1) < base + k + more:
            self.had[b] = base + k + more
            self.engine.wait_ge(sem[b], n + more)
        return b


STEPS = {"phase1": 64, "routed": 1, "layer1": 96, "phase3": 132, "last": 16}


def build(nc, ins, out):
    x_in, ctx_in, mask_qk, mask_bk = ins["x"], ins["ctx"], ins["mask_qk"], ins["mask_bk"]

    bp = BankPlan()
    pre = bp.phase([("wab", 0), ("wab", 1)], 1)
    k1 = [("cT", 0), ("cT", 1), ("kT", 0), ("kT", 1)] + [("v", t) for t in range(T)]
    k1 += [("xT0", 0), ("xT0", 1), ("qT", 0), ("qT", 1)]
    UNITS = 2 * T
    att_order = []
    for n in range(UNITS + 3):
        att_order += [(a, n - lag) for a, lag in (("s", 0), ("p", 2), ("o", 3)) if 0 <= n - lag < UNITS]
    for a, i in att_order:
        if a != "o":
            k1 += [(a, i, 0), (a, i, 1)]
        elif i % 2 == 0:
            k1.append(("acc", "o", i // 2))
    k1 += [("aT", 0), ("aT", 1)] + [("xo", t) for t in range(T)] + [("xT1", 0), ("xT1", 1), ("lg",)]
    ffn_steps = []
    for i in range(T + 3):
        if i < T:
            ffn_steps.append(("up", i))
        if 2 <= i < T + 2:
            ffn_steps.append(("hT", i - 2))
        if i >= 3:
            ffn_steps.append(("down", i - 3))
    for s, i in ffn_steps:
        k1.append(("acc", "y", i) if s == "down" else (s, i))
    j1 = bp.phase(k1, GROUPS)
    jr0 = bp.phase([("cnt",), ("gt",)], 1)
    jr = bp.phase([("ow",)] + [("gu", t) for t in range(T)] + [("hs",)], GROUPS)
    jr1 = bp.phase([("dn",)], 1)
    j2 = bp.phase([("xT3", 0), ("xT3", 1), ("lg1",), ("rk",)], GROUPS)

    def moe_steps(hc, second):
        seq = [(u, c) for u in range(2 if second else 1) for c in range(hc)]
        steps = [("xsT", 0)]
        for i in range(len(seq) + 2):
            if i < len(seq):
                steps.append(("up",) + seq[i])
                if seq[i][0] == 0 and seq[i][1] == hc - 3 and second:
                    steps.append(("xsT", 1))
            if i >= 2:
                steps.append(("down",) + seq[i - 2])
        return steps

    def moe_keys(steps):
        keys = []
        for s in steps:
            if s[0] == "down":
                if s[2] == 0:
                    keys += [("acc", "y", s[1], 0), ("acc", "y", s[1], 1)]
            else:
                keys.append(s)
        return keys

    moe = {}
    LOOPS = MOE_TILES // 2
    moe[1] = [(moe_steps(4, True), bp.phase(moe_keys(moe_steps(4, True)), LOOPS)),
              (moe_steps(4, False), bp.phase(moe_keys(moe_steps(4, False)), 1))]
    k3 = []
    for names in (("cT", "k2", "v2"), ("xT4", "q2"), ("s2",), ("k4", "v4"), ("p2", "o2"), ("oT2", "x2"), ("xT5", "f2"),
                  ("xT6", "q3", "k3"), ("s3",), ("v3",), ("p3", "o3"), ("aT", "q4"), ("s4",), ("p4", "o4"), ("nT", "h"), ("ff",),
                  ("xT7",)):
        for u in range(STREAMS):
            k3 += [(n, u) for n in names]
    k3 += [("lg1",), ("rk",)]
    j3 = bp.phase(k3, GROUPS)
    moe[3] = [(moe_steps(8, True), bp.phase(moe_keys(moe_steps(8, True)), LOOPS)),
              (moe_steps(8, False), bp.phase(moe_keys(moe_steps(8, False)), 1))]

    tiles_before = {1: (0, 0), 3: (LOOPS + 1, LOOPS)}

    ctx = ExitStack()
    with ctx:
        def sb(name, shape, dt=F32):
            return ctx.enter_context(nc.sbuf_tensor(name, shape, dt))

        sems = {}

        def sem(name):
            if name not in sems:
                sems[name] = ctx.enter_context(nc.semaphore(name))
            return sems[name]

        bank = [ctx.enter_context(nc.psum_tensor(f"bank{b}", [P, 512], F32)) for b in range(8)]
        bank_full = [sem(f"bank_full{b}") for b in range(8)]
        bank_empty = [sem(f"bank_empty{b}") for b in range(8)]

        xs_dram = nc.dram_tensor("expert_rows_in", ((SPARE + 1) * SLOT, D), F32, kind="Internal").ap()
        ys_dram = nc.dram_tensor("expert_rows_out", ((SPARE + 1) * SLOT, D), F32, kind="Internal").ap()

        X = sb("x_stream", [P, TILES * D])
        ident = sb("ident", [P, P])
        tri = sb("tri", [P, P], BF16)
        ones = sb("ones", [P, P], BF16)
        neg_half = sb("neg_half", [P, T])
        lower8 = sb("lower8", [P, E, E])
        lower4 = sb("lower4", [P, 4, 4])
        head_of = sb("head_of_row", [P, 8])
        region0 = sb("region_start", [P, E])
        causal = sb("causal", [P, P])
        causal16 = sb("causal16", [P, H, H])
        row_bias = sb("row_bias", [P, 8, D])
        BV0, BO0, BV2, BO2, BF2, GAM, BET, BB2 = range(8)
        col_bias = sb("col_bias", [P, 5, KC])
        CQ0, CK0, CQ2, CK2, CB1 = range(5)
        ebias = sb("expert_bias", [P, E])
        keymask = sb("keymask", [P, TILES * P])
        keymask8 = sb("keymask8", [P, TILES * P // 4], I32)
        mask01 = sb("mask01", [P, P])
        maski = sb("maski", [P, P], I32)
        Wr0 = sb("w_router0", [P, KC, E])
        Wr = {1: sb("w_router1", [P, KC, E]), 3: sb("w_router3", [P, KC, E])}
        IDX = sb("slot_index", [P, (TILES + T) * 2], U32)
        IDXG = sb("slot_index_group", [P, T * 2], U32)
        IDXP = sb("slot_index_gather", [P, 2, T * 2], U32)
        CW = sb("combine_weight", [P, TILES * 2])
        CWP = sb("combine_weight_group", [P, T * 2])
        WREG = sb("weights", [P, 9984])
        BIG = sb("work", [P, 12288])
        Kb = BIG[:, 0:4096].rearrange("p (b h k) -> p b h k", b=4, h=8)
        SC = BIG[:, 4096:8192].rearrange("p (b h k) -> p b h k", b=4, h=8)
        PT = BIG[:, 8192:12288].rearrange("p (b h q) -> p b h q", b=4, h=8)
        PR = BIG[:, 7168:7168 + PRW]
        PRD = BIG[:, 7168 + PRW:7168 + 2 * PRW]
        ZERO = sb("zero", [P, D])
        NBG = sb("key_penalty", [P, T * P])
        CG = sb("ctx_rows", [P, T, D])
        cT = sb("ctx_cols", [P, KC, T * P])
        kT = sb("k_cols", [P, KC, T * P])
        qT = sb("q_cols", [P, KC, T * P])
        XN = sb("norm_rows", [P, T, D])
        xT = sb("norm_cols", [P, KC, T * P])
        AO = sb("att_rows", [P, T, D])
        aT = sb("att_cols", [P, KC, T * P])
        V0 = sb("v_rows", [P, T, H, VW])
        SCORE_BIAS = sb("score_bias", [P, H, P])
        EXTRA = sb("extra", [P, 3072])
        ST = sb("stats", [P, T, 6])
        MV = sb("mean_var", [P, T, 2])
        VE = sb("var_eps", [P, T])
        RS = sb("rstd", [P, T])
        MX = sb("row_max", [P, 64])
        RC = sb("row_rec", [P, 64])
        small = sb("small", [P, 16, T * E])
        cmpa = sb("cmpa", [P, T * E * E])
        cmpb = sb("cmpb", [P, T * E * E])
        SRC = sb("source_row", [P, TILES * 2 * E])
        WV = sb("choice_weight", [P, TILES * 2])
        FLAT = sb("flat_place", [P, TILES * 2])
        X8 = sb("first_rows_cols", [P, GROUPS * KC * E])
        RANK = sb("rank", [P, T, E])
        OH = sb("onehot", [P, T, 2, E])
        OHT = sb("onehot_t", [P, T, 2, E])
        SEL = sb("selected", [P, T, E], BF16)
        base = sb("list_len", [P, E])
        wide = sb("tile_math", [1, 6, MOE_TILES * E])
        lens_i = sb("lens_i", [1, E], I32)
        t8 = sb("tile8", [1, 6, E])
        jrow_i = sb("jrow_i", [1, MOE_TILES * E], I32)
        LAB = sb("lora_product", [P, KC, D])
        jrow = sb("jrow", [1, MOE_TILES * E])
        tile_e = sb("tile_expert", [1, MOE_TILES], I32)
        tile_r = sb("tile_region", [1, MOE_TILES], I32)

        def wview(off, k):
            return WREG[:, off:off + KC * k].rearrange("p (c n) -> p c n", c=KC)

        W0 = {n: wview(i * 512, D) for i, n in enumerate(("q", "k", "v", "o"))}
        W13 = wview(2048, E0 * 2 * HID0)
        W2 = WREG[:, 2048 + KC * E0 * 256:2048 + KC * E0 * 256 + E0 * D].rearrange("p (e n) -> p e n", e=E0)
        L3N = ("q2", "k2", "v2", "o2", "k3", "q3", "v3", "k4", "q4", "v4", "h", "ff")
        W3 = {n: wview(i * 512, D) for i, n in enumerate(L3N)}
        WEFF = wview(12 * 512, D)
        KER = wview(13 * 512, D)
        QTMP = wview(14 * 512, D)
        LORA_A = sb("lora_a", [16, D])
        LORA_B = sb("lora_b", [16, D])
        WB = [BIG[:, 6144 * u:6144 * (u + 1)] for u in range(2)]

        SG0 = EXTRA[:, 0:1536].rearrange("p (b n) -> p b n", b=len(RING))
        HB0 = EXTRA[:, 1536:2304].rearrange("p (b n) -> p b n", b=3)
        HT0 = EXTRA[:, 2304:3072].rearrange("p (b n) -> p b n", b=3)
        S16 = EXTRA[:, 0:1024].rearrange("p (t h k) -> p t h k", t=T, h=H)
        S16b = EXTRA[:, 1024:2048].rearrange("p (t h k) -> p t h k", t=T, h=H)
        O16 = EXTRA[:, 2048:3072].rearrange("p (t n) -> p t n", t=T)
        DIAG = 2 * E * E + E
        XE = BIG[:, 0:KC * E * DIAG].rearrange("p (c n) -> p c n", c=KC)
        OHS = BIG[:, 2176:2688].rearrange("p (a n) -> p a n", a=2 * T)
        OWS = BIG[:, 2688:3200].rearrange("p (t n) -> p t n", t=T)
        OWT = BIG[:, 3200:3712].rearrange("p (t n) -> p t n", t=T)
        GT = BIG[:, 3712:4224]
        SGR = BIG[:, 4224:5248].rearrange("p (t k n) -> p t k n", t=T, k=2)
        HR = BIG[:, 5248:6272].rearrange("p (a n) -> p a n", a=2 * T)
        HS = BIG[:, 6272:6336]
        EO = BIG[:, 6336:6592]
        XS = aT[:, :, :].rearrange("p c (h n) -> p c h n", h=2)
        xsT = xT[:, :, :].rearrange("p c (u n) -> p u c n", u=2)
        SG = SCORE_BIAS[:, 0:12, :].rearrange("p (b a) k -> p b (a k)", b=len(RING))
        HT = EXTRA[:, 0:2048].rearrange("p (c n) -> p c n", c=8)
        YS = AO[:, :, :].rearrange("p (u h) n -> p u h n", u=2)
        SC2 = BIG[:, 0:512].rearrange("p (t k) -> p t k", t=T)
        PT2 = BIG[:, 512:1024].rearrange("p (t k) -> p t k", t=T)
        V2 = BIG[:, 1024:2048].rearrange("p (t n) -> p t n", t=T)
        V4 = BIG[:, 2048:3072].rearrange("p (t n) -> p t n", t=T)
        V3 = BIG[:, 3072:4096].rearrange("p (t n) -> p t n", t=T)
        k4T = BIG[:, 4096:5120].rearrange("p (c n) -> p c n", c=KC)
        IN3 = BIG[:, 5120:6144].rearrange("p (t n) -> p t n", t=T)
        N1 = BIG[:, 6144:7168].rearrange("p (t n) -> p t n", t=T)
        N2 = BIG[:, 7168:8192].rearrange("p (t n) -> p t n", t=T)
        R3 = BIG[:, 8192:9216].rearrange("p (t n) -> p t n", t=T)
        hT3 = BIG[:, 9216:10240].rearrange("p (c n) -> p c n", c=KC)
        hTt = BIG[:, 10240:11264].rearrange("p (c n) -> p c n", c=KC)
        N2B = BIG[:, 11264:12288].rearrange("p (t n) -> p t n", t=T)
        YA = [buf[:, 0:2 * T * D].rearrange("p (a n) -> p a n", n=D) for buf in (EXTRA, BIG)]

        def tiles(buf, u):
            return buf[:, u * TS:(u + 1) * TS, :]

        def cols_of(buf, u):
            return buf[:, :, u * TS * P:(u + 1) * TS * P]

        def per_chunk(ps):
            return ps[:, :].rearrange("p (c n) -> p c n", c=KC)

        def per_tile(ps, n=D):
            return ps[:, 0:TS * n].rearrange("p (t n) -> p t n", t=TS)

        xstream = lambda g, u: X[:, ds((T * g + TS * u) * D, TS * D)]
        dist_i = AO[:, 2, 0:P].bitcast(I32)
        flat_i = AO[:, 3, 0:2 * TILES].bitcast(I32)
        DIST = AO[:, 0, 0:P]
        NEG = AO[:, 1, 0:P]

        xg = lambda g, t: X[:, ds((T * g + t) * D, D)]
        xgroup = lambda g: X[:, ds(g * T * D, T * D)].rearrange("p (t n) -> p t n", t=T)

        def bc(ap, n):
            return ap.unsqueeze(len(ap.shape)).to_broadcast(list(ap.shape) + [n])

        def rep(ap, n, at=1):
            s = list(ap.shape)
            return ap.unsqueeze(at).to_broadcast(s[:at] + [n] + s[at:])

        consts = [(maski[:, :], mask_qk), (keymask8[:, :].bitcast(U8), mask_bk.partition_broadcast(P)),
                  (ebias[:, :], ins["ebias"].partition_broadcast(P)),
                  (Wr0[:, :, :], ins["wr0"]), (Wr[1][:, :, :], ins["wr1"]), (Wr[3][:, :, :], ins["wr3"]),
                  (LORA_A[:, :], ins["lora_a"]), (LORA_B[:, :], ins["lora_b"]),
                  (row_bias[:, :, :].rearrange("p a n -> p (a n)"), ins["row_bias"].partition_broadcast(P)),
                  (col_bias[:, :, :], ins["col_bias"])]
        w1loads = [(W0["q"], ins["w0q"]), (W0["k"], ins["w0k"]), (W0["v"], ins["w0v"]), (W0["o"], ins["w0o"]),
                   (W13, ins["w13"]), (W2, ins["w2"])]
        w3loads = [(W3[n], ins["w3" + n]) for n in L3N] + [(KER, ins["kernel"])]
        ZCHUNK = 10
        zrows = xs_dram.rearrange("(a p r) d -> a p (r d)", p=P, r=ZCHUNK)

        yrows = ys_dram.rearrange("(a p r) d -> a p (r d)", p=P, r=ZCHUNK)

        def score_products(tt, dst, t):
            q = AO[:, t, :].rearrange("p (h d) -> p h d", h=H)
            kv = CG[:, t, :].rearrange("p (k d) -> p k d", k=H)
            off = 0
            for k, nk in enumerate(PAIRBLK):
                part = dst[:, off:off + 4 * nk * HD].rearrange("p (h k d) -> p h k d", h=4, d=HD)
                off += 4 * nk * HD
                yield tt(part, rep(q[:, 4 * k:4 * k + 4, :], nk, 2), rep(kv[:, 0:nk, :], 4), ALU.mult)

        def value_products(tt, dst, t):
            vt = CG[:, t, :].rearrange("p (k d) -> p d k", k=H)
            off = 0
            for k, nk in enumerate(PAIRBLK):
                part = dst[:, off:off + 4 * nk * HD].rearrange("p (h d k) -> p h d k", h=4, d=HD)
                off += 4 * nk * HD
                yield tt(part, rep(S16b[:, t, 4 * k:4 * k + 4, 0:nk], HD, 2), rep(vt[:, :, 0:nk], 4), ALU.mult)

        block = ctx.enter_context(nc.Block())

        @block.sync
        def _(sp):
            def load_x(g, name):
                sp.dma_start(xgroup(g), x_in[ds(g * T, T), :, :].rearrange("t p n -> p t n")).then_inc(sem(name), 16)

            load_x(0, "x0_loaded")
            for dst, src in consts:
                sp.dma_start(dst, src).then_inc(sem("const_loaded"), 16)
            sp.dma_start(CG[:, :, :], ctx_in[0:T, :, :].rearrange("t p n -> p t n")).then_inc(sem("ctx_loaded"), 16)
            for dst, src in w1loads[:len(W0)]:
                sp.dma_start(dst, src).then_inc(sem("w0_loaded"), 16)
            for dst, src in w1loads[len(W0):]:
                sp.dma_start(dst, src).then_inc(sem("w1_loaded"), 16)
            for g in range(1, GROUPS):
                load_x(g, "x_loaded")
            sp.wait_ge(sem("zero_set"), 1)
            for i in range(zrows.shape[0]):
                sp.dma_start(zrows[i, :, :].rearrange("p (r d) -> p r d", d=D), rep(ZERO[:, :], ZCHUNK)).then_inc(sem("lists_zeroed"), 16)

            def ctx_loads():
                with sp.Fori(1, GROUPS) as g:
                    b, n = job(j1, ("cT", 1), g)
                    sp.wait_ge(bank_full[b], n)
                    sp.dma_start(CG[:, :, :], ctx_in[ds(g * T, T), :, :].rearrange("t p n -> p t n")).then_inc(sem("ctx_loaded"), 16)
                b, n = job(j1, ("cT", 1), GROUPS)
                sp.wait_ge(bank_full[b], n)
                sp.dma_start(CG[:, :, :], ctx_in[0:T, :, :].rearrange("t p n -> p t n")).then_inc(sem("ctx_loaded"), 16)
                for i in range(yrows.shape[0]):
                    sp.dma_start(yrows[i, :, :].rearrange("p (r d) -> p r d", d=D), rep(ZERO[:, :], ZCHUNK)).then_inc(sem("results_zeroed"), 16)
                with sp.Fori(1, GROUPS) as g:
                    sp.wait_ge(sem("normed"), 2 * g + 2 * GROUPS)
                    sp.dma_start(CG[:, :, :], ctx_in[ds(g * T, T), :, :].rearrange("t p n -> p t n")).then_inc(sem("ctx_loaded"), 16)
                    sp.wait_ge(sem("rows_sent"), 16 * 2 * T * g)
                    sp.sem_inc(sem("norm_rows_free"), 1)

            def experts(layer):
                wsrc = ins[f"moe{layer}"]
                width = wsrc.shape[2]

                def load(u, j):
                    e = sp.value_load(tile_e[0:1, ds(j, 1)], min_val=0, max_val=E - 1)
                    r = sp.value_load(tile_r[0:1, ds(j, 1)], min_val=0, max_val=SPARE)
                    sp.dma_start(XS[:, u, :, :], xs_dram[ds(r * SLOT, SLOT), :].rearrange("(h p) d -> p h d", p=P)).then_inc(sem(f"rows_loaded{u}"), 16)
                    sp.dma_start(WB[u][:, 0:width], wsrc[ds(e, 1), :, :].rearrange("a p n -> p (a n)")).then_inc(sem(f"w_loaded{u}"), 16)

                def buffers_free(plan, turn, u):
                    b, n = job(plan, ("acc", "y", u, 1), turn)
                    sp.wait_ge(bank_full[b], n + 1)

                def store(plan, turn, pair, u, j):
                    for h in range(2):
                        b, n = job(plan, ("acc", "y", u, h), turn)
                        sp.wait_ge(bank_empty[b], n + 1)
                    r = sp.value_load(tile_r[0:1, ds(j, 1)], min_val=0, max_val=SPARE)
                    sp.dma_start(ys_dram[ds(r * SLOT, SLOT), :].rearrange("(h p) d -> p h d", p=P), YS[:, u, :, :]).then_inc(sem(f"y_stored{u}"), 16)
                    sp.wait_ge(sem(f"y_stored{u}"), (pair + tiles_before[layer][u] + 1) * 16)
                    sp.sem_inc(sem(f"result_free{u}"), 1)

                loop, tail = moe[layer][0][1], moe[layer][1][1]
                load(0, 0)
                load(1, 1)
                if layer == 1:
                    for dst, src in w3loads:
                        sp.dma_start(dst, src).then_inc(sem("w3_loaded"), 16)
                    sp.dma_start(CG[:, :, :], ctx_in[0:T, :, :].rearrange("t p n -> p t n")).then_inc(sem("ctx_loaded"), 16)
                with sp.Fori(0, LOOPS - 1) as i:
                    for u in range(2):
                        buffers_free(loop, i, u)
                        load(u, 2 * i + (2 + u))
                        store(loop, i, i, u, 2 * i + u)
                i = LOOPS - 1
                buffers_free(loop, i, 0)
                load(0, 2 * LOOPS)
                for u in range(2):
                    store(loop, i, i, u, 2 * i + u)
                store(tail, 0, LOOPS, 0, 2 * LOOPS)

            ctx_loads()
            sp.wait_ge(sem("rows_sent"), 16 * 2 * TILES)
            sp.sem_inc(sem("norm_rows_free"), 1)
            sp.wait_ge(sem("tiles_planned"), 1)
            sp.wait_ge(sem("results_zeroed"), 16 * yrows.shape[0])
            experts(1)
            with sp.Fori(1, GROUPS) as g:
                b, n = job(j3, ("cT", 1), g)
                sp.wait_ge(bank_full[b], n)
                sp.dma_start(CG[:, :, :], ctx_in[ds(g * T, T), :, :].rearrange("t p n -> p t n")).then_inc(sem("ctx_loaded"), 16)
                sp.wait_ge(sem("rows_sent"), 16 * 2 * T * (g + GROUPS))
                sp.sem_inc(sem("norm_rows_free"), 1)
            sp.wait_ge(sem("rows_sent"), 16 * 2 * TILES * 2)
            sp.wait_ge(sem("tiles_planned"), 2)
            experts(3)
            with sp.Fori(0, GROUPS) as g:
                sp.wait_ge(sem("x_final"), PRIMED + g + 1)
                sp.dma_start(out[ds(g * T, T), :, :].rearrange("t p n -> p t n"), xgroup(g)).then_inc(sem("out_stored"), 16)
            sp.wait_ge(sem("out_stored"), 16 * GROUPS)

        @block.tensor
        def _(pe):
            empties = Waits(pe)

            def fill(plan, g, key):
                b = empties.at_least(bank_empty, plan, key, g, 0)
                return bank[b], b

            def ready(plan, g, key):
                empties.at_least(bank_empty, plan, key, g, 1)

            def mm(o, l, r, a=True, z=True):
                return pe.matmul(o, l, r, start=a, stop=z)

            def turn_rows(plan, g, name, rows):
                for c in range(KC):
                    ps, b = fill(plan, g, (name, c))
                    for t in range(T):
                        m = pe.transpose(ps[:, t * P:(t + 1) * P], rows[:, t, c * P:(c + 1) * P], ident[:, :])
                    m.then_inc(bank_full[b], 1)

            def cols(plan, g, name, w, src):
                for m in range(KC):
                    ps, b = fill(plan, g, (name, m))
                    for c in range(KC):
                        last = mm(ps[:, :], w[:, c, m * P:(m + 1) * P], src[:, c, :], c == 0, c == KC - 1)
                    last.then_inc(bank_full[b], 1)

            def rows2(plan, g, name, w, src):
                for a in range(2):
                    ps, b = fill(plan, g, (name, a))
                    for i in range(2):
                        t = 2 * a + i
                        for c in range(KC):
                            last = mm(ps[:, i * D:(i + 1) * D], src[:, c, t * P:(t + 1) * P], w[:, c, :], c == 0, c == KC - 1)
                    last.then_inc(bank_full[b], 1)

            def rows1(plan, g, name, w, src):
                for t in range(T):
                    ps, b = fill(plan, g, (name, t))
                    for c in range(KC):
                        last = mm(ps[:, 0:D], src[:, c, t * P:(t + 1) * P], w[:, c, :], c == 0, c == KC - 1)
                    last.then_inc(bank_full[b], 1)

            def logits(plan, g, name, w):
                ps, b = fill(plan, g, (name,))
                for t in range(T):
                    for c in range(KC):
                        last = mm(ps[:, t * E:(t + 1) * E], xT[:, c, t * P:(t + 1) * P], w[:, c, :], c == 0, c == KC - 1)
                last.then_inc(bank_full[b], 1)

            def list_ranks(plan, g, turn):
                ps, b = fill(plan, g, ("rk",))
                pe.wait_ge(sem("selected"), turn + 1)
                for t in range(T):
                    for s in range(t + 1):
                        mm(ps[:, t * E:(t + 1) * E], tri[:, :] if s == t else ones[:, :], SEL[:, s, :], s == 0, s == t)
                for s in range(T):
                    last = mm(ps[:, T * E:(T + 1) * E], ones[:, :], SEL[:, s, :], s == 0, s == T - 1)
                last.then_inc(bank_full[b], 1)

            def phase1(g):
                pe.wait_ge(sem("ctx_loaded"), 16 * (g + 1))
                turn_rows(j1, g, "cT", CG)
                ready(j1, g, ("cT", 0))
                ready(j1, g, ("cT", 1))
                cols(j1, g, "kT", W0["k"], cT)
                rows1(j1, g, "v", W0["v"], cT)
                pe.wait_ge(sem("normed"), 2 * g + 1)
                turn_rows(j1, g, "xT0", XN)
                ready(j1, g, ("xT0", 0))
                ready(j1, g, ("xT0", 1))
                cols(j1, g, "qT", W0["q"], xT)
                ready(j1, g, ("qT", 0))
                ready(j1, g, ("qT", 1))
                for a, i in att_order:
                    t, m, u = i // 2, i % 2, i % 4
                    if a == "s":
                        pe.wait_ge(sem("k_heads"), UNITS * g + (i + 1))
                        for j in range(2):
                            ps, b = fill(j1, g, ("s", i, j))
                            mm(ps[:, :].rearrange("p (h k) -> p h k", h=4), qT[:, m, t * P:(t + 1) * P],
                               Kb[:, u, 4 * j:4 * j + 4, :]).then_inc(bank_full[b], 1)
                    elif a == "p":
                        pe.wait_ge(sem("probs"), UNITS * g + (i + 1))
                        for j in range(2):
                            ps, b = fill(j1, g, ("p", i, j))
                            for h in range(4):
                                last = pe.transpose(ps[:, h * P:(h + 1) * P], SC[:, u, 4 * j + h, :], ident[:, :])
                            last.then_inc(bank_full[b], 1)
                    else:
                        if m == 0:
                            ready(j1, g, ("v", t))
                            ps_o, b_o = fill(j1, g, ("acc", "o", t))
                        for j in range(2):
                            ready(j1, g, ("p", i, j))
                        for h in range(8):
                            last = mm(ps_o[:, (8 * m + h) * VW:(8 * m + h + 1) * VW], PT[:, u, h, :], V0[:, t, 8 * m + h, :])
                        if m == 1:
                            last.then_inc(bank_full[b_o], 1)
                for t in range(T):
                    ready(j1, g, ("acc", "o", t))
                turn_rows(j1, g, "aT", AO)
                ready(j1, g, ("aT", 0))
                ready(j1, g, ("aT", 1))
                rows1(j1, g, "xo", W0["o"], aT)
                pe.wait_ge(sem("normed"), 2 * g + 2)
                turn_rows(j1, g, "xT1", XN)
                ready(j1, g, ("xT1", 0))
                ready(j1, g, ("xT1", 1))
                logits(j1, g, "lg", Wr0)
                pe.wait_ge(sem("w1_loaded"), 16 * (len(w1loads) - len(W0)))
                for s, i in ffn_steps:
                    t, p = i, PAIR
                    if s == "up":
                        ps, b = fill(j1, g, ("up", i))
                        for c in range(KC):
                            last = mm(ps[:, :], xT[:, c, t * P:(t + 1) * P], W13[:, c, p * 512:(p + 1) * 512], c == 0, c == KC - 1)
                        last.then_inc(bank_full[b], 1)
                    elif s == "hT":
                        ready(j1, g, ("up", i))
                        ps, b = fill(j1, g, ("hT", i))
                        for a in range(2):
                            last = pe.transpose(ps[:, a * P:(a + 1) * P], HB0[:, i % 3, a * P:(a + 1) * P], ident[:, :])
                        last.then_inc(bank_full[b], 1)
                    else:
                        ps, b = fill(j1, g, ("acc", "y", t))
                        ready(j1, g, ("hT", i))
                        for a in range(2):
                            last = mm(ps[:, 0:D], HT0[:, i % 3, a * P:(a + 1) * P], W2[:, 2 * p + a, :],
                                      a == 0, a == 1)
                        last.then_inc(bank_full[b], 1)

            def routed_start():
                pe.wait_ge(sem("choices_counted"), 1)
                ps, b = fill(jr0, 0, ("cnt",))
                mm(ps[:, 0:E], ones[:, :], SEL[:, 0, :]).then_inc(bank_full[b], 1)
                pe.wait_ge(sem("first_rows_spread"), 2)
                ps, b = fill(jr0, 0, ("gt",))
                for e in range(E):
                    for c in range(KC):
                        last = mm(ps[:, 0:256], XE[:, c, P * e:P * e + P], W13[:, c, 256 * e:256 * e + 256],
                                  e == 0 and c == 0, e == E - 1 and c == KC - 1)
                last.then_inc(bank_full[b], 1)
                ready(jr0, 0, ("gt",))

            def routed(g):
                pe.wait_ge(sem("pairs_built"), g + 1)
                ps, b = fill(jr, g, ("ow",))
                for t in range(T):
                    last = pe.transpose(ps[:, t * P:(t + 1) * P], OWS[:, t, :], ident[:, :])
                last.then_inc(bank_full[b], 1)
                ready(jr, g, ("ow",))
                for t in range(T):
                    ps, b = fill(jr, g, ("gu", t))
                    mm(ps[:, :], OWT[:, t, :], GT).then_inc(bank_full[b], 1)
                ps, b = fill(jr, g, ("hs",))
                for t in range(T):
                    ready(jr, g, ("gu", t))
                    for k in range(2):
                        last = mm(ps[:, 0:64], HR[:, 2 * t + k, :], OHS[:, 2 * t + k, :], t == 0 and k == 0, t == T - 1 and k == 1)
                last.then_inc(bank_full[b], 1)

            def routed_end():
                ready(jr, GROUPS - 1, ("hs",))
                ps, b = fill(jr1, 0, ("dn",))
                for e in range(E):
                    last = mm(ps[0:E, 0:D], HS[:, E * e:E * e + E], W2[:, e, :], e == 0, e == E - 1)
                last.then_inc(bank_full[b], 1)

            def layer1(g):
                pe.wait_ge(sem("normed"), 2 * g + (2 * GROUPS + 2))
                turn_rows(j2, g, "xT3", XN)
                ready(j2, g, ("xT3", 0))
                ready(j2, g, ("xT3", 1))
                logits(j2, g, "lg1", Wr[1])
                list_ranks(j2, g, g)

            def experts(layer, turn, pair, steps, plan):
                hc = HIDS[layer] // P
                before = [pair + n for n in tiles_before[layer]]
                ybank = {}
                up = {u: WB[u][:, 0:KC * 2 * hc * P].rearrange("p (c n) -> p c n", c=KC) for u in range(2)}
                dn = {u: WB[u][:, KC * 2 * hc * P:KC * 2 * hc * P + hc * D].rearrange("p (c n) -> p c n", c=hc) for u in range(2)}
                for s in steps:
                    u = s[1]
                    if s[0] == "xsT":
                        pe.wait_ge(sem(f"rows_loaded{u}"), 16 * (before[u] + 1))
                        ps, b = fill(plan, turn, s)
                        for c in range(KC):
                            for h in range(2):
                                last = pe.transpose(ps[:, (2 * c + h) * P:(2 * c + h + 1) * P], XS[:, u, h, c * P:(c + 1) * P], ident[:, :])
                        last.then_inc(bank_full[b], 1)
                    elif s[0] == "up":
                        c = s[2]
                        if c == 0:
                            pe.wait_ge(sem(f"w_loaded{u}"), 16 * (before[u] + 1))
                            ready(plan, turn, ("xsT", u))
                        ps, b = fill(plan, turn, s)
                        for a in range(2):
                            for k in range(KC):
                                last = mm(ps[:, a * 256:(a + 1) * 256], up[u][:, k, (a * hc + c) * P:(a * hc + c + 1) * P],
                                          xsT[:, u, k, :], k == 0, k == KC - 1)
                        last.then_inc(bank_full[b], 1)
                    else:
                        c = s[2]
                        if c == 0:
                            ybank[u] = [fill(plan, turn, ("acc", "y", u, h)) for h in range(2)]
                        ready(plan, turn, ("up", u, c))
                        for h in range(2):
                            ps, b = ybank[u][h]
                            last = mm(ps[:, 0:D], HT[:, c, h * P:(h + 1) * P], dn[u][:, c, :], c == 0, c == hc - 1)
                            if c == hc - 1:
                                last.then_inc(bank_full[b], 1)

            def phase3(g):
                def turned(name, u, rows):
                    ps, b = fill(j3, g, (name, u))
                    for c in range(KC):
                        for t in range(TS):
                            last = pe.transpose(ps[:, (c * TS + t) * P:(c * TS + t + 1) * P], rows[:, u * TS + t, c * P:(c + 1) * P], ident[:, :])
                    last.then_inc(bank_full[b], 1)
                    ready(j3, g, (name, u))

                def project(name, u, w, src):
                    ps, b = fill(j3, g, (name, u))
                    for m in range(KC):
                        for c in range(KC):
                            last = mm(ps[:, m * TS * P:(m + 1) * TS * P], w[:, c, m * P:(m + 1) * P], cols_of(src, u)[:, c, :], c == 0, c == KC - 1)
                    last.then_inc(bank_full[b], 1)

                def project_rows(name, u, w, src):
                    ps, b = fill(j3, g, (name, u))
                    for t in range(TS):
                        for c in range(KC):
                            last = mm(ps[:, t * D:(t + 1) * D], cols_of(src, u)[:, c, t * P:(t + 1) * P], w[:, c, :], c == 0, c == KC - 1)
                    last.then_inc(bank_full[b], 1)

                def scores(name, u, q, k):
                    ps, b = fill(j3, g, (name, u))
                    for t in range(TS):
                        for m in range(KC):
                            last = mm(ps[:, t * P:(t + 1) * P], cols_of(q, u)[:, m, t * P:(t + 1) * P], cols_of(k, u)[:, m, t * P:(t + 1) * P], m == 0, m == KC - 1)
                    last.then_inc(bank_full[b], 1)

                def attend(i, u, pname, oname, v):
                    pe.wait_ge(sem(f"probs_s{u}"), 3 * g + (i + 1))
                    ps, b = fill(j3, g, (pname, u))
                    for t in range(TS):
                        last = pe.transpose(ps[:, t * P:(t + 1) * P], SC2[:, u * TS + t, :], ident[:, :])
                    last.then_inc(bank_full[b], 1)
                    ready(j3, g, (pname, u))
                    ps, b = fill(j3, g, (oname, u))
                    for t in range(TS):
                        last = mm(ps[:, t * D:(t + 1) * D], PT2[:, u * TS + t, :], v[:, u * TS + t, :])
                    last.then_inc(bank_full[b], 1)

                def turned_norm(i, name, u, rows):
                    pe.wait_ge(sem(f"normed_s{u}"), 5 * g + (i + 1))
                    turned(name, u, rows)

                streams = range(STREAMS)
                pe.wait_ge(sem("ctx_loaded"), 16 * (g + (2 * GROUPS + 1)))
                for u in streams:
                    turned("cT", u, CG)
                    project("k2", u, W3["k2"], cT)
                    project_rows("v2", u, W3["v2"], cT)
                for u in streams:
                    turned_norm(0, "xT4", u, N1)
                    project("q2", u, W3["q2"], xT)
                for u in streams:
                    ready(j3, g, ("k2", u))
                    ready(j3, g, ("q2", u))
                    scores("s2", u, qT, kT)
                for u in streams:
                    project("k4", u, W3["k4"], cT)
                    project_rows("v4", u, W3["v4"], cT)
                for u in streams:
                    ready(j3, g, ("v2", u))
                    attend(0, u, "p2", "o2", V2)
                for u in streams:
                    ready(j3, g, ("o2", u))
                    turned("oT2", u, AO)
                    project_rows("x2", u, W3["o2"], aT)
                pe.wait_ge(sem("weff_ready"), 2)
                for u in streams:
                    turned_norm(1, "xT5", u, XN)
                    project_rows("f2", u, WEFF, xT)
                for u in streams:
                    turned_norm(2, "xT6", u, IN3)
                    project("q3", u, W3["q3"], xT)
                    project("k3", u, W3["k3"], xT)
                for u in streams:
                    ready(j3, g, ("k4", u))
                    ready(j3, g, ("v4", u))
                    ready(j3, g, ("q3", u))
                    ready(j3, g, ("k3", u))
                    scores("s3", u, qT, kT)
                for u in streams:
                    project_rows("v3", u, W3["v3"], xT)
                for u in streams:
                    ready(j3, g, ("v3", u))
                    attend(1, u, "p3", "o3", V3)
                for u in streams:
                    ready(j3, g, ("o3", u))
                    turned("aT", u, AO)
                    project("q4", u, W3["q4"], aT)
                for u in streams:
                    ready(j3, g, ("q4", u))
                    scores("s4", u, qT, k4T)
                for u in streams:
                    attend(2, u, "p4", "o4", V4)
                for u in streams:
                    turned_norm(3, "nT", u, N2)
                    project("h", u, W3["h"], xT)
                for u in streams:
                    pe.wait_ge(sem(f"leaky_s{u}"), g + 1)
                    project_rows("ff", u, W3["ff"], hT3)
                for u in streams:
                    turned_norm(4, "xT7", u, XN)
                logits(j3, g, "lg1", Wr[3])
                list_ranks(j3, g, g + GROUPS)

            pe.wait_ge(sem("masks_built"), 1)
            pe.wait_ge(sem("const_loaded"), 16 * len(consts))
            for m in range(KC):
                ps, b = fill(pre, 0, ("wab", m))
                mm(ps[:, 0:D], LORA_A[:, m * P:(m + 1) * P], LORA_B[:, :]).then_inc(bank_full[b], 1)
            pe.wait_ge(sem("w0_loaded"), 16 * len(W0))
            with pe.Fori(0, GROUPS) as g:
                phase1(g)
            routed_start()
            with pe.Fori(0, GROUPS) as g:
                routed(g)
            routed_end()
            with pe.Fori(0, GROUPS) as g:
                layer1(g)

            def all_experts(layer):
                with pe.Fori(0, LOOPS) as i:
                    experts(layer, i, i, *moe[layer][0])
                experts(layer, 0, LOOPS, *moe[layer][1])

            all_experts(1)
            pe.wait_ge(sem("w3_loaded"), 16 * len(w3loads))
            with pe.Fori(0, GROUPS) as g:
                phase3(g)
            all_experts(3)

        @block.scalar
        def _(act):
            fulls = Waits(act)

            def full(plan, g, key):
                b = fulls.at_least(bank_full, plan, key, g, 1)
                return bank[b], b

            def copy_cols(plan, g, name, dst, bias=None):
                for m in range(KC):
                    ps, b = full(plan, g, (name, m))
                    if bias is None:
                        act.activation(dst[:, m, :], ps[:, :], ACT.Copy).then_inc(bank_empty[b], 1)
                    else:
                        act.activation(dst[:, m, :], ps[:, :], ACT.Identity, bias=col_bias[:, bias, m:m + 1]).then_inc(bank_empty[b], 1)

            def phase1(g):
                copy_cols(j1, g, "cT", cT)
                copy_cols(j1, g, "kT", kT, CK0)
                copy_cols(j1, g, "xT0", xT)
                copy_cols(j1, g, "qT", qT, CQ0)
                for n in range(UNITS + 1):
                    if n < UNITS:
                        u = n % 4
                        act.wait_ge(sem("maxima"), UNITS * g + (n + 1))
                        for h in range(8):
                            last = act.activation(SC[:, u, h, :], SC[:, u, h, :], ACT.Exp, bias=MX[:, 32 + 8 * u + h:33 + 8 * u + h])
                        last.then_inc(sem("probs"), 1)
                    if n >= 1:
                        i = n - 1
                        for j in range(2):
                            ps, b = full(j1, g, ("p", i, j))
                            act.activation(PT[:, i % 4, 4 * j:4 * j + 4, :], ps[:, :].rearrange("p (h k) -> p h k", h=4), ACT.Copy).then_inc(bank_empty[b], 1)
                copy_cols(j1, g, "aT", aT)
                copy_cols(j1, g, "xT1", xT)
                b, n = job(j1, ("lg",), g)
                act.wait_ge(bank_empty[b], n + 1)
                act.activation(small[:, 0, :], small[:, 0, :], ACT.Exp).then_inc(sem("logits_exp"), 1)
                for i in range(T + 2):
                    if i < T:
                        t, p = i, PAIR
                        ps, b = full(j1, g, ("up", i))
                        for a in range(2):
                            last = act.activation(SG0[:, b, a * P:(a + 1) * P], ps[:, a * 256:a * 256 + P], ACT.Silu)
                        last.then_inc(sem("silu_rows"), 1)
                    if i >= 2:
                        ps, b = full(j1, g, ("hT", i - 2))
                        act.activation(HT0[:, (i - 2) % 3, :], ps[:, 0:256], ACT.Copy).then_inc(bank_empty[b], 1)

            def routed(g):
                ps, b = full(jr, g, ("ow",))
                act.activation(OWT, ps[:, :].rearrange("p (t n) -> p t n", t=T), ACT.Copy).then_inc(bank_empty[b], 1)
                for t in range(T):
                    ps, b = full(jr, g, ("gu", t))
                    act.activation(SGR[:, t, :, :], ps[:, :].rearrange("p (k n) -> p k n", k=2)[:, :, 0:HID0], ACT.Silu).then_inc(sem("routed_silu"), 1)

            def layer1(g):
                act.wait_ge(sem("shifted16"), g + 1)
                act.activation(EXTRA[:, 1024:2048], EXTRA[:, 1024:2048], ACT.Exp).then_inc(sem("probs16"), 1)
                copy_cols(j2, g, "xT3", xT)
                router_exps(g)

            def router_exps(turn):
                act.wait_ge(sem("router_in"), 2 * turn + 1)
                act.activation(small[:, 1, :], small[:, 1, :], ACT.Exp).then_inc(sem("router_exp"), 1)
                act.wait_ge(sem("router_in"), 2 * turn + 2)
                act.activation(small[:, 8, 0:T], small[:, 8, 0:T], ACT.Exp).then_inc(sem("router_exp"), 1)

            def experts(layer, turn, pair, steps, plan):
                hc = HIDS[layer] // P
                for s in steps:
                    if s[0] == "up":
                        ps, b = full(plan, turn, s)
                        act.activation(SG[:, b, :], ps[:, 0:256], ACT.Silu).then_inc(sem("silu_slots"), 1)
                    elif s[0] == "down" and s[2] == hc - 1:
                        u = s[1]
                        ps, b = full(plan, turn, ("acc", "y", u, 0))
                        act.wait_ge(sem(f"result_free{u}"), pair + (PRIMED + tiles_before[layer][u]))
                        act.activation(YS[:, u, 0, :], ps[:, 0:D], ACT.Copy).then_inc(bank_empty[b], 1)

            def phase3(g):
                def copy(name, u, dst):
                    ps, b = full(j3, g, (name, u))
                    act.activation(dst, per_chunk(ps), ACT.Copy).then_inc(bank_empty[b], 1)

                def biased(name, u, dst, bias):
                    ps, b = full(j3, g, (name, u))
                    for m in range(KC):
                        last = act.activation(cols_of(dst, u)[:, m, :], per_chunk(ps)[:, m, :], ACT.Identity, bias=col_bias[:, bias, m:m + 1])
                    last.then_inc(bank_empty[b], 1)

                def exps(i, u):
                    act.wait_ge(sem(f"shifted_s{u}"), 3 * g + (i + 1))
                    act.activation(tiles(SC2, u), tiles(SC2, u), ACT.Exp).then_inc(sem(f"probs_s{u}"), 1)

                def turned_probs(name):
                    for u in streams:
                        ps, b = full(j3, g, (name, u))
                        act.activation(tiles(PT2, u), per_tile(ps, P), ACT.Copy).then_inc(bank_empty[b], 1)

                streams = range(STREAMS)
                for u in streams:
                    copy("cT", u, cols_of(cT, u))
                    biased("k2", u, kT, CK2)
                for u in streams:
                    copy("xT4", u, cols_of(xT, u))
                    biased("q2", u, qT, CQ2)
                for u in streams:
                    copy("k4", u, cols_of(k4T, u))
                    exps(0, u)
                turned_probs("p2")
                for u in streams:
                    copy("oT2", u, cols_of(aT, u))
                for u in streams:
                    copy("xT5", u, cols_of(xT, u))
                for u in streams:
                    copy("xT6", u, cols_of(xT, u))
                    copy("q3", u, cols_of(qT, u))
                    copy("k3", u, cols_of(kT, u))
                for u in streams:
                    ps, b = full(j3, g, ("v3", u))
                    act.activation(tiles(V3, u), per_tile(ps), ACT.Copy).then_inc(bank_empty[b], 1)
                    exps(1, u)
                turned_probs("p3")
                for u in streams:
                    copy("aT", u, cols_of(aT, u))
                    copy("q4", u, cols_of(qT, u))
                for u in streams:
                    exps(2, u)
                turned_probs("p4")
                for u in streams:
                    copy("nT", u, cols_of(xT, u))
                for u in streams:
                    copy("xT7", u, cols_of(xT, u))
                router_exps(g + GROUPS)

            act.wait_ge(sem("const_loaded"), 16 * len(consts))
            with act.Fori(0, GROUPS) as g:
                phase1(g)
            with act.Fori(0, GROUPS) as g:
                routed(g)
            with act.Fori(0, GROUPS) as g:
                layer1(g)

            def all_experts(layer):
                with act.Fori(0, LOOPS) as i:
                    experts(layer, i, i, *moe[layer][0])
                experts(layer, 0, LOOPS, *moe[layer][1])

            all_experts(1)
            with act.Fori(0, GROUPS) as g:
                phase3(g)
            all_experts(3)

        @block.vector
        def _(dve):
            step = [0, 0, 0]
            turn_of = [0]

            def d(ins):
                ins.then_inc(sem("dve_step"), 1)
                step[2] += 1
                return ins

            def settle():
                dve.wait_ge(sem("dve_step"), turn_of[0] * step[1] + (step[0] + step[2]))

            def alone():
                dve.sem_inc(sem("dve_passed"), 1)

            def enter(turn, per):
                turn_of[0], step[1], step[2] = turn, per, 0

            def leave(turns):
                assert step[2] == step[1], f"steps of a turn: {step[2]}"
                step[0] += step[1] * turns
                turn_of[0], step[1], step[2] = 0, 0, 0

            fulls, empties = Waits(dve), Waits(dve)

            def full(plan, g, key):
                b = fulls.at_least(bank_full, plan, key, g, 1)
                return bank[b], b

            def evacuated(plan, g, key):
                empties.at_least(bank_empty, plan, key, g, 1)

            def tt(o, a, b, op):
                return dve.tensor_tensor(o, a, b, op)

            def norm(src, dst, eps, count, last=None, which=range(T), stream=""):
                lo, hi = which[0], which[-1] + 1
                for t in which:
                    d(dve.bn_stats(ST[:, t, :], src(t)))
                settle()
                alone()
                for t in which:
                    d(dve.bn_aggr(MV[:, t, :], ST[:, t, :]))
                settle()
                dve.tensor_scalar(VE[:, lo:hi], MV[:, lo:hi, 1], eps, None, ALU.add).then_inc(sem("variance" + stream), 1)
                dve.wait_ge(sem("rstd" + stream), count)
                for t in which:
                    i = dve.tensor_scalar(dst(t), src(t), MV[:, t, 0:1], RS[:, t:t + 1], ALU.subtract, ALU.mult)
                    if t < hi - 1 or last is None:
                        d(i)
                    else:
                        i.then_inc(sem(last + stream), 1)

            def rank(v, n, lower, o):
                gt = cmpa[:, 0:T * n * n].rearrange("p (t i j) -> p t i j", t=T, i=n)
                eq = cmpb[:, 0:T * n * n].rearrange("p (t i j) -> p t i j", t=T, i=n)
                settle()
                d(tt(gt, rep(v, n, 2), bc(v, n), ALU.is_gt))
                d(tt(eq, rep(v, n, 2), bc(v, n), ALU.is_equal))
                settle()
                d(tt(eq, eq, rep(lower[:, :, :], T), ALU.mult))
                settle()
                d(tt(gt, gt, eq, ALU.add))
                settle()
                d(dve.tensor_reduce(o, gt, AX, ALU.add))
                settle()

            sm = lambda i, n=E: small[:, i, 0:T * n].rearrange("p (t e) -> p t e", t=T)

            def phase1(g):
                norm(lambda t: xg(g, t), lambda t: XN[:, t, :], 1e-5, 2 * g + 1, "normed")
                for t in range(T):
                    ps, b = full(j1, g, ("v", t))
                    tt(V0[:, t, :, 0:HD], ps[:, 0:D].rearrange("p (h d) -> p h d", h=H),
                       row_bias[:, BV0, :].rearrange("p (h d) -> p h d", h=H), ALU.add).then_inc(bank_empty[b], 1)

                def evac_scores(i):
                    for j in range(2):
                        ps, b = full(j1, g, ("s", i, j))
                        tt(SC[:, i % 4, 4 * j:4 * j + 4, :], ps[:, :].rearrange("p (h k) -> p h k", h=4),
                           rep(mask01[:, :], 4), ALU.mult).then_inc(bank_empty[b], 1)

                def maxima(i):
                    u = i % 4
                    if i % 2:
                        dve.wait_ge(sem("biased"), T * g + (i // 2 + 1))
                    else:
                        for j in range(2):
                            evacuated(j1, g, ("s", i, j))
                        d(tt(SC[:, u, :, :], SC[:, u, :, :], SCORE_BIAS[:, 0:8, :], ALU.add))
                        settle()
                    m = MX[:, 8 * u:8 * u + 8]
                    d(dve.tensor_reduce(m, SC[:, u, :, :], AX, ALU.max))
                    settle()
                    dve.tensor_scalar(MX[:, 32 + 8 * u:40 + 8 * u], m, -1.0, None, ALU.mult).then_inc(sem("maxima"), 1)

                def norm_out(t):
                    ps, b = full(j1, g, ("acc", "o", t))
                    o = ps[:, 0:H * VW].rearrange("p (h d) -> p h d", h=H)
                    r = RC[:, H * (t % 2):H * (t % 2) + H]
                    d(dve.reciprocal(r, o[:, :, HD]))
                    settle()
                    tt(AO[:, t, :].rearrange("p (h d) -> p h d", h=H), o[:, :, 0:HD], bc(r, HD), ALU.mult).then_inc(bank_empty[b], 1)

                for n in range(UNITS + 4):
                    if n < UNITS:
                        evac_scores(n)
                    if 1 <= n <= UNITS:
                        maxima(n - 1)
                    if n >= 5 and n % 2:
                        norm_out((n - 5) // 2)
                dve.wait_ge(sem("x_biased"), g + 1)
                for t in range(T):
                    ps, b = full(j1, g, ("xo", t))
                    tt(xg(g, t), xg(g, t), ps[:, 0:D], ALU.add).then_inc(bank_empty[b], 1)
                for t in range(T):
                    evacuated(j1, g, ("xo", t))
                alone()
                norm(lambda t: xg(g, t), lambda t: XN[:, t, :], 1e-5, 2 * g + 2, "normed")

                dve.wait_ge(sem("x_loaded"), 16 * (GROUPS - 1))
                ps, b = full(j1, g, ("lg",))
                l = ps[:, 0:T * E].rearrange("p (t e) -> p t e", t=T)
                d(dve.tensor_reduce(MX[:, 0:T], l, AX, ALU.max))
                settle()
                tt(sm(0), l, bc(MX[:, 0:T], E), ALU.subtract).then_inc(bank_empty[b], 1)
                dve.wait_ge(sem("logits_exp"), g + 1)
                d(dve.tensor_reduce(MX[:, T:2 * T], sm(0), AX, ALU.add))
                settle()
                d(dve.reciprocal(RC[:, 0:T], MX[:, T:2 * T]))
                settle()
                d(tt(sm(1), sm(0), bc(RC[:, 0:T], E), ALU.mult))
                settle()
                d(tt(sm(2), sm(1), rep(ebias[:, :], T), ALU.add))
                settle()
                d(dve.tensor_reduce(small[:, 3, 0:4 * T], small[:, 2, :].rearrange("p (a b) -> p a b", b=2), AX, ALU.add))
                rank(sm(3, 4), 4, lower4, small[:, 4, 0:4 * T].rearrange("p (t e) -> p t e", t=T))
                d(dve.tensor_scalar(small[:, 5, 0:4 * T], small[:, 4, 0:4 * T], 2.0, None, ALU.is_lt))
                settle()
                d(dve.tensor_scalar(small[:, 6, 0:4 * T], small[:, 5, 0:4 * T], 1e30, -1e30, ALU.mult, ALU.add))
                pairs = lambda i: small[:, i, :].rearrange("p (a b) -> p a b", b=2)
                d(tt(pairs(7), pairs(2), bc(small[:, 5, 0:4 * T], 2), ALU.mult))
                settle()
                d(tt(pairs(7), pairs(7), bc(small[:, 6, 0:4 * T], 2), ALU.add))
                rank(sm(7), E, lower8, RANK[:, :, :])
                for k in range(2):
                    d(dve.tensor_scalar(OH[:, :, k, :], RANK[:, :, :], float(k), None, ALU.is_equal))
                settle()
                d(dve.tensor_copy(SRC[:, ds(g * 2 * T * E, 2 * T * E)], OH[:, :, :, :].rearrange("p t k e -> p (t k e)")))
                d(tt(OHT[:, :, :, :], OH[:, :, :, :], rep(sm(1), 2, 2), ALU.mult))
                d(dve.tensor_copy(X8[:, ds(g * KC * E, KC * E)].rearrange("p (c s) -> p c s", c=KC), xT[:, :, 0:E]))
                settle()
                d(dve.tensor_reduce(WV[:, ds(g * 2 * T, 2 * T)], OHT[:, :, :, :].rearrange("p t k e -> p (t k) e"), AX, ALU.add))

                def add_y(t):
                    ps, b = full(j1, g, ("acc", "y", t))
                    tt(xg(g, t), xg(g, t), ps[:, 0:D], ALU.add).then_inc(bank_empty[b], 1)

                for i in range(T):
                    ps, b = full(j1, g, ("up", i))
                    dve.wait_ge(sem("silu_rows"), T * g + (i + 1))
                    pair = ps[:, :].rearrange("p (a n) -> p a n", a=2)
                    tt(HB0[:, i % 3, :].rearrange("p (a n) -> p a n", a=2), pair[:, :, P:2 * P],
                       SG0[:, b, :].rearrange("p (a n) -> p a n", a=2), ALU.mult).then_inc(bank_empty[b], 1)
                    if i > 0:
                        add_y(i - 1)
                add_y(T - 1)
                for t in reversed(range(T)):
                    evacuated(j1, g, ("acc", "y", t))
                settle()

            def routed_start():
                flat3 = lambda ap: ap.rearrange("p (a e) -> p a e", e=E)
                d(dve.memset(XE, 0.0))
                d(dve.memset(HS, 0.0))
                d(dve.memset(GT, 0.0))
                d(dve.tensor_reduce(small[:, 0, 0:E], SRC[:, :].rearrange("p (a e) -> p e a", e=E), AX, ALU.add))
                settle()
                dve.tensor_copy(SEL[:, 0, :], small[:, 0, 0:E]).then_inc(sem("choices_counted"), 1)
                for half in range(2):
                    i = dve.tensor_copy(XE.rearrange("p c (e n) -> p c e n", n=DIAG)[:, :, :, E * E * half:E * E * half + E],
                                        rep(X8[:, 0:KC * E].rearrange("p (c s) -> p c s", c=KC), E, 2))
                    i.then_inc(sem("first_rows_spread"), 1)
                ps, b = full(jr0, 0, ("cnt",))
                dve.tensor_copy(small[:, 1, 0:E], ps[:, 0:E]).then_inc(bank_empty[b], 1)
                evacuated(jr0, 0, ("cnt",))
                count, begin, end = small[:, 1, 0:E], small[:, 2, 0:E], small[:, 3, 0:E]
                before = cmpa[:, 0:E * E].rearrange("p (i j) -> p i j", i=E)
                d(tt(before, lower8[:, :, :], rep(count, E), ALU.mult))
                settle()
                d(dve.tensor_reduce(begin, before, AX, ALU.add))
                settle()
                d(tt(end, begin, count, ALU.add))
                place = bc(FLAT[:, :], E)
                d(tt(flat3(EO), place, rep(begin, 2 * TILES), ALU.is_ge))
                settle()
                d(tt(flat3(cmpb[:, :]), place, rep(end, 2 * TILES), ALU.is_lt))
                settle()
                d(tt(EO, EO, cmpb[:, :], ALU.mult))
                ps, b = full(jr0, 0, ("gt",))
                d(dve.tensor_copy(GT[0:64, 0:256], ps[0:64, 0:256]))
                dve.tensor_copy(GT[64:P, 256:512], ps[64:P, 0:256]).then_inc(bank_empty[b], 1)
                settle()

            def routed(g):
                eo = EO[:, ds(g * 2 * T * E, 2 * T * E)].rearrange("p (a e) -> p a e", e=E)
                src = SRC[:, ds(g * 2 * T * E, 2 * T * E)].rearrange("p (a e) -> p a e", e=E)
                d(tt(OHS.rearrange("p a (e s) -> p a e s", e=E), bc(eo, E), rep(src, E, 2), ALU.mult))
                settle()
                tt(OWS.rearrange("p t (k n) -> p (t k) n", k=2), OHS, bc(WV[:, ds(g * 2 * T, 2 * T)], E * E), ALU.mult).then_inc(sem("pairs_built"), 1)
                for t in range(T):
                    ps, b = full(jr, g, ("gu", t))
                    dve.wait_ge(sem("routed_silu"), T * g + (t + 1))
                    tt(HR[:, 2 * t:2 * t + 2, :], ps[:, :].rearrange("p (k n) -> p k n", k=2)[:, :, HID0:2 * HID0],
                       SGR[:, t, :, :], ALU.mult).then_inc(bank_empty[b], 1)
                ps, b = full(jr, g, ("hs",))
                tt(HS, HS, ps[:, 0:64], ALU.add).then_inc(bank_empty[b], 1)
                evacuated(jr, g, ("hs",))
                alone()

            def routed_end():
                ps, b = full(jr1, 0, ("dn",))
                tt(X[0:E, 0:D], X[0:E, 0:D], ps[0:E, 0:D], ALU.add).then_inc(bank_empty[b], 1)
                evacuated(jr1, 0, ("dn",))

            def layer1(g):
                alone()
                norm(lambda t: xg(g, t), lambda t: AO[:, t, :], 1e-5, 2 * g + (2 * GROUPS + 1), "normed")

                d(dve.memset(S16, 0.0))
                settle()

                def sums(pr, dst, signal):
                    off = 0
                    for k in range(4):
                        last = dst(k, pr[:, off:off + 4 * PAIRBLK[k] * HD])
                        off += 4 * PAIRBLK[k] * HD
                        if k < 3 or not signal:
                            d(last)
                    if signal:
                        last.then_inc(sem("products_used"), 1)

                def score_sums(t, pr, signal):
                    sums(pr, lambda k, part: dve.tensor_reduce(S16[:, t, 4 * k:4 * k + 4, 0:PAIRBLK[k]],
                                                               part.rearrange("p (h k d) -> p h k d", h=4, d=HD), AX, ALU.add), signal)

                def value_sums(t, pr, signal):
                    sums(pr, lambda k, part: dve.tensor_reduce(O16[:, t, 64 * k:64 * k + 64].rearrange("p (h d) -> p h d", h=4),
                                                               part.rearrange("p (h d k) -> p h d k", h=4, d=HD), AX, ALU.add), signal)

                def both(products, total, first):
                    for i in range(2):
                        for part in products(tt, PRD, 2 * i + 1):
                            d(part)
                        settle()
                        total(2 * i + 1, PRD, False)
                        dve.wait_ge(sem("products"), 4 * g + (first + i + 1))
                        total(2 * i, PR, True)
                        settle()

                dve.wait_ge(sem("ctx_loaded"), 16 * (g + (GROUPS + 1)))
                dve.wait_ge(sem("normed"), 2 * g + (2 * GROUPS + 1))
                both(score_products, score_sums, 0)
                dve.wait_ge(sem("products_used"), 4 * g + 2)
                settle()
                sv, sbv = EXTRA[:, 0:1024].rearrange("p (t n) -> p t n", t=T), EXTRA[:, 1024:2048].rearrange("p (t n) -> p t n", t=T)
                d(dve.scalar_tensor_tensor(sbv, sv, float(HD) ** -0.5, rep(causal16[:, :, :].rearrange("p h k -> p (h k)"), T), ALU.mult, ALU.add))
                settle()
                rows = EXTRA[:, 1024:2048].rearrange("p (a k) -> p a k", k=H)
                d(dve.tensor_reduce(MX[:, :], rows, AX, ALU.max))
                settle()
                tt(rows, rows, bc(MX[:, :], H), ALU.subtract).then_inc(sem("shifted16"), 1)
                dve.wait_ge(sem("probs16"), g + 1)
                d(dve.tensor_reduce(MX[:, :], rows, AX, ALU.add))
                settle()
                d(dve.reciprocal(RC[:, :], MX[:, :]))
                both(value_products, value_sums, 2)
                dve.wait_ge(sem("products_used"), 4 * g + 4)
                settle()
                o = EXTRA[:, 2048:3072].rearrange("p (a d) -> p a d", d=HD)
                d(tt(o, o, bc(RC[:, :], HD), ALU.mult))
                settle()
                d(tt(X[:, ds(g * T * D, T * D)], X[:, ds(g * T * D, T * D)], EXTRA[:, 2048:3072], ALU.add))
                settle()
                dve.wait_ge(sem("norm_rows_free"), g + PRIMED)
                alone()
                norm(lambda t: xg(g, t), lambda t: XN[:, t, :], 1e-5, 2 * g + (2 * GROUPS + 2), "normed")
                lists(j2, g, g, True)

            def lists(plan, g, turn, of_probs):
                ps, b = full(plan, g, ("lg1",))
                dve.tensor_copy(sm(2), ps[:, 0:T * E].rearrange("p (t e) -> p t e", t=T)).then_inc(bank_empty[b], 1)
                evacuated(plan, g, ("lg1",))
                d(dve.tensor_reduce(MX[:, 0:T], sm(2), AX, ALU.max))
                settle()
                tt(sm(1), sm(2), bc(MX[:, 0:T], E), ALU.subtract).then_inc(sem("router_in"), 1)
                rank(sm(2), E, lower8, RANK[:, :, :])
                dve.tensor_scalar(SEL[:, :, :], RANK[:, :, :], 2.0, None, ALU.is_lt).then_inc(sem("selected"), 1)
                d(dve.tensor_scalar(OH[:, :, 0, :], RANK[:, :, :], 0.0, None, ALU.is_equal))
                d(dve.tensor_scalar(OH[:, :, 1, :], RANK[:, :, :], 1.0, None, ALU.is_equal))
                dve.wait_ge(sem("router_exp"), 2 * turn + 1)
                v = sm(2)
                if of_probs:
                    d(dve.tensor_reduce(MX[:, T:2 * T], sm(1), AX, ALU.add))
                    settle()
                    d(dve.reciprocal(RC[:, 0:T], MX[:, T:2 * T]))
                    settle()
                    d(tt(sm(3), sm(1), bc(RC[:, 0:T], E), ALU.mult))
                    v = sm(3)
                settle()
                d(tt(OHT[:, :, :, :], OH[:, :, :, :], rep(v, 2, 2), ALU.mult))
                settle()
                d(dve.tensor_reduce(sm(4, 2), OHT[:, :, :, :], AX, ALU.add))
                settle()
                two = sm(4, 2)
                tt(small[:, 8, 0:T], two[:, :, 1], two[:, :, 0], ALU.subtract).then_inc(sem("router_in"), 1)
                dve.wait_ge(sem("router_exp"), 2 * turn + 2)
                d(dve.tensor_scalar(small[:, 5, 0:T], small[:, 8, 0:T], 1.0, None, ALU.add))
                settle()
                d(dve.reciprocal(small[:, 6, 0:T], small[:, 5, 0:T]))
                settle()
                d(tt(small[:, 7, 0:T], small[:, 6, 0:T], small[:, 8, 0:T], ALU.mult))
                cw = CW[:, ds(g * 2 * T, 2 * T)].rearrange("p (t k) -> p t k", k=2)
                d(dve.tensor_copy(cw[:, :, 0], small[:, 6, 0:T]))
                settle()
                d(dve.tensor_copy(cw[:, :, 1], small[:, 7, 0:T]))
                ps, b = full(plan, g, ("rk",))
                d(tt(sm(10), ps[:, 0:T * E].rearrange("p (t e) -> p t e", t=T), rep(base[:, :], T), ALU.add))
                settle()
                tt(base[:, :], base[:, :], ps[:, T * E:(T + 1) * E], ALU.add).then_inc(bank_empty[b], 1)
                d(tt(sm(11), sm(10), rep(region0[:, :], T), ALU.add))
                settle()
                d(tt(OHT[:, :, :, :], OH[:, :, :, :], rep(sm(11), 2, 2), ALU.mult))
                settle()
                d(dve.tensor_reduce(sm(12, 2), OHT[:, :, :, :], AX, ALU.add))
                settle()
                d(dve.tensor_copy(IDX[:, ds(g * 2 * T, 2 * T)], small[:, 12, 0:2 * T]))
                dve.tensor_copy(IDXG[:, :], small[:, 12, 0:2 * T]).then_inc(sem("slots_found"), 1)
                evacuated(plan, g, ("rk",))
                settle()

            def plan_tiles():
                J = MOE_TILES
                w = lambda i: wide[0:1, i, :].rearrange("p (j e) -> p j e", e=E)
                r = lambda i: t8[0:1, i, :]
                d(dve.tensor_scalar(r(0), base[0:1, :], float(SLOT - 1), None, ALU.add))
                settle()
                d(dve.tensor_copy(lens_i[0:1, :], r(0)))
                settle()
                d(dve.tensor_scalar(lens_i[0:1, :], lens_i[0:1, :], SLOT.bit_length() - 1, None, ALU.logical_shift_right))
                settle()
                d(dve.tensor_copy(r(1), lens_i[0:1, :]))
                settle()
                d(dve.tensor_copy(r(2), r(1)))
                for e in range(1, E):
                    settle()
                    d(tt(t8[0:1, 2, e:e + 1], t8[0:1, 2, e - 1:e], t8[0:1, 1, e:e + 1], ALU.add))
                settle()
                d(tt(r(3), r(2), r(1), ALU.subtract))
                j = jrow[0:1, :].rearrange("p (j e) -> p j e", e=E)
                d(tt(w(0), j, rep(r(2), J), ALU.is_ge))
                settle()
                d(tt(w(1), j, rep(r(3), J), ALU.is_ge))
                d(tt(w(2), j, rep(r(3), J), ALU.subtract))
                settle()
                d(tt(w(1), w(1), w(0), ALU.subtract))
                d(tt(w(2), w(2), rep(r(5), J), ALU.add))
                settle()
                d(tt(w(2), w(2), w(1), ALU.mult))
                d(dve.tensor_reduce(wide[0:1, 3, 0:J], w(0), AX, ALU.add))
                settle()
                d(dve.tensor_reduce(wide[0:1, 4, 0:J], w(2), AX, ALU.add))
                d(dve.tensor_scalar(wide[0:1, 3, 0:J], wide[0:1, 3, 0:J], float(E - 1), None, ALU.min))
                settle()
                d(dve.scalar_tensor_tensor(wide[0:1, 5, 0:J], w(0)[:, :, E - 1], float(SPARE), wide[0:1, 4, 0:J], ALU.mult, ALU.add))
                d(dve.tensor_copy(tile_e[0:1, :], wide[0:1, 3, 0:J]))
                settle()
                dve.tensor_copy(tile_r[0:1, :], wide[0:1, 5, 0:J]).then_inc(sem("tiles_planned"), 1)
                d(dve.memset(base[:, :], 0.0))
                settle()

            def experts(layer, turn, pair, steps, plan):
                hc = HIDS[layer] // P
                first = 0 if layer == 1 else MOE_TILES * (HIDS[1] // P)
                n = 0
                for s in steps:
                    if s[0] == "xsT":
                        ps, b = full(plan, turn, s)
                        dve.tensor_copy(xsT[:, s[1], :, :], ps[:, :].rearrange("p (c n) -> p c n", c=KC)).then_inc(bank_empty[b], 1)
                    elif s[0] == "up":
                        _, u, c = s
                        n += 1
                        ps, b = full(plan, turn, s)
                        dve.wait_ge(sem("silu_slots"), pair * (2 * hc) + (first + n))
                        tt(HT[:, c, :], ps[:, 256:512], SG[:, b, :], ALU.mult).then_inc(bank_empty[b], 1)
                    elif s[2] == hc - 1:
                        u = s[1]
                        ps, b = full(plan, turn, ("acc", "y", u, 1))
                        dve.wait_ge(sem(f"result_free{u}"), pair + (PRIMED + tiles_before[layer][u]))
                        dve.tensor_copy(YS[:, u, 1, :], ps[:, 0:D]).then_inc(bank_empty[b], 1)

            def all_experts(layer):
                with dve.Fori(0, LOOPS) as i:
                    experts(layer, i, i, *moe[layer][0])
                experts(layer, 0, LOOPS, *moe[layer][1])

            def combine(g, turn, u=0):
                d(dve.tensor_copy(CWP[:, :], CW[:, ds(g * 2 * T, 2 * T)]))
                dve.wait_ge(sem(f"rows_gathered{u}"), 16 * 2 * T * (turn + 1))
                settle()
                for t in range(T):
                    d(dve.scalar_tensor_tensor(xg(g, t), YA[u][:, 2 * t, :], CWP[:, 2 * t:2 * t + 1], xg(g, t), ALU.mult, ALU.add))
                settle()

            def phase3(g):
                combine(g, g)
                for t in range(T):
                    i = dve.scalar_tensor_tensor(xg(g, t), YA[0][:, 2 * t + 1, :], CWP[:, 2 * t + 1:2 * t + 2], xg(g, t), ALU.mult, ALU.add)
                    i.then_inc(sem("combined"), 1)
                dve.wait_ge(sem("combined"), T * (g + 1))
                alone()
                streams = range(STREAMS)
                xrows, xn = (lambda t: xg(g, t)), (lambda t: XN[:, t, :])

                def norm_s(u, i, src, dst, eps, last=None):
                    norm(src, dst, eps, 7 * g + i, last, range(u * TS, (u + 1) * TS), f"_s{u}")

                def shift(u):
                    sc = tiles(SC2, u)
                    d(dve.tensor_reduce(MX[:, TS * u:TS * (u + 1)], sc, AX, ALU.max))
                    settle()
                    tt(sc, sc, bc(MX[:, TS * u:TS * (u + 1)], P), ALU.subtract).then_inc(sem(f"shifted_s{u}"), 1)

                def sum_probs(u, i):
                    dve.wait_ge(sem(f"probs_s{u}"), 3 * g + (i + 1))
                    d(dve.tensor_reduce(MX[:, T + TS * u:T + TS * (u + 1)], tiles(SC2, u), AX, ALU.add))
                    settle()
                    d(dve.reciprocal(RC[:, TS * u:TS * (u + 1)], MX[:, T + TS * u:T + TS * (u + 1)]))
                    settle()

                def weighted(u, name, dst):
                    ps, b = full(j3, g, (name, u))
                    tt(tiles(dst, u), per_tile(ps), bc(RC[:, TS * u:TS * (u + 1)], D), ALU.mult).then_inc(bank_empty[b], 1)

                def add_to_x(u, name, n):
                    dve.wait_ge(sem(f"x_biased_s{u}"), 2 * g + n)
                    ps, b = full(j3, g, (name, u))
                    tt(xstream(g, u), xstream(g, u), ps[:, :], ALU.add).then_inc(bank_empty[b], 1)
                    evacuated(j3, g, (name, u))
                    alone()

                for u in streams:
                    norm_s(u, 1, xrows, lambda t: N1[:, t, :], 1e-5, "normed")
                for u in streams:
                    ps, b = full(j3, g, ("v2", u))
                    tt(tiles(V2, u), per_tile(ps), rep(row_bias[:, BV2, :], TS), ALU.add).then_inc(bank_empty[b], 1)
                d(dve.tensor_scalar(NBG[:, :], keymask[:, ds(g * T * P, T * P)], 1e9, -1e9, ALU.mult, ALU.add))
                settle()
                for u in streams:
                    ps, b = full(j3, g, ("s2", u))
                    km = keymask[:, ds(g * T * P + u * TS * P, TS * P)]
                    half = BIG[:, TS * P * u:TS * P * (u + 1)]
                    dve.scalar_tensor_tensor(half, ps[:, 0:TS * P], float(D) ** -0.5, km, ALU.mult, ALU.mult).then_inc(bank_empty[b], 1)
                    evacuated(j3, g, ("s2", u))
                    d(tt(half, half, NBG[:, TS * P * u:TS * P * (u + 1)], ALU.add))
                    settle()
                    shift(u)
                for u in streams:
                    ps, b = full(j3, g, ("v4", u))
                    dve.tensor_copy(tiles(V4, u), per_tile(ps)).then_inc(bank_empty[b], 1)
                    sum_probs(u, 0)
                for u in streams:
                    weighted(u, "o2", AO)
                dve.wait_ge(sem("norm_rows_free"), g + (PRIMED + GROUPS))
                for u in streams:
                    add_to_x(u, "x2", 1)
                    norm_s(u, 2, xrows, xn, 1e-5, "normed")
                for u in streams:
                    add_to_x(u, "f2", 2)
                    norm_s(u, 3, xrows, lambda t: IN3[:, t, :], 1e-5, "normed")
                for u in streams:
                    ps, b = full(j3, g, ("s3", u))
                    dve.scalar_tensor_tensor(tiles(SC2, u), per_tile(ps, P), float(P) ** -0.5, rep(causal[:, :], TS), ALU.mult, ALU.add).then_inc(bank_empty[b], 1)
                    evacuated(j3, g, ("s3", u))
                    shift(u)
                for u in streams:
                    sum_probs(u, 1)
                r3 = lambda t: R3[:, t, :]
                for u in streams:
                    weighted(u, "o3", AO)
                for u in streams:
                    evacuated(j3, g, ("o3", u))
                    d(tt(tiles(R3, u), tiles(AO, u), tiles(IN3, u), ALU.add))
                    settle()
                    norm_s(u, 4, r3, lambda t: N1[:, t, :], 1e-3, "n1_raw")
                for u in streams:
                    ps, b = full(j3, g, ("s4", u))
                    dve.tensor_scalar(tiles(SC2, u), per_tile(ps, P), float(P) ** -0.5, None, ALU.mult).then_inc(bank_empty[b], 1)
                    evacuated(j3, g, ("s4", u))
                    shift(u)
                for u in streams:
                    sum_probs(u, 2)
                for u in streams:
                    weighted(u, "o4", R3)
                    evacuated(j3, g, ("o4", u))
                    dve.wait_ge(sem(f"n1_ready_s{u}"), g + 1)
                    d(tt(tiles(R3, u), tiles(R3, u), tiles(N1, u), ALU.add))
                    settle()
                    norm_s(u, 5, r3, lambda t: N2[:, t, :], 1e-3)
                    settle()
                    d(tt(tiles(N2, u), tiles(N2, u), rep(row_bias[:, GAM, :], TS), ALU.mult))
                    settle()
                    tt(tiles(N2, u), tiles(N2, u), rep(row_bias[:, BET, :], TS), ALU.add).then_inc(sem(f"normed_s{u}"), 1)
                for u in streams:
                    ps, b = full(j3, g, ("h", u))
                    tt(cols_of(hTt, u), per_chunk(ps), bc(col_bias[:, CB1, :], TS * P), ALU.add).then_inc(bank_empty[b], 1)
                    evacuated(j3, g, ("h", u))
                    dve.scalar_tensor_tensor(cols_of(hT3, u), cols_of(hTt, u), 0.2, cols_of(hTt, u), ALU.mult, ALU.max).then_inc(sem(f"leaky_s{u}"), 1)
                for u in streams:
                    dve.wait_ge(sem(f"n2_biased_s{u}"), g + 1)
                    ps, b = full(j3, g, ("ff", u))
                    tt(tiles(R3, u), per_tile(ps), tiles(N2B, u), ALU.add).then_inc(bank_empty[b], 1)
                    evacuated(j3, g, ("ff", u))
                    norm_s(u, 6, r3, lambda t: N1[:, t, :], 1e-3)
                    settle()
                    d(tt(tiles(N1, u), tiles(N1, u), rep(row_bias[:, GAM, :], TS), ALU.mult))
                    settle()
                    d(tt(tiles(N1, u), tiles(N1, u), rep(row_bias[:, BET, :], TS), ALU.add))
                    settle()
                    flat = N1.rearrange("p t n -> p (t n)")[:, u * TS * D:(u + 1) * TS * D]
                    d(dve.scalar_tensor_tensor(xstream(g, u), flat, 0.0, xstream(g, u), ALU.max, ALU.add))
                    settle()
                    alone()
                    norm_s(u, 7, xrows, xn, 1e-5, "normed")
                lists(j3, g, g + GROUPS, False)

            def quantized_weight():
                d(dve.tensor_reduce(MX[:, 0:1], KER, mybir.AxisListType.XY, ALU.max, apply_absolute_value=True))
                settle()
                dve.tensor_copy(MX[:, 1:2], MX[:, 0:1]).then_inc(sem("absmax"), 1)
                dve.wait_ge(sem("absmax_all"), 1)
                d(dve.tensor_scalar(MX[:, 4:5], MX[:, 2:3], 1.0 / 7.0, None, ALU.mult))
                settle()
                d(dve.reciprocal(MX[:, 3:4], MX[:, 4:5]))
                settle()
                q = QTMP
                d(dve.tensor_scalar(q, KER, MX[:, 3:4], None, ALU.mult))
                settle()
                half = 1.5 * 2.0 ** 23
                d(dve.tensor_scalar(q, q, half, -half, ALU.add, ALU.add))
                settle()
                d(dve.tensor_scalar(q, q, -8.0, 7.0, ALU.max, ALU.min))
                settle()
                for m in range(KC):
                    dve.scalar_tensor_tensor(WEFF[:, m, :], q[:, m, :], MX[:, 4:5], LAB[:, m, :], ALU.mult, ALU.add).then_inc(sem("weff_ready"), 1)

            dve.wait_ge(sem("const_loaded"), 16 * len(consts))
            dve.wait_ge(sem("masks_built"), 1)
            d(dve.tensor_copy(mask01[:, :], maski[:, :]))
            d(dve.tensor_copy(keymask[:, :], keymask8[:, :].bitcast(U8)))
            settle()
            d(dve.tensor_scalar(mask01[:, :], mask01[:, :], 0.0, None, ALU.not_equal))
            d(dve.tensor_scalar(DIST, DIST, 0.0, None, ALU.max))
            settle()
            d(tt(DIST, DIST, mask01[:, :], ALU.mult))
            d(dve.tensor_scalar(NEG, mask01[:, :], 1e9, -1e9, ALU.mult, ALU.add))
            settle()
            for h in range(H):
                i = dve.scalar_tensor_tensor(SCORE_BIAS[:, h, :], DIST, -(0.5 ** (h + 1)), NEG, ALU.mult, ALU.add)
                if h < H - 1:
                    d(i)
            i.then_inc(sem("score_bias_ready"), 1)
            for m in range(KC):
                ps, b = full(pre, 0, ("wab", m))
                dve.tensor_copy(LAB[:, m, :], ps[:, 0:D]).then_inc(bank_empty[b], 1)
            step[0], step[2] = step[2], 0
            dve.wait_ge(sem("x0_loaded"), 16)
            enter_loop = dve.Fori(0, GROUPS)
            with enter_loop as g:
                enter(g, STEPS["phase1"])
                phase1(g)
            leave(GROUPS)

            def straight(body):
                step[1] = 0
                body()
                step[0], step[2] = step[0] + step[2], 0

            straight(routed_start)
            with dve.Fori(0, GROUPS) as g:
                enter(g, STEPS["routed"])
                routed(g)
            leave(GROUPS)
            routed_end()
            with dve.Fori(0, GROUPS) as g:
                enter(g, STEPS["layer1"])
                layer1(g)
            leave(GROUPS)

            straight(plan_tiles)
            all_experts(1)
            dve.wait_ge(sem("w3_loaded"), 16 * len(w3loads))
            straight(quantized_weight)
            with dve.Fori(0, GROUPS) as g:
                enter(g, STEPS["phase3"])
                phase3(g)
            leave(GROUPS)
            straight(plan_tiles)
            all_experts(3)
            with dve.Fori(0, GROUPS // 2) as i:
                enter(i, STEPS["last"])
                for u in range(2):
                    g = 2 * i + u
                    dve.wait_ge(sem("x_final"), g + PRIMED)
                    alone()
                    combine(g, i + (0 if u else GROUPS + 1), u)
                    for t in range(T):
                        last = dve.scalar_tensor_tensor(xg(g, t), YA[u][:, 2 * t + 1, :], CWP[:, 2 * t + 1:2 * t + 2], xg(g, t), ALU.mult, ALU.add)
                        if t < T - 1:
                            d(last)
                    last.then_inc(sem("x_final"), 1)
            leave(GROUPS // 2)

        @block.gpsimd
        def _(pool):
            def alone():
                pool.sem_inc(sem("pool_passed"), 1)

            def power(count):
                pool.wait_ge(sem("variance"), count)
                pool.tensor_tensor(RS[:, :], VE[:, :], neg_half[:, :], ALU.pow).then_inc(sem("rstd"), 1)

            def powers(count, more=1):
                for u in range(STREAMS):
                    part = slice(u * TS, (u + 1) * TS)
                    for n in range(more):
                        pool.wait_ge(sem(f"variance_s{u}"), count + n)
                        pool.tensor_tensor(RS[:, part], VE[:, part], neg_half[:, part], ALU.pow).then_inc(sem(f"rstd_s{u}"), 1)

            def x_bias(g):
                pool.wait_ge(sem("normed"), 2 * g + 1)
                alone()
                xx = xgroup(g)
                pool.tensor_tensor(xx, xx, rep(row_bias[:, BO0, :], T), ALU.add).then_inc(sem("x_biased"), 1)

            def x_bias_streams(g, normed, which):
                for u in range(STREAMS):
                    pool.wait_ge(sem(f"normed_s{u}"), normed)
                    alone()
                    xx = xstream(g, u).rearrange("p (t n) -> p t n", t=TS)
                    pool.tensor_tensor(xx, xx, rep(row_bias[:, which, :], TS), ALU.add).then_inc(sem(f"x_biased_s{u}"), 1)

            def scatter(turn):
                pool.wait_ge(sem("slots_found"), turn + 1)
                alone()
                for t in range(T):
                    for k in range(2):
                        pool.indirect_dma_start(out=xs_dram, out_offset=bass.IndirectOffsetOnAxis(ap=IDXG[:, 2 * t + k:2 * t + k + 1], axis=0),
                                                in_=XN[:, t, :], in_offset=None).then_inc(sem("rows_sent"), 16)

            def gather(g, turn, u=0):
                pool.tensor_copy(IDXP[:, u, :], IDX[:, ds(g * 2 * T, 2 * T)]).then_inc(sem("gather_index"), 1)
                pool.wait_ge(sem("gather_index"), turn + 1)
                alone()
                for t in range(T):
                    for k in range(2):
                        pool.indirect_dma_start(out=YA[u][:, 2 * t + k, :], out_offset=None, in_=ys_dram,
                                                in_offset=bass.IndirectOffsetOnAxis(ap=IDXP[:, u, 2 * t + k:2 * t + k + 1], axis=0)).then_inc(sem(f"rows_gathered{u}"), 16)

            def phase1(g):
                power(2 * g + 1)

                def spread(i):
                    t, m = i // 2, i % 2
                    b, n = job(j1, ("kT", m), g)
                    if t == 0:
                        pool.wait_ge(bank_empty[b], n + 1)
                    if i >= 4:
                        b, n = job(j1, ("s", i - 4, 1), g)
                        pool.wait_ge(bank_full[b], n + 1)
                    pool.tensor_tensor(Kb[:, i % 4, :, :], rep(kT[:, m, t * P:(t + 1) * P], 8), bc(head_of[:, :], P), ALU.mult).then_inc(sem("k_heads"), 1)

                def bias(i):
                    for j in range(2):
                        b, n = job(j1, ("s", i, j), g)
                        pool.wait_ge(bank_empty[b], n + 1)
                    pool.tensor_tensor(SC[:, i % 4, :, :], SC[:, i % 4, :, :], SCORE_BIAS[:, 8:16, :], ALU.add).then_inc(sem("biased"), 1)

                for i in range(4):
                    spread(i)
                x_bias(g)
                for i in range(UNITS):
                    if i % 2:
                        bias(i)
                    if i + 4 < UNITS:
                        spread(i + 4)
                power(2 * g + 2)

            def layer1(g):
                power(2 * g + (2 * GROUPS + 1))
                pool.wait_ge(sem("normed"), 2 * g + (2 * GROUPS + 1))
                pool.wait_ge(sem("ctx_loaded"), 16 * (g + (GROUPS + 1)))
                for n in range(4):
                    if n == 2:
                        pool.wait_ge(sem("probs16"), g + 1)
                    if n >= 1:
                        pool.wait_ge(sem("products_used"), 4 * g + n)
                    for last in (score_products if n < 2 else value_products)(pool.tensor_tensor, PR, 2 * (n % 2)):
                        pass
                    last.then_inc(sem("products"), 1)
                power(2 * g + (2 * GROUPS + 2))
                scatter(g)

            def phase3(g):
                powers(7 * g + 1)
                x_bias_streams(g, 5 * g + 1, BO2)
                pool.wait_ge(sem("combined"), T * (g + 1))
                gather(g + 1, g + 1)
                powers(7 * g + 2)
                x_bias_streams(g, 5 * g + 2, BF2)
                powers(7 * g + 3)
                powers(7 * g + 4)
                for u in range(STREAMS):
                    n1 = tiles(N1, u)
                    pool.wait_ge(sem(f"n1_raw_s{u}"), g + 1)
                    pool.tensor_tensor(n1, n1, rep(row_bias[:, GAM, :], TS), ALU.mult).then_inc(sem("n1_scaled"), 1)
                    pool.wait_ge(sem("n1_scaled"), 2 * g + (u + 1))
                    pool.tensor_tensor(n1, n1, rep(row_bias[:, BET, :], TS), ALU.add).then_inc(sem(f"n1_ready_s{u}"), 1)
                powers(7 * g + 5)
                for u in range(STREAMS):
                    pool.wait_ge(sem(f"normed_s{u}"), 5 * g + 4)
                    pool.tensor_tensor(tiles(N2B, u), tiles(N2, u), rep(row_bias[:, BB2, :], TS), ALU.add).then_inc(sem(f"n2_biased_s{u}"), 1)
                powers(7 * g + 6, 2)
                scatter(g + GROUPS)

            c = sem("pool_const")
            cn = [0]

            def k(ins):
                ins.then_inc(c, 1)
                cn[0] += 1

            def kwait():
                pool.wait_ge(c, cn[0])

            for b in range(8):
                pool.sem_inc(bank_full[b], 1)
                pool.sem_inc(bank_empty[b], 1)
            for n in PRIMED_SEMS:
                pool.sem_inc(sem(n), PRIMED)
            pool.memset(ZERO[:, :], 0.0).then_inc(sem("zero_set"), 1)
            k(pool.memset(ident[:, :], 0.0))
            k(pool.memset(tri[:, :], 1.0))
            k(pool.memset(ones[:, :], 1.0))
            k(pool.memset(neg_half[:, :], -0.5))
            k(pool.memset(lower8[:, :, :], 1.0))
            k(pool.memset(lower4[:, :, :], 1.0))
            k(pool.memset(head_of[:, :], 1.0))
            k(pool.memset(causal[:, :], 0.0))
            k(pool.memset(causal16[:, :, :], 0.0))
            k(pool.memset(V0[:, :, :, :], 1.0))
            k(pool.memset(base[:, :], 0.0))
            k(pool.memset(IDX[:, 2 * TILES:2 * (TILES + T)].bitcast(F32), 0.0))
            for e in range(E):
                k(pool.memset(region0[:, e:e + 1], float(e * CAP)))
                k(pool.memset(t8[0:1, 5, e:e + 1], float(e * REGION)))
            k(pool.iota(jrow_i[0:1, :], [[1, MOE_TILES], [0, E]], base=0, channel_multiplier=0))
            k(pool.iota(flat_i, [[2 * P, TILES], [1, 2]], base=0, channel_multiplier=2))
            k(pool.iota(dist_i, [[-1, P]], base=0, channel_multiplier=1))
            kwait()
            sel = lambda o, pat, b, cm, fill, op=ALU.is_ge: k(pool.affine_select(out=o, in_=o, pattern=pat, compare_op=op, fill=fill, base=b, channel_multiplier=cm))
            sel(ident[:, :], [[-1, P]], 0, 1, 1.0, ALU.not_equal)
            sel(tri[:, :], [[1, P]], -1, -1, 0.0)
            sel(lower8[:, :, :], [[1, E], [-1, E]], -1, 0, 0.0)
            sel(lower4[:, :, :], [[1, 4], [-1, 4]], -1, 0, 0.0)
            sel(head_of[:, :], [[-HD, 8]], 0, 1, 0.0)
            sel(causal[:, :], [[-1, P]], 0, 1, -1e30)
            sel(causal16[:, :, :], [[1, H], [-1, H]], 0, 0, -1e30)
            k(pool.tensor_copy(jrow[0:1, :], jrow_i[0:1, :]))
            k(pool.tensor_copy(DIST, dist_i))
            k(pool.tensor_copy(FLAT[:, :], flat_i))
            kwait()
            pool.affine_select(out=head_of[:, :], in_=head_of[:, :], pattern=[[HD, 8]], compare_op=ALU.is_ge, fill=0.0,
                               base=HD - 1, channel_multiplier=-1).then_inc(sem("masks_built"), 1)
            pool.wait_ge(sem("masks_built"), 1)
            pool.wait_ge(sem("score_bias_ready"), 1)
            with pool.Fori(0, GROUPS) as g:
                phase1(g)
            pool.wait_ge(sem("lists_zeroed"), 16 * zrows.shape[0])
            with pool.Fori(0, GROUPS) as g:
                layer1(g)
            pool.wait_ge(sem("absmax"), 1)
            pool.partition_all_reduce(MX[:, 2:3], MX[:, 1:2], P, RMAX).then_inc(sem("absmax_all"), 1)
            for u in range(2):
                pool.wait_ge(sem(f"y_stored{u}"), 16 * (LOOPS + 1 - u))
            gather(0, 0)
            with pool.Fori(0, GROUPS) as g:
                phase3(g)
            pool.wait_ge(sem("rows_gathered0"), 16 * 2 * T * (GROUPS + 1))
            for u in range(2):
                pool.wait_ge(sem(f"y_stored{u}"), 32 * (LOOPS + 1 - u))
            with pool.Fori(0, GROUPS // 2) as i:
                for u in range(2):
                    pool.wait_ge(sem("x_final"), 2 * i + (PRIMED + u - 1))
                    gather(2 * i + u, 2 * i + (GROUPS + 1 + u), u)


_OUT_SHAPE = (TILES, P, D)


def kernel(**inputs):
    import numpy as np
    import concourse.bacc as bacc
    from concourse.bass_utils import run_bass_kernel_spmd

    A = {k: np.asarray(v) for k, v in inputs.items()}
    kc = lambda w: np.ascontiguousarray(w.reshape(w.shape[0] // P, P, w.shape[1]).transpose(1, 0, 2))
    L0, L1, L2, L3 = "L0_xattn_", "L1_ffn_", "L2_xattn_", "L3_xattn_"
    arrays = {
        "x": A["x"], "ctx": A["ctx_1024"], "mask_qk": A["mask_1x1xSxS2_ik0"].reshape(P, P),
        "mask_bk": A["mask_BxS2_bk0"].reshape(-1),
        "ebias": A["L0_ffn_expert_bias"],
        "wr0": kc(A["L0_ffn_w_gate"].T), "wr1": kc(A["L1_ffn_router_kernel_DE"]), "wr3": kc(A["L3_ffn_gate_w"].T),
        "lora_a": A["L2_ffn_a"].T, "lora_b": A["L2_ffn_b"], "kernel": kc(A["L2_ffn_kernel"]),
        "row_bias": np.concatenate([A[L0 + "wv_b"], A[L0 + "out_b"], A[L2 + "bv"], A[L2 + "bo"], A["L2_ffn_bias"],
                                    A[L3 + "gamma"], A[L3 + "beta"], A[L3 + "b2"]]),
        "col_bias": np.stack([A[n].reshape(KC, P) for n in (L0 + "wq_b", L0 + "wk_b", L2 + "bq", L2 + "bk", L3 + "b1")]).transpose(2, 0, 1),
        "w0q": kc(A[L0 + "wq_w"].T), "w0k": kc(A[L0 + "wk_w"].T), "w0v": kc(A[L0 + "wv_w"].T), "w0o": kc(A[L0 + "out_w"].T),
        "w3q2": kc(A[L2 + "Wq"]), "w3k2": kc(A[L2 + "Wk"]), "w3v2": kc(A[L2 + "Wv"]), "w3o2": kc(A[L2 + "Wo"]),
        "w3k3": kc(A[L3 + "Wk1"]), "w3q3": kc(A[L3 + "Wq1"]), "w3v3": kc(A[L3 + "Wv1"]),
        "w3k4": kc(A[L3 + "Wk2"]), "w3q4": kc(A[L3 + "Wq2"]), "w3v4": kc(A[L3 + "Wv2"]),
        "w3h": kc(A[L3 + "W1"]), "w3ff": kc(A[L3 + "W2"]),
    }
    F = "L0_ffn_"
    gate = np.concatenate([A[F + "w1"], A[F + "sw1"].T.reshape(D, 2, HID0).transpose(1, 0, 2)])
    up = np.concatenate([A[F + "w3"], A[F + "sw3"].T.reshape(D, 2, HID0).transpose(1, 0, 2)])
    down = np.concatenate([A[F + "w2"], A[F + "sw2"].T.reshape(2, HID0, D)])
    w13 = np.stack([gate, up], axis=1).transpose(2, 0, 1, 3).reshape(D, E0 * 2 * HID0)
    arrays["w13"] = kc(w13)
    arrays["w2"] = down.transpose(1, 0, 2)

    def experts(gate, up, down):
        hid = gate.shape[2]
        gu = np.concatenate([gate, up], axis=2).reshape(E, KC, P, 2 * hid).transpose(0, 2, 1, 3).reshape(E, P, -1)
        dn = down.reshape(E, hid // P, P, D).transpose(0, 2, 1, 3).reshape(E, P, -1)
        return np.concatenate([gu, dn], axis=2)

    tr = lambda a: a.transpose(0, 2, 1)
    arrays["moe1"] = experts(A[L1 + "kernel_gating_EDF"], A[L1 + "kernel_up_EDF"], A[L1 + "kernel_down_EFD"])
    arrays["moe3"] = experts(tr(A["L3_ffn_w1"]), tr(A["L3_ffn_w3"]), tr(A["L3_ffn_w2"]))
    arrays = {n: np.ascontiguousarray(a) for n, a in arrays.items()}
    nc = bacc.Bacc("TRN2", target_bir_lowering=False, num_devices=1)
    ins = {n: nc.dram_tensor(f"in_{n}", a.shape, mybir.dt.from_np(a.dtype), kind="ExternalInput").ap() for n, a in arrays.items()}
    out = nc.dram_tensor("out_x", _OUT_SHAPE, F32, kind="ExternalOutput").ap()
    build(nc, ins, out)
    r = run_bass_kernel_spmd(nc, [{f"in_{n}": a for n, a in arrays.items()}], core_ids=[0])
    return r.results[0]["out_x"]
```

```python
from contextlib import ExitStack

import concourse.bass as bass
from concourse import mybir

P = 128
TILES = 16
T = 4
GROUPS = TILES // T
STREAMS = 2
TS = T // STREAMS
FIRST = TILES - T
D = 256
KC = D // P
H = 16
HD = D // H
E = 8
NTOK = TILES * P
CAP = NTOK
SLOT = 256
REGION = CAP // SLOT
MOE_TILES = 2 * NTOK // SLOT + E - 1
SPARE = E * REGION
HID0 = 128
E0 = 10
PAIR = E0 // 2 - 1
VW = HD + 1
HIDS = {1: 512, 3: 1024}
PAIRBLK = [4 * (b + 1) for b in range(4)]
PRW = sum(4 * n * HD for n in PAIRBLK)

F32 = mybir.dt.float32
BF16 = mybir.dt.bfloat16
I32 = mybir.dt.int32
U32 = mybir.dt.uint32
U8 = mybir.dt.uint8
ALU = mybir.AluOpType
ACT = mybir.ActivationFunctionType
AX = mybir.AxisListType.X
RMAX = bass.bass_isa.ReduceOp.max
ds = bass.ds

PRIMED = 2
PRIMED_SEMS = ["norm_rows_free", "result_free0", "result_free1", "x_final"]

RING = [0, 1, 2, 3, 4, 5]
ACC = [6, 7]


class BankPlan:

    def __init__(self):
        self.done = [0] * 8
        self.ring = 0
        self.acc = 0

    def phase(self, keys, turns):
        per, table = [0] * 8, {}
        for key in keys:
            if key[0] == "acc":
                b = ACC[self.acc % len(ACC)]
                self.acc += 1
            else:
                b = RING[self.ring % len(RING)]
                self.ring += 1
            table[key] = (b, self.done[b], per[b])
            per[b] += 1
        plan = {key: (b, base, per[b], k) for key, (b, base, k) in table.items()}
        for b in range(8):
            self.done[b] += turns * per[b]
        return plan


def job(plan, key, turn):
    b, base, per, k = plan[key]
    return b, turn * per + (base + k + 1)


class Waits:

    def __init__(self, engine):
        self.engine = engine
        self.plan = None

    def at_least(self, sem, plan, key, turn, more):
        b, n = job(plan, key, turn)
        _, base, _, k = plan[key]
        if self.plan is not plan:
            self.plan, self.had = plan, {}
        if self.had.get(b, -1) < base + k + more:
            self.had[b] = base + k + more
            self.engine.wait_ge(sem[b], n + more)
        return b


STEPS = {"phase1": 160, "routed": 1, "layer1": 96, "phase3": 133, "last": 16}


def build(nc, ins, out):
    x_in, ctx_in, mask_qk, mask_bk = ins["x"], ins["ctx"], ins["mask_qk"], ins["mask_bk"]

    bp = BankPlan()
    pre = bp.phase([("wab", 0), ("wab", 1)], 1)
    k1 = [("cT", 0), ("cT", 1), ("kT", 0), ("kT", 1)] + [("v", t) for t in range(T)]
    k1 += [("xT0", 0), ("xT0", 1), ("qT", 0), ("qT", 1)]
    UNITS = 2 * T
    att_order = []
    for n in range(UNITS + 4):
        att_order += [(a, n - lag) for a, lag in (("s", 0), ("p", 3), ("o", 4)) if 0 <= n - lag < UNITS]
    for a, i in att_order:
        if a != "o":
            k1 += [(a, i, 0), (a, i, 1)]
        elif i % 2 == 0:
            k1.append(("acc", "o", i // 2))
    k1 += [("aT", 0), ("aT", 1)] + [("xo", t) for t in range(T)] + [("xT1", 0), ("xT1", 1), ("lg",)]
    ffn_steps = []
    for i in range(T + 3):
        if i < T:
            ffn_steps.append(("up", i))
        if 2 <= i < T + 2:
            ffn_steps.append(("hT", i - 2))
        if i >= 3:
            ffn_steps.append(("down", i - 3))
    for s, i in ffn_steps:
        k1.append(("acc", "y", i) if s == "down" else (s, i))
    l1_keys = [("xT3", 0), ("xT3", 1), ("lg1",), ("rk",)]
    j1 = bp.phase(k1, 1)
    k1f = []
    for key in k1:
        if key == ("xT1", 0):
            k1f += l1_keys[0:3]
        k1f.append(key)
        if key == ("lg",):
            k1f.append(("rk",))
    jf = bp.phase(k1f, GROUPS - 1)
    jr0 = bp.phase([("cnt",), ("gt",)], 1)
    jr = bp.phase([("ow",)] + [("gu", t) for t in range(T)] + [("hs",)], GROUPS)
    jr1 = bp.phase([("dn",)], 1)
    j2 = bp.phase(l1_keys, 1)

    def moe_steps(hc, second):
        seq = [(u, c) for u in range(2 if second else 1) for c in range(hc)]
        steps = [("xsT", 0)]
        for i in range(len(seq) + 2):
            if i < len(seq):
                steps.append(("up",) + seq[i])
                if seq[i][0] == 0 and seq[i][1] == hc - 3 and second:
                    steps.append(("xsT", 1))
            if i >= 2:
                steps.append(("down",) + seq[i - 2])
        return steps

    def moe_keys(steps):
        keys = []
        for s in steps:
            if s[0] == "down":
                if s[2] == 0:
                    keys += [("acc", "y", s[1], 0), ("acc", "y", s[1], 1)]
            else:
                keys.append(s)
        return keys

    moe = {}
    LOOPS = MOE_TILES // 2
    moe[1] = [(moe_steps(4, True), bp.phase(moe_keys(moe_steps(4, True)), LOOPS)),
              (moe_steps(4, False), bp.phase(moe_keys(moe_steps(4, False)), 1))]
    k3 = []
    for names in (("xT4", "q2"), ("s2",), ("k4", "v4"), ("p2", "o2"), ("oT2", "x2"), ("xT5", "f2"),
                  ("xT6", "q3", "k3"), ("s3",), ("v3",), ("p3", "o3"), ("aT", "q4"), ("s4",), ("p4", "o4"), ("nT", "h"), ("ff",),
                  ("xT7",)):
        for u in range(STREAMS):
            k3 += [(n, u) for n in names]
    front3 = [(n, u) for u in range(STREAMS) for n in ("cT", "k2", "v2")]
    j3f = bp.phase(front3, 1)
    at = k3.index(("xT7", 0))
    j3 = bp.phase(k3[:at] + front3 + k3[at:] + [("lg1",), ("rk",)], GROUPS - 1)
    j3e = bp.phase(k3 + [("lg1",), ("rk",)], 1)
    moe[3] = [(moe_steps(8, True), bp.phase(moe_keys(moe_steps(8, True)), LOOPS)),
              (moe_steps(8, False), bp.phase(moe_keys(moe_steps(8, False)), 1))]

    tiles_before = {1: (0, 0), 3: (LOOPS + 1, LOOPS)}

    ctx = ExitStack()
    with ctx:
        def sb(name, shape, dt=F32):
            return ctx.enter_context(nc.sbuf_tensor(name, shape, dt))

        sems = {}

        def sem(name):
            if name not in sems:
                sems[name] = ctx.enter_context(nc.semaphore(name))
            return sems[name]

        bank = [ctx.enter_context(nc.psum_tensor(f"bank{b}", [P, 512], F32)) for b in range(8)]
        bank_full = [sem(f"bank_full{b}") for b in range(8)]
        bank_empty = [sem(f"bank_empty{b}") for b in range(8)]

        xs_dram = nc.dram_tensor("expert_rows_in", ((SPARE + 1) * SLOT, D), F32, kind="Internal").ap()
        ys_dram = nc.dram_tensor("expert_rows_out", ((SPARE + 1) * SLOT, D), F32, kind="Internal").ap()

        X = sb("x_stream", [P, TILES * D])
        ident = sb("ident", [P, P])
        tri = sb("tri", [P, P], BF16)
        ones = sb("ones", [P, P], BF16)
        neg_half = sb("neg_half", [P, T])
        lower8 = sb("lower8", [P, E, E])
        lower4 = sb("lower4", [P, 4, 4])
        head_of = sb("head_of_row", [P, 8])
        region0 = sb("region_start", [P, E])
        causal = sb("causal", [P, P])
        causal16 = sb("causal16", [P, H, H])
        row_bias = sb("row_bias", [P, 8, D])
        BV0, BO0, BV2, BO2, BF2, GAM, BET, BB2 = range(8)
        col_bias = sb("col_bias", [P, 5, KC])
        CQ0, CK0, CQ2, CK2, CB1 = range(5)
        ebias = sb("expert_bias", [P, E])
        keymask8 = sb("keymask8", [P, TILES * P // 4], I32)
        mask01 = sb("mask01", [P, P])
        maski = sb("maski", [P, P], I32)
        Wr0 = sb("w_router0", [P, KC, E])
        Wr = {1: sb("w_router1", [P, KC, E]), 3: sb("w_router3", [P, KC, E])}
        IDX = sb("slot_index", [P, TILES * 2], U32)
        IDXG = sb("slot_index_group", [P, T * 2], U32)
        IDXP = sb("slot_index_gather", [P, 2, T * 2], U32)
        CW = sb("combine_weight", [P, TILES * 2])
        CWP = sb("combine_weight_group", [P, T * 2])
        WREG = sb("weights", [P, 9984])
        BIG = sb("work", [P, 12288])
        KB, SB = 3, 4
        Kb = BIG[:, 0:1024 * KB].rearrange("p (b h k) -> p b h k", b=KB, h=8)
        SC = BIG[:, 3072:3072 + 1024 * SB].rearrange("p (b h k) -> p b h k", b=SB, h=8)
        PT = BIG[:, 7168:7168 + 1024 * KB].rearrange("p (b h q) -> p b h q", b=KB, h=8)
        PR = [BIG[:, 10240 + 4 * HD * sum(PAIRBLK[:k]):10240 + 4 * HD * sum(PAIRBLK[:k + 1])] for k in range(3)]
        PR.append(sb("products_last_block", [P, 4 * H * HD])[:, :])
        ZERO = sb("zero", [P, D])
        NBG = sb("key_penalty", [P, T * P])
        CG = sb("ctx_rows", [P, T, D])
        CG2 = sb("ctx_rows_layer1", [P, T, D])
        NA = sb("norm_rows_layer1", [P, T, D])
        PRD = sb("products_dve", [P, 4 * H * HD])
        cT = sb("ctx_cols", [P, KC, T * P])
        kT = sb("k_cols", [P, KC, T * P])
        qT = sb("q_cols", [P, KC, T * P])
        XN = sb("norm_rows", [P, T, D])
        xT = sb("norm_cols", [P, KC, T * P])
        AO = sb("att_rows", [P, T, D])
        aT = sb("att_cols", [P, KC, T * P])
        V0 = sb("v_rows", [P, T, H, VW])
        SCORE_BIAS = sb("score_bias", [P, H, P])
        EXTRA = sb("extra", [P, 3072])
        ST = sb("stats", [P, T, 6])
        MV = sb("mean_var", [P, T, 2])
        VE = sb("var_eps", [P, T])
        RS = sb("rstd", [P, T])
        MX = sb("row_max", [P, 64])
        RC = sb("row_rec", [P, 64])
        MX16 = sb("row_max16", [P, T * H])
        RC16 = sb("row_rec16", [P, T * H])
        small = sb("small", [P, 16, T * E])
        cmpa = sb("cmpa", [P, T * E * E])
        cmpb = sb("cmpb", [P, T * E * E])
        SRC = sb("source_row", [P, TILES * 2 * E])
        WV = sb("choice_weight", [P, TILES * 2])
        FLAT = sb("flat_place", [P, TILES * 2])
        X8 = sb("first_rows_cols", [P, GROUPS * KC * E])
        RANK = sb("rank", [P, T, E])
        OH = sb("onehot", [P, T, 2, E])
        OHT = sb("onehot_t", [P, T, 2, E])
        SEL = sb("selected", [P, T, E], BF16)
        base = sb("list_len", [P, E])
        lens_i = sb("lens_i", [1, E], I32)
        t8 = sb("tile8", [1, 6, E])
        jrow_i = sb("jrow_i", [1, MOE_TILES * E], I32)
        LAB = sb("lora_product", [P, KC, D])
        jrow = sb("jrow", [1, MOE_TILES * E])
        tile_e = sb("tile_expert", [1, MOE_TILES], I32)
        tile_r = sb("tile_region", [1, MOE_TILES], I32)

        def wview(off, k):
            return WREG[:, off:off + KC * k].rearrange("p (c n) -> p c n", c=KC)

        W0 = {n: wview(i * 512, D) for i, n in enumerate(("q", "k", "v", "o"))}
        W13 = wview(2048, E0 * 2 * HID0)
        W2 = WREG[:, 2048 + KC * E0 * 256:2048 + KC * E0 * 256 + E0 * D].rearrange("p (e n) -> p e n", e=E0)
        L3N = ("q2", "k2", "v2", "o2", "k3", "q3", "v3", "k4", "q4", "v4", "h", "ff")
        W3 = {n: wview(i * 512, D) for i, n in enumerate(L3N)}
        WEFF = wview(12 * 512, D)
        KER = wview(13 * 512, D)
        QTMP = wview(14 * 512, D)
        LORA_A = sb("lora_a", [16, D])
        LORA_B = sb("lora_b", [16, D])
        WB = [BIG[:, 6144 * u:6144 * (u + 1)] for u in range(2)]

        SG0 = BIG[:, 7168:8704].rearrange("p (b n) -> p b n", b=len(RING))
        HB0 = BIG[:, 8704:9472].rearrange("p (b n) -> p b n", b=3)
        HT0 = BIG[:, 9472:10240].rearrange("p (b n) -> p b n", b=3)
        S16 = EXTRA[:, 0:1024].rearrange("p (t h k) -> p t h k", t=T, h=H)
        S16b = EXTRA[:, 1024:2048].rearrange("p (t h k) -> p t h k", t=T, h=H)
        O16 = EXTRA[:, 2048:3072].rearrange("p (t n) -> p t n", t=T)
        DIAG = 2 * E * E + E
        XE = BIG[:, 0:KC * E * DIAG].rearrange("p (c n) -> p c n", c=KC)
        OHS = BIG[:, 2176:2688].rearrange("p (a n) -> p a n", a=2 * T)
        OWS = BIG[:, 2688:3200].rearrange("p (t n) -> p t n", t=T)
        OWT = BIG[:, 3200:3712].rearrange("p (t n) -> p t n", t=T)
        GT = BIG[:, 3712:4224]
        SGR = BIG[:, 4224:5248].rearrange("p (t k n) -> p t k n", t=T, k=2)
        HR = BIG[:, 5248:6272].rearrange("p (a n) -> p a n", a=2 * T)
        HS = BIG[:, 6272:6336]
        EO = BIG[:, 6336:6592]
        wide = SCORE_BIAS[0:1, :, :].rearrange("p h k -> p (h k)")[:, 0:6 * MOE_TILES * E].rearrange("p (a n) -> p a n", a=6)
        XS = aT[:, :, :].rearrange("p c (h n) -> p c h n", h=2)
        xsT = xT[:, :, :].rearrange("p c (u n) -> p u c n", u=2)
        SG = SCORE_BIAS[:, 0:12, :].rearrange("p (b a) k -> p b (a k)", b=len(RING))
        HT = EXTRA[:, 0:2048].rearrange("p (c n) -> p c n", c=8)
        YS = AO[:, :, :].rearrange("p (u h) n -> p u h n", u=2)
        SC2 = BIG[:, 0:512].rearrange("p (t k) -> p t k", t=T)
        PT2 = BIG[:, 512:1024].rearrange("p (t k) -> p t k", t=T)
        V2 = BIG[:, 1024:2048].rearrange("p (t n) -> p t n", t=T)
        V4 = BIG[:, 2048:3072].rearrange("p (t n) -> p t n", t=T)
        V3 = BIG[:, 3072:4096].rearrange("p (t n) -> p t n", t=T)
        k4T = BIG[:, 4096:5120].rearrange("p (c n) -> p c n", c=KC)
        IN3 = BIG[:, 5120:6144].rearrange("p (t n) -> p t n", t=T)
        N1 = BIG[:, 6144:7168].rearrange("p (t n) -> p t n", t=T)
        N2 = BIG[:, 7168:8192].rearrange("p (t n) -> p t n", t=T)
        R3 = BIG[:, 8192:9216].rearrange("p (t n) -> p t n", t=T)
        hT3 = BIG[:, 9216:10240].rearrange("p (c n) -> p c n", c=KC)
        hTt = BIG[:, 10240:11264].rearrange("p (c n) -> p c n", c=KC)
        N2B = BIG[:, 11264:12288].rearrange("p (t n) -> p t n", t=T)
        YA = [buf[:, 0:2 * T * D].rearrange("p (a n) -> p a n", n=D) for buf in (EXTRA, BIG)]

        def tiles(buf, u):
            return buf[:, u * TS:(u + 1) * TS, :]

        def cols_of(buf, u):
            return buf[:, :, u * TS * P:(u + 1) * TS * P]

        def per_chunk(ps):
            return ps[:, :].rearrange("p (c n) -> p c n", c=KC)

        def per_tile(ps, n=D):
            return ps[:, 0:TS * n].rearrange("p (t n) -> p t n", t=TS)

        xstream = lambda g, u: X[:, ds((T * g + TS * u) * D, TS * D)]
        KM = EXTRA[:, 2048:2048 + T * P]
        dist_i = AO[:, 2, 0:P].bitcast(I32)
        flat_i = AO[:, 3, 0:2 * TILES].bitcast(I32)
        DIST = AO[:, 0, 0:P]
        NEG = AO[:, 1, 0:P]

        xg = lambda g, t: X[:, ds((T * g + t) * D, D)]
        xgroup = lambda g: X[:, ds(g * T * D, T * D)].rearrange("p (t n) -> p t n", t=T)

        def bc(ap, n):
            return ap.unsqueeze(len(ap.shape)).to_broadcast(list(ap.shape) + [n])

        def rep(ap, n, at=1):
            s = list(ap.shape)
            return ap.unsqueeze(at).to_broadcast(s[:at] + [n] + s[at:])

        consts = [(maski[:, :], mask_qk), (keymask8[:, :].bitcast(U8), mask_bk.partition_broadcast(P)),
                  (ebias[:, :], ins["ebias"].partition_broadcast(P)),
                  (Wr0[:, :, :], ins["wr0"]), (Wr[1][:, :, :], ins["wr1"]), (Wr[3][:, :, :], ins["wr3"]),
                  (LORA_A[:, :], ins["lora_a"]), (LORA_B[:, :], ins["lora_b"]),
                  (row_bias[:, :, :].rearrange("p a n -> p (a n)"), ins["row_bias"].partition_broadcast(P)),
                  (col_bias[:, :, :], ins["col_bias"])]
        w1loads = [(W0["q"], ins["w0q"]), (W0["k"], ins["w0k"]), (W0["v"], ins["w0v"]), (W0["o"], ins["w0o"]),
                   (W13, ins["w13"]), (W2, ins["w2"])]
        w3loads = [(W3[n], ins["w3" + n]) for n in L3N] + [(KER, ins["kernel"])]
        ZCHUNK = 10
        zrows = xs_dram.rearrange("(a p r) d -> a p (r d)", p=P, r=ZCHUNK)

        yrows = ys_dram.rearrange("(a p r) d -> a p (r d)", p=P, r=ZCHUNK)

        def score_products(tt, dst, t, k):
            nk = PAIRBLK[k]
            q = NA[:, t, :].rearrange("p (h d) -> p h d", h=H)
            kv = CG2[:, t, :].rearrange("p (k d) -> p k d", k=H)
            return tt(dst.rearrange("p (h k d) -> p h k d", h=4, d=HD), rep(q[:, 4 * k:4 * k + 4, :], nk, 2), rep(kv[:, 0:nk, :], 4), ALU.mult)

        def value_products(tt, dst, t, k):
            nk = PAIRBLK[k]
            vt = CG2[:, t, :].rearrange("p (k d) -> p d k", k=H)
            return tt(dst.rearrange("p (h d k) -> p h d k", h=4, d=HD), rep(S16b[:, t, 4 * k:4 * k + 4, 0:nk], HD, 2), rep(vt[:, :, 0:nk], 4), ALU.mult)

        block = ctx.enter_context(nc.Block())

        @block.sync
        def _(sp):
            def load_x(g, name):
                sp.dma_start(xgroup(g), x_in[ds(g * T, T), :, :].rearrange("t p n -> p t n")).then_inc(sem(name), 16)

            load_x(0, "x0_loaded")
            for dst, src in consts:
                sp.dma_start(dst, src).then_inc(sem("const_loaded"), 16)
            sp.dma_start(CG[:, :, :], ctx_in[0:T, :, :].rearrange("t p n -> p t n")).then_inc(sem("ctx_loaded"), 16)
            for dst, src in w1loads[:len(W0)]:
                sp.dma_start(dst, src).then_inc(sem("w0_loaded"), 16)
            sp.dma_start(CG2[:, :, :], ctx_in[0:T, :, :].rearrange("t p n -> p t n")).then_inc(sem("ctx2_loaded"), 16)
            for dst, src in w1loads[len(W0):]:
                sp.dma_start(dst, src).then_inc(sem("w1_loaded"), 16)
            for g in range(1, GROUPS):
                load_x(g, "x_loaded")
            sp.wait_ge(sem("zero_set"), 1)
            for i in range(zrows.shape[0]):
                sp.dma_start(zrows[i, :, :].rearrange("p (r d) -> p r d", d=D), rep(ZERO[:, :], ZCHUNK)).then_inc(sem("lists_zeroed"), 16)

            def ctx_loads():
                b, n = job(j1, ("cT", 1), 0)
                sp.wait_ge(bank_full[b], n + 1)
                sp.dma_start(CG[:, :, :], ctx_in[T:2 * T, :, :].rearrange("t p n -> p t n")).then_inc(sem("ctx_loaded"), 16)
                with sp.Fori(1, GROUPS - 1) as g:
                    b, n = job(jf, ("cT", 1), g)
                    sp.wait_ge(bank_full[b], n)
                    sp.dma_start(CG[:, :, :], ctx_in[ds((g + 1) * T, T), :, :].rearrange("t p n -> p t n")).then_inc(sem("ctx_loaded"), 16)
                    sp.wait_ge(sem("normed_l1"), 2 * g)
                    sp.dma_start(CG2[:, :, :], ctx_in[ds(g * T, T), :, :].rearrange("t p n -> p t n")).then_inc(sem("ctx2_loaded"), 16)
                    sp.wait_ge(sem("rows_sent"), 16 * 2 * T * g)
                    sp.sem_inc(sem("norm_rows_free"), 1)
                last = GROUPS - 1
                sp.wait_ge(sem("normed_l1"), 2 * last)
                sp.dma_start(CG2[:, :, :], ctx_in[last * T:GROUPS * T, :, :].rearrange("t p n -> p t n")).then_inc(sem("ctx2_loaded"), 16)
                sp.wait_ge(sem("rows_sent"), 16 * 2 * T * last)
                sp.sem_inc(sem("norm_rows_free"), 1)
                for i in range(yrows.shape[0]):
                    sp.dma_start(yrows[i, :, :].rearrange("p (r d) -> p r d", d=D), rep(ZERO[:, :], ZCHUNK)).then_inc(sem("results_zeroed"), 16)

            def experts(layer):
                wsrc = ins[f"moe{layer}"]
                width = wsrc.shape[2]

                def load_weights(u, j):
                    e = sp.value_load(tile_e[0:1, ds(j, 1)], min_val=0, max_val=E - 1)
                    sp.dma_start(WB[u][:, 0:width], wsrc[ds(e, 1), :, :].rearrange("a p n -> p (a n)")).then_inc(sem(f"w_loaded{u}"), 16)

                def load_rows(u, j):
                    r = sp.value_load(tile_r[0:1, ds(j, 1)], min_val=0, max_val=SPARE)
                    sp.dma_start(XS[:, u, :, :], xs_dram[ds(r * SLOT, SLOT), :].rearrange("(h p) d -> p h d", p=P)).then_inc(sem(f"rows_loaded{u}"), 16)

                def load(u, j):
                    load_rows(u, j)
                    load_weights(u, j)

                def buffers_free(plan, turn, u):
                    b, n = job(plan, ("acc", "y", u, 1), turn)
                    sp.wait_ge(bank_full[b], n + 1)

                def store(plan, turn, pair, u, j):
                    for h in range(2):
                        b, n = job(plan, ("acc", "y", u, h), turn)
                        sp.wait_ge(bank_empty[b], n + 1)
                    r = sp.value_load(tile_r[0:1, ds(j, 1)], min_val=0, max_val=SPARE)
                    sp.dma_start(ys_dram[ds(r * SLOT, SLOT), :].rearrange("(h p) d -> p h d", p=P), YS[:, u, :, :]).then_inc(sem(f"y_stored{u}"), 16)
                    sp.wait_ge(sem(f"y_stored{u}"), (pair + tiles_before[layer][u] + 1) * 16)
                    sp.sem_inc(sem(f"result_free{u}"), 1)

                loop, tail = moe[layer][0][1], moe[layer][1][1]
                load_weights(0, 0)
                sp.wait_ge(sem("rows_sent"), 16 * 2 * TILES * (1 if layer == 1 else 2))
                load_rows(0, 0)
                load_rows(1, 1)
                load_weights(1, 1)
                if layer == 1:
                    sp.sem_inc(sem("norm_rows_free"), 1)
                    for dst, src in w3loads:
                        sp.dma_start(dst, src).then_inc(sem("w3_loaded"), 16)
                    sp.dma_start(CG[:, :, :], ctx_in[0:T, :, :].rearrange("t p n -> p t n")).then_inc(sem("ctx_loaded"), 16)
                with sp.Fori(0, LOOPS - 1) as i:
                    for u in range(2):
                        buffers_free(loop, i, u)
                        load(u, 2 * i + (2 + u))
                        store(loop, i, i, u, 2 * i + u)
                i = LOOPS - 1
                buffers_free(loop, i, 0)
                load(0, 2 * LOOPS)
                for u in range(2):
                    store(loop, i, i, u, 2 * i + u)
                store(tail, 0, LOOPS, 0, 2 * LOOPS)

            ctx_loads()
            sp.wait_ge(sem("tiles_planned"), 1)
            sp.wait_ge(sem("results_zeroed"), 16 * yrows.shape[0])
            experts(1)
            b, n = job(j3f, ("cT", 1), 0)
            sp.wait_ge(bank_full[b], n + 1)
            sp.dma_start(CG[:, :, :], ctx_in[T:2 * T, :, :].rearrange("t p n -> p t n")).then_inc(sem("ctx_loaded"), 16)
            with sp.Fori(0, GROUPS - 2) as i:
                b, n = job(j3, ("cT", 1), i)
                sp.wait_ge(bank_full[b], n + 1)
                sp.dma_start(CG[:, :, :], ctx_in[ds((i + 2) * T, T), :, :].rearrange("t p n -> p t n")).then_inc(sem("ctx_loaded"), 16)
                sp.wait_ge(sem("rows_sent"), 16 * 2 * T * (i + (GROUPS + 1)))
                sp.sem_inc(sem("norm_rows_free"), 1)
            sp.wait_ge(sem("rows_sent"), 16 * 2 * T * (2 * GROUPS - 1))
            sp.sem_inc(sem("norm_rows_free"), 1)
            sp.wait_ge(sem("tiles_planned"), 2)
            experts(3)
            with sp.Fori(0, GROUPS) as g:
                sp.wait_ge(sem("x_final"), PRIMED + g + 1)
                sp.dma_start(out[ds(g * T, T), :, :].rearrange("t p n -> p t n"), xgroup(g)).then_inc(sem("out_stored"), 16)
            sp.wait_ge(sem("out_stored"), 16 * GROUPS)

        @block.tensor
        def _(pe):
            empties = Waits(pe)

            def fill(plan, g, key):
                b = empties.at_least(bank_empty, plan, key, g, 0)
                return bank[b], b

            def ready(plan, g, key):
                empties.at_least(bank_empty, plan, key, g, 1)

            def mm(o, l, r, a=True, z=True):
                return pe.matmul(o, l, r, start=a, stop=z)

            def turn_rows(plan, g, name, rows):
                for c in range(KC):
                    ps, b = fill(plan, g, (name, c))
                    for t in range(T):
                        m = pe.transpose(ps[:, t * P:(t + 1) * P], rows[:, t, c * P:(c + 1) * P], ident[:, :])
                    m.then_inc(bank_full[b], 1)

            def cols(plan, g, name, w, src):
                for m in range(KC):
                    ps, b = fill(plan, g, (name, m))
                    for c in range(KC):
                        last = mm(ps[:, :], w[:, c, m * P:(m + 1) * P], src[:, c, :], c == 0, c == KC - 1)
                    last.then_inc(bank_full[b], 1)

            def rows2(plan, g, name, w, src):
                for a in range(2):
                    ps, b = fill(plan, g, (name, a))
                    for i in range(2):
                        t = 2 * a + i
                        for c in range(KC):
                            last = mm(ps[:, i * D:(i + 1) * D], src[:, c, t * P:(t + 1) * P], w[:, c, :], c == 0, c == KC - 1)
                    last.then_inc(bank_full[b], 1)

            def rows1(plan, g, name, w, src):
                for t in range(T):
                    ps, b = fill(plan, g, (name, t))
                    for c in range(KC):
                        last = mm(ps[:, 0:D], src[:, c, t * P:(t + 1) * P], w[:, c, :], c == 0, c == KC - 1)
                    last.then_inc(bank_full[b], 1)

            def logits(plan, g, name, w, src=xT):
                ps, b = fill(plan, g, (name,))
                for t in range(T):
                    for c in range(KC):
                        last = mm(ps[:, t * E:(t + 1) * E], src[:, c, t * P:(t + 1) * P], w[:, c, :], c == 0, c == KC - 1)
                last.then_inc(bank_full[b], 1)

            def list_ranks(plan, g, turn):
                ps, b = fill(plan, g, ("rk",))
                pe.wait_ge(sem("selected"), turn + 1)
                for t in range(T):
                    for s in range(t + 1):
                        mm(ps[:, t * E:(t + 1) * E], tri[:, :] if s == t else ones[:, :], SEL[:, s, :], s == 0, s == t)
                for s in range(T):
                    last = mm(ps[:, T * E:(T + 1) * E], ones[:, :], SEL[:, s, :], s == 0, s == T - 1)
                last.then_inc(bank_full[b], 1)

            def layer1_logits(plan, turn, g):
                pe.wait_ge(sem("normed_l1"), 2 * g + 2)
                turn_rows(plan, turn, "xT3", NA)
                ready(plan, turn, ("xT3", 0))
                ready(plan, turn, ("xT3", 1))
                logits(plan, turn, "lg1", Wr[1], kT)

            def phase1(plan, turn, g, prev):
                pe.wait_ge(sem("ctx_loaded"), 16 * (g + 1))
                turn_rows(plan, turn, "cT", CG)
                ready(plan, turn, ("cT", 0))
                ready(plan, turn, ("cT", 1))
                cols(plan, turn, "kT", W0["k"], cT)
                rows1(plan, turn, "v", W0["v"], cT)
                pe.wait_ge(sem("normed"), 2 * g + 1)
                turn_rows(plan, turn, "xT0", XN)
                ready(plan, turn, ("xT0", 0))
                ready(plan, turn, ("xT0", 1))
                cols(plan, turn, "qT", W0["q"], xT)
                ready(plan, turn, ("qT", 0))
                ready(plan, turn, ("qT", 1))
                for a, i in att_order:
                    t, m, u, w = i // 2, i % 2, i % KB, i % SB
                    if a == "s":
                        pe.wait_ge(sem("k_heads"), UNITS * g + (i + 1))
                        for j in range(2):
                            ps, b = fill(plan, turn, ("s", i, j))
                            mm(ps[:, :].rearrange("p (h k) -> p h k", h=4), qT[:, m, t * P:(t + 1) * P],
                               Kb[:, u, 4 * j:4 * j + 4, :]).then_inc(bank_full[b], 1)
                    elif a == "p":
                        pe.wait_ge(sem("probs"), UNITS * g + (i + 1))
                        for j in range(2):
                            ps, b = fill(plan, turn, ("p", i, j))
                            for h in range(4):
                                last = pe.transpose(ps[:, h * P:(h + 1) * P], SC[:, w, 4 * j + h, :], ident[:, :])
                            last.then_inc(bank_full[b], 1)
                    else:
                        if m == 0:
                            ready(plan, turn, ("v", t))
                            ps_o, b_o = fill(plan, turn, ("acc", "o", t))
                        for j in range(2):
                            ready(plan, turn, ("p", i, j))
                        for h in range(8):
                            last = mm(ps_o[:, (8 * m + h) * VW:(8 * m + h + 1) * VW], PT[:, u, h, :], V0[:, t, 8 * m + h, :])
                        if m == 1:
                            last.then_inc(bank_full[b_o], 1)
                for t in range(T):
                    ready(plan, turn, ("acc", "o", t))
                turn_rows(plan, turn, "aT", AO)
                ready(plan, turn, ("aT", 0))
                ready(plan, turn, ("aT", 1))
                rows1(plan, turn, "xo", W0["o"], aT)
                if prev is not None:
                    layer1_logits(plan, turn, prev)
                pe.wait_ge(sem("normed"), 2 * g + 2)
                turn_rows(plan, turn, "xT1", XN)
                ready(plan, turn, ("xT1", 0))
                ready(plan, turn, ("xT1", 1))
                logits(plan, turn, "lg", Wr0)
                if prev is not None:
                    list_ranks(plan, turn, prev)
                pe.wait_ge(sem("w1_loaded"), 16 * (len(w1loads) - len(W0)))
                for s, i in ffn_steps:
                    t, p = i, PAIR
                    if s == "up":
                        ps, b = fill(plan, turn, ("up", i))
                        for c in range(KC):
                            last = mm(ps[:, :], xT[:, c, t * P:(t + 1) * P], W13[:, c, p * 512:(p + 1) * 512], c == 0, c == KC - 1)
                        last.then_inc(bank_full[b], 1)
                    elif s == "hT":
                        ready(plan, turn, ("up", i))
                        ps, b = fill(plan, turn, ("hT", i))
                        for a in range(2):
                            last = pe.transpose(ps[:, a * P:(a + 1) * P], HB0[:, i % 3, a * P:(a + 1) * P], ident[:, :])
                        last.then_inc(bank_full[b], 1)
                    else:
                        ps, b = fill(plan, turn, ("acc", "y", t))
                        ready(plan, turn, ("hT", i))
                        for a in range(2):
                            last = mm(ps[:, 0:D], HT0[:, i % 3, a * P:(a + 1) * P], W2[:, 2 * p + a, :],
                                      a == 0, a == 1)
                        last.then_inc(bank_full[b], 1)

            def routed_start():
                pe.wait_ge(sem("choices_counted"), 1)
                ps, b = fill(jr0, 0, ("cnt",))
                mm(ps[:, 0:E], ones[:, :], SEL[:, 0, :]).then_inc(bank_full[b], 1)
                pe.wait_ge(sem("first_rows_spread"), 2)
                ps, b = fill(jr0, 0, ("gt",))
                for e in range(E):
                    for c in range(KC):
                        last = mm(ps[:, 0:256], XE[:, c, P * e:P * e + P], W13[:, c, 256 * e:256 * e + 256],
                                  e == 0 and c == 0, e == E - 1 and c == KC - 1)
                last.then_inc(bank_full[b], 1)
                ready(jr0, 0, ("gt",))

            def routed(g):
                pe.wait_ge(sem("pairs_built"), g + 1)
                ps, b = fill(jr, g, ("ow",))
                for t in range(T):
                    last = pe.transpose(ps[:, t * P:(t + 1) * P], OWS[:, t, :], ident[:, :])
                last.then_inc(bank_full[b], 1)
                ready(jr, g, ("ow",))
                for t in range(T):
                    ps, b = fill(jr, g, ("gu", t))
                    mm(ps[:, :], OWT[:, t, :], GT).then_inc(bank_full[b], 1)
                ps, b = fill(jr, g, ("hs",))
                for t in range(T):
                    ready(jr, g, ("gu", t))
                    for k in range(2):
                        last = mm(ps[:, 0:64], HR[:, 2 * t + k, :], OHS[:, 2 * t + k, :], t == 0 and k == 0, t == T - 1 and k == 1)
                last.then_inc(bank_full[b], 1)

            def routed_end():
                ready(jr, GROUPS - 1, ("hs",))
                ps, b = fill(jr1, 0, ("dn",))
                for e in range(E):
                    last = mm(ps[0:E, 0:D], HS[:, E * e:E * e + E], W2[:, e, :], e == 0, e == E - 1)
                last.then_inc(bank_full[b], 1)

            def experts(layer, turn, pair, steps, plan):
                hc = HIDS[layer] // P
                before = [pair + n for n in tiles_before[layer]]
                ybank = {}
                up = {u: WB[u][:, 0:KC * 2 * hc * P].rearrange("p (c n) -> p c n", c=KC) for u in range(2)}
                dn = {u: WB[u][:, KC * 2 * hc * P:KC * 2 * hc * P + hc * D].rearrange("p (c n) -> p c n", c=hc) for u in range(2)}
                for s in steps:
                    u = s[1]
                    if s[0] == "xsT":
                        pe.wait_ge(sem(f"rows_loaded{u}"), 16 * (before[u] + 1))
                        ps, b = fill(plan, turn, s)
                        for c in range(KC):
                            for h in range(2):
                                last = pe.transpose(ps[:, (2 * c + h) * P:(2 * c + h + 1) * P], XS[:, u, h, c * P:(c + 1) * P], ident[:, :])
                        last.then_inc(bank_full[b], 1)
                    elif s[0] == "up":
                        c = s[2]
                        if c == 0:
                            pe.wait_ge(sem(f"w_loaded{u}"), 16 * (before[u] + 1))
                            ready(plan, turn, ("xsT", u))
                        ps, b = fill(plan, turn, s)
                        for a in range(2):
                            for k in range(KC):
                                last = mm(ps[:, a * 256:(a + 1) * 256], up[u][:, k, (a * hc + c) * P:(a * hc + c + 1) * P],
                                          xsT[:, u, k, :], k == 0, k == KC - 1)
                        last.then_inc(bank_full[b], 1)
                    else:
                        c = s[2]
                        if c == 0:
                            ybank[u] = [fill(plan, turn, ("acc", "y", u, h)) for h in range(2)]
                        ready(plan, turn, ("up", u, c))
                        for h in range(2):
                            ps, b = ybank[u][h]
                            last = mm(ps[:, 0:D], HT[:, c, h * P:(h + 1) * P], dn[u][:, c, :], c == 0, c == hc - 1)
                            if c == hc - 1:
                                last.then_inc(bank_full[b], 1)

            def phase3(plan, turn, g, following, front_only=False):
                def turned(name, u, rows):
                    ps, b = fill(plan, turn, (name, u))
                    for c in range(KC):
                        for t in range(TS):
                            last = pe.transpose(ps[:, (c * TS + t) * P:(c * TS + t + 1) * P], rows[:, u * TS + t, c * P:(c + 1) * P], ident[:, :])
                    last.then_inc(bank_full[b], 1)
                    ready(plan, turn, (name, u))

                def project(name, u, w, src):
                    ps, b = fill(plan, turn, (name, u))
                    for m in range(KC):
                        for c in range(KC):
                            last = mm(ps[:, m * TS * P:(m + 1) * TS * P], w[:, c, m * P:(m + 1) * P], cols_of(src, u)[:, c, :], c == 0, c == KC - 1)
                    last.then_inc(bank_full[b], 1)

                def project_rows(name, u, w, src):
                    ps, b = fill(plan, turn, (name, u))
                    for t in range(TS):
                        for c in range(KC):
                            last = mm(ps[:, t * D:(t + 1) * D], cols_of(src, u)[:, c, t * P:(t + 1) * P], w[:, c, :], c == 0, c == KC - 1)
                    last.then_inc(bank_full[b], 1)

                def scores(name, u, q, k):
                    ps, b = fill(plan, turn, (name, u))
                    for t in range(TS):
                        for m in range(KC):
                            last = mm(ps[:, t * P:(t + 1) * P], cols_of(q, u)[:, m, t * P:(t + 1) * P], cols_of(k, u)[:, m, t * P:(t + 1) * P], m == 0, m == KC - 1)
                    last.then_inc(bank_full[b], 1)

                def attend(i, u, pname, oname, v):
                    pe.wait_ge(sem(f"probs_s{u}"), 3 * g + (i + 1))
                    ps, b = fill(plan, turn, (pname, u))
                    for t in range(TS):
                        last = pe.transpose(ps[:, t * P:(t + 1) * P], SC2[:, u * TS + t, :], ident[:, :])
                    last.then_inc(bank_full[b], 1)
                    ready(plan, turn, (pname, u))
                    ps, b = fill(plan, turn, (oname, u))
                    for t in range(TS):
                        last = mm(ps[:, t * D:(t + 1) * D], PT2[:, u * TS + t, :], v[:, u * TS + t, :])
                    last.then_inc(bank_full[b], 1)

                def turned_norm(i, name, u, rows):
                    pe.wait_ge(sem(f"normed_s{u}"), 5 * g + (i + 1))
                    turned(name, u, rows)

                streams = range(STREAMS)

                def front(g):
                    pe.wait_ge(sem("ctx_loaded"), 16 * (g + (GROUPS + 1)))
                    for u in streams:
                        turned("cT", u, CG)
                        project("k2", u, W3["k2"], cT)
                        project_rows("v2", u, W3["v2"], cT)

                def front_out():
                    for name in ("k2", "v2"):
                        for u in streams:
                            ready(plan, turn, (name, u))

                if front_only:
                    front(g)
                    front_out()
                    return
                for u in streams:
                    turned_norm(0, "xT4", u, N1)
                    project("q2", u, W3["q2"], xT)
                for u in streams:
                    ready(plan, turn, ("q2", u))
                    scores("s2", u, qT, kT)
                for u in streams:
                    project("k4", u, W3["k4"], cT)
                    project_rows("v4", u, W3["v4"], cT)
                for u in streams:
                    attend(0, u, "p2", "o2", V2)
                for u in streams:
                    ready(plan, turn, ("o2", u))
                    turned("oT2", u, AO)
                    project_rows("x2", u, W3["o2"], aT)
                pe.wait_ge(sem("weff_ready"), 2)
                for u in streams:
                    turned_norm(1, "xT5", u, XN)
                    project_rows("f2", u, WEFF, xT)
                for u in streams:
                    turned_norm(2, "xT6", u, IN3)
                    project("q3", u, W3["q3"], xT)
                    project("k3", u, W3["k3"], xT)
                for u in streams:
                    ready(plan, turn, ("k4", u))
                    ready(plan, turn, ("v4", u))
                    ready(plan, turn, ("q3", u))
                    ready(plan, turn, ("k3", u))
                    scores("s3", u, qT, kT)
                for u in streams:
                    project_rows("v3", u, W3["v3"], xT)
                for u in streams:
                    ready(plan, turn, ("v3", u))
                    attend(1, u, "p3", "o3", V3)
                for u in streams:
                    ready(plan, turn, ("o3", u))
                    turned("aT", u, AO)
                    project("q4", u, W3["q4"], aT)
                for u in streams:
                    ready(plan, turn, ("q4", u))
                    scores("s4", u, qT, k4T)
                for u in streams:
                    attend(2, u, "p4", "o4", V4)
                for u in streams:
                    turned_norm(3, "nT", u, N2)
                    project("h", u, W3["h"], xT)
                for u in streams:
                    pe.wait_ge(sem(f"leaky_s{u}"), g + 1)
                    project_rows("ff", u, W3["ff"], hT3)
                if following is not None:
                    front(following)
                for u in streams:
                    turned_norm(4, "xT7", u, XN)
                logits(plan, turn, "lg1", Wr[3])
                list_ranks(plan, turn, g + GROUPS)
                if following is not None:
                    front_out()

            pe.wait_ge(sem("masks_built"), 1)
            pe.wait_ge(sem("const_loaded"), 16 * len(consts))
            for m in range(KC):
                ps, b = fill(pre, 0, ("wab", m))
                mm(ps[:, 0:D], LORA_A[:, m * P:(m + 1) * P], LORA_B[:, :]).then_inc(bank_full[b], 1)
            pe.wait_ge(sem("w0_loaded"), 16 * len(W0))
            phase1(j1, 0, 0, None)
            with pe.Fori(0, GROUPS - 1) as n:
                phase1(jf, n, n + 1, n)
            routed_start()
            with pe.Fori(0, GROUPS) as g:
                routed(g)
            routed_end()
            layer1_logits(j2, 0, GROUPS - 1)
            list_ranks(j2, 0, GROUPS - 1)

            def all_experts(layer):
                with pe.Fori(0, LOOPS) as i:
                    experts(layer, i, i, *moe[layer][0])
                experts(layer, 0, LOOPS, *moe[layer][1])

            all_experts(1)
            pe.wait_ge(sem("w3_loaded"), 16 * len(w3loads))
            phase3(j3f, 0, 0, None, True)
            with pe.Fori(0, GROUPS - 1) as g:
                phase3(j3, g, g, g + 1)
            phase3(j3e, 0, GROUPS - 1, None)
            all_experts(3)

        @block.scalar
        def _(act):
            fulls = Waits(act)

            def full(plan, g, key):
                b = fulls.at_least(bank_full, plan, key, g, 1)
                return bank[b], b

            def copy_cols(plan, g, name, dst, bias=None):
                for m in range(KC):
                    ps, b = full(plan, g, (name, m))
                    if bias is None:
                        act.activation(dst[:, m, :], ps[:, :], ACT.Copy).then_inc(bank_empty[b], 1)
                    else:
                        act.activation(dst[:, m, :], ps[:, :], ACT.Identity, bias=col_bias[:, bias, m:m + 1]).then_inc(bank_empty[b], 1)

            def phase1(plan, turn, g, prev):
                copy_cols(plan, turn, "cT", cT)
                copy_cols(plan, turn, "kT", kT, CK0)
                copy_cols(plan, turn, "xT0", xT)
                copy_cols(plan, turn, "qT", qT, CQ0)
                if prev is not None:
                    exps16(prev)
                for n in range(UNITS + 2):
                    if n < UNITS:
                        u = n % SB
                        act.wait_ge(sem("maxima"), UNITS * g + (n + 1))
                        for h in range(8):
                            last = act.activation(SC[:, u, h, :], SC[:, u, h, :], ACT.Exp, bias=MX[:, 32 + 8 * u + h:33 + 8 * u + h])
                        last.then_inc(sem("probs"), 1)
                    if n >= 2:
                        i = n - 2
                        for j in range(2):
                            ps, b = full(plan, turn, ("p", i, j))
                            act.activation(PT[:, i % KB, 4 * j:4 * j + 4, :], ps[:, :].rearrange("p (h k) -> p h k", h=4), ACT.Copy).then_inc(bank_empty[b], 1)
                copy_cols(plan, turn, "aT", aT)
                if prev is not None:
                    copy_cols(plan, turn, "xT3", kT)
                copy_cols(plan, turn, "xT1", xT)
                if prev is not None:
                    router_exps(prev)
                b, n = job(plan, ("lg",), turn)
                act.wait_ge(bank_empty[b], n + 1)
                act.activation(small[:, 0, :], small[:, 0, :], ACT.Exp).then_inc(sem("logits_exp"), 1)
                for i in range(T + 2):
                    if i < T:
                        t, p = i, PAIR
                        ps, b = full(plan, turn, ("up", i))
                        for a in range(2):
                            last = act.activation(SG0[:, b, a * P:(a + 1) * P], ps[:, a * 256:a * 256 + P], ACT.Silu)
                        last.then_inc(sem("silu_rows"), 1)
                    if i >= 2:
                        ps, b = full(plan, turn, ("hT", i - 2))
                        act.activation(HT0[:, (i - 2) % 3, :], ps[:, 0:256], ACT.Copy).then_inc(bank_empty[b], 1)

            def routed(g):
                ps, b = full(jr, g, ("ow",))
                act.activation(OWT, ps[:, :].rearrange("p (t n) -> p t n", t=T), ACT.Copy).then_inc(bank_empty[b], 1)
                for t in range(T):
                    ps, b = full(jr, g, ("gu", t))
                    act.activation(SGR[:, t, :, :], ps[:, :].rearrange("p (k n) -> p k n", k=2)[:, :, 0:HID0], ACT.Silu).then_inc(sem("routed_silu"), 1)

            def exps16(g):
                act.wait_ge(sem("shifted16"), g + 1)
                act.activation(EXTRA[:, 1024:2048], EXTRA[:, 1024:2048], ACT.Exp).then_inc(sem("probs16"), 1)

            def router_exps(turn):
                act.wait_ge(sem("router_in"), 2 * turn + 1)
                act.activation(small[:, 1, :], small[:, 1, :], ACT.Exp).then_inc(sem("router_exp"), 1)
                act.wait_ge(sem("router_in"), 2 * turn + 2)
                act.activation(small[:, 8, 0:T], small[:, 8, 0:T], ACT.Exp).then_inc(sem("router_exp"), 1)

            def experts(layer, turn, pair, steps, plan):
                hc = HIDS[layer] // P
                for s in steps:
                    if s[0] == "up":
                        ps, b = full(plan, turn, s)
                        act.activation(SG[:, b, :], ps[:, 0:256], ACT.Silu).then_inc(sem("silu_slots"), 1)
                    elif s[0] == "down" and s[2] == hc - 1:
                        u = s[1]
                        ps, b = full(plan, turn, ("acc", "y", u, 0))
                        act.wait_ge(sem(f"result_free{u}"), pair + (PRIMED + tiles_before[layer][u]))
                        act.activation(YS[:, u, 0, :], ps[:, 0:D], ACT.Copy).then_inc(bank_empty[b], 1)

            def phase3(plan, turn, g, following, front_only=False):
                def copy(name, u, dst):
                    ps, b = full(plan, turn, (name, u))
                    act.activation(dst, per_chunk(ps), ACT.Copy).then_inc(bank_empty[b], 1)

                def biased(name, u, dst, bias):
                    ps, b = full(plan, turn, (name, u))
                    for m in range(KC):
                        last = act.activation(cols_of(dst, u)[:, m, :], per_chunk(ps)[:, m, :], ACT.Identity, bias=col_bias[:, bias, m:m + 1])
                    last.then_inc(bank_empty[b], 1)

                def exps(i, u):
                    act.wait_ge(sem(f"shifted_s{u}"), 3 * g + (i + 1))
                    act.activation(tiles(SC2, u), tiles(SC2, u), ACT.Exp).then_inc(sem(f"probs_s{u}"), 1)

                def turned_probs(name):
                    for u in streams:
                        ps, b = full(plan, turn, (name, u))
                        act.activation(tiles(PT2, u), per_tile(ps, P), ACT.Copy).then_inc(bank_empty[b], 1)

                streams = range(STREAMS)

                def front():
                    for u in streams:
                        copy("cT", u, cols_of(cT, u))
                        biased("k2", u, kT, CK2)

                if front_only:
                    front()
                    return
                for u in streams:
                    copy("xT4", u, cols_of(xT, u))
                    biased("q2", u, qT, CQ2)
                for u in streams:
                    copy("k4", u, cols_of(k4T, u))
                    exps(0, u)
                turned_probs("p2")
                for u in streams:
                    copy("oT2", u, cols_of(aT, u))
                for u in streams:
                    copy("xT5", u, cols_of(xT, u))
                for u in streams:
                    copy("xT6", u, cols_of(xT, u))
                    copy("q3", u, cols_of(qT, u))
                    copy("k3", u, cols_of(kT, u))
                for u in streams:
                    ps, b = full(plan, turn, ("v3", u))
                    act.activation(tiles(V3, u), per_tile(ps), ACT.Copy).then_inc(bank_empty[b], 1)
                    exps(1, u)
                turned_probs("p3")
                for u in streams:
                    copy("aT", u, cols_of(aT, u))
                    copy("q4", u, cols_of(qT, u))
                for u in streams:
                    exps(2, u)
                turned_probs("p4")
                for u in streams:
                    copy("nT", u, cols_of(xT, u))
                if following is not None:
                    front()
                for u in streams:
                    copy("xT7", u, cols_of(xT, u))
                router_exps(g + GROUPS)

            act.wait_ge(sem("const_loaded"), 16 * len(consts))
            phase1(j1, 0, 0, None)
            with act.Fori(0, GROUPS - 1) as n:
                phase1(jf, n, n + 1, n)
            with act.Fori(0, GROUPS) as g:
                routed(g)
            exps16(GROUPS - 1)
            copy_cols(j2, 0, "xT3", kT)
            router_exps(GROUPS - 1)

            def all_experts(layer):
                with act.Fori(0, LOOPS) as i:
                    experts(layer, i, i, *moe[layer][0])
                experts(layer, 0, LOOPS, *moe[layer][1])

            all_experts(1)
            phase3(j3f, 0, 0, None, True)
            with act.Fori(0, GROUPS - 1) as g:
                phase3(j3, g, g, g + 1)
            phase3(j3e, 0, GROUPS - 1, None)
            all_experts(3)

        @block.vector
        def _(dve):
            step = [0, 0, 0]
            turn_of = [0]

            def d(ins):
                ins.then_inc(sem("dve_step"), 1)
                step[2] += 1
                return ins

            def settle():
                dve.wait_ge(sem("dve_step"), turn_of[0] * step[1] + (step[0] + step[2]))

            def alone():
                dve.sem_inc(sem("dve_passed"), 1)

            def enter(turn, per):
                turn_of[0], step[1], step[2] = turn, per, 0

            def leave(turns):
                assert step[2] == step[1], f"steps of a turn: {step[2]}"
                step[0] += step[1] * turns
                turn_of[0], step[1], step[2] = 0, 0, 0

            fulls, empties = Waits(dve), Waits(dve)

            def full(plan, g, key):
                b = fulls.at_least(bank_full, plan, key, g, 1)
                return bank[b], b

            def evacuated(plan, g, key):
                empties.at_least(bank_empty, plan, key, g, 1)

            def tt(o, a, b, op):
                return dve.tensor_tensor(o, a, b, op)

            def norm_stats(src, eps, which=range(T), stream=""):
                lo, hi = which[0], which[-1] + 1
                for t in which:
                    d(dve.bn_stats(ST[:, t, :], src(t)))
                settle()
                alone()
                for t in which:
                    d(dve.bn_aggr(MV[:, t, :], ST[:, t, :]))
                settle()
                dve.tensor_scalar(VE[:, lo:hi], MV[:, lo:hi, 1], eps, None, ALU.add).then_inc(sem("variance" + stream), 1)

            def norm_apply(src, dst, count, last=None, which=range(T), stream=""):
                dve.wait_ge(sem("rstd" + stream), count)
                for t in which:
                    i = dve.tensor_scalar(dst(t), src(t), MV[:, t, 0:1], RS[:, t:t + 1], ALU.subtract, ALU.mult)
                    if t < which[-1] or last is None:
                        d(i)
                    else:
                        i.then_inc(sem(last + stream), 1)

            def norm(src, dst, eps, count, last=None, which=range(T), stream=""):
                norm_stats(src, eps, which, stream)
                norm_apply(src, dst, count, last, which, stream)

            def norm_both(src, dst, eps, count, last=None):
                for u in range(STREAMS):
                    norm_stats(src, eps, range(u * TS, (u + 1) * TS), f"_s{u}")
                for u in range(STREAMS):
                    norm_apply(src, dst, count, last, range(u * TS, (u + 1) * TS), f"_s{u}")

            def rank(v, n, lower, o):
                gt = cmpa[:, 0:T * n * n].rearrange("p (t i j) -> p t i j", t=T, i=n)
                eq = cmpb[:, 0:T * n * n].rearrange("p (t i j) -> p t i j", t=T, i=n)
                settle()
                d(tt(gt, rep(v, n, 2), bc(v, n), ALU.is_gt))
                d(tt(eq, rep(v, n, 2), bc(v, n), ALU.is_equal))
                settle()
                d(tt(eq, eq, rep(lower[:, :, :], T), ALU.mult))
                settle()
                d(tt(gt, gt, eq, ALU.add))
                settle()
                d(dve.tensor_reduce(o, gt, AX, ALU.add))
                settle()

            sm = lambda i, n=E: small[:, i, 0:T * n].rearrange("p (t e) -> p t e", t=T)

            def phase1(plan, turn, g, prev):
                norm(lambda t: xg(g, t), lambda t: XN[:, t, :], 1e-5, 2 * g + 1, "normed")
                def evac_v():
                    for t in range(T):
                        ps, b = full(plan, turn, ("v", t))
                        tt(V0[:, t, :, 0:HD], ps[:, 0:D].rearrange("p (h d) -> p h d", h=H),
                           row_bias[:, BV0, :].rearrange("p (h d) -> p h d", h=H), ALU.add).then_inc(bank_empty[b], 1)

                if prev is None:
                    evac_v()
                else:
                    layer1_scores(prev, evac_v)

                def evac_scores(i):
                    for j in range(2):
                        ps, b = full(plan, turn, ("s", i, j))
                        tt(SC[:, i % SB, 4 * j:4 * j + 4, :], ps[:, :].rearrange("p (h k) -> p h k", h=4),
                           rep(mask01[:, :], 4), ALU.mult).then_inc(bank_empty[b], 1)

                def maxima(i):
                    u = i % SB
                    if i % 2:
                        dve.wait_ge(sem("biased"), T * g + (i // 2 + 1))
                    else:
                        for j in range(2):
                            evacuated(plan, turn, ("s", i, j))
                        d(tt(SC[:, u, :, :], SC[:, u, :, :], SCORE_BIAS[:, 0:8, :], ALU.add))
                        settle()
                    m = MX[:, 8 * u:8 * u + 8]
                    d(dve.tensor_reduce(m, SC[:, u, :, :], AX, ALU.max))
                    settle()
                    dve.tensor_scalar(MX[:, 32 + 8 * u:40 + 8 * u], m, -1.0, None, ALU.mult).then_inc(sem("maxima"), 1)

                def norm_out(t):
                    ps, b = full(plan, turn, ("acc", "o", t))
                    o = ps[:, 0:H * VW].rearrange("p (h d) -> p h d", h=H)
                    r = RC[:, H * (t % 2):H * (t % 2) + H]
                    d(dve.reciprocal(r, o[:, :, HD]))
                    settle()
                    tt(AO[:, t, :].rearrange("p (h d) -> p h d", h=H), o[:, :, 0:HD], bc(r, HD), ALU.mult).then_inc(bank_empty[b], 1)

                early_tiles = range(T if prev is None else T - 2)
                for n in range(UNITS + 5):
                    if n < UNITS:
                        evac_scores(n)
                    if 1 <= n <= UNITS:
                        maxima(n - 1)
                    if n >= 6 and n % 2 == 0 and n // 2 - 3 < len(early_tiles):
                        norm_out(n // 2 - 3)
                if prev is not None:
                    layer1_values(prev, (lambda: norm_out(T - 2), lambda: norm_out(T - 1)))
                dve.wait_ge(sem("x_biased"), g + 1)
                for t in range(T):
                    ps, b = full(plan, turn, ("xo", t))
                    tt(xg(g, t), xg(g, t), ps[:, 0:D], ALU.add).then_inc(bank_empty[b], 1)
                for t in range(T):
                    evacuated(plan, turn, ("xo", t))
                alone()
                norm(lambda t: xg(g, t), lambda t: XN[:, t, :], 1e-5, 2 * g + 2, "normed")

                if prev is not None:
                    logits_out(plan, turn)
                    lists(plan, turn, prev, prev, True)
                dve.wait_ge(sem("x_loaded"), 16 * (GROUPS - 1))
                ps, b = full(plan, turn, ("lg",))
                l = ps[:, 0:T * E].rearrange("p (t e) -> p t e", t=T)
                d(dve.tensor_reduce(MX[:, 0:T], l, AX, ALU.max))
                settle()
                tt(sm(0), l, bc(MX[:, 0:T], E), ALU.subtract).then_inc(bank_empty[b], 1)
                dve.wait_ge(sem("logits_exp"), g + 1)
                d(dve.tensor_reduce(MX[:, T:2 * T], sm(0), AX, ALU.add))
                settle()
                d(dve.reciprocal(RC[:, 0:T], MX[:, T:2 * T]))
                settle()
                d(tt(sm(1), sm(0), bc(RC[:, 0:T], E), ALU.mult))
                settle()
                d(tt(sm(2), sm(1), rep(ebias[:, :], T), ALU.add))
                settle()
                d(dve.tensor_reduce(small[:, 3, 0:4 * T], small[:, 2, :].rearrange("p (a b) -> p a b", b=2), AX, ALU.add))
                rank(sm(3, 4), 4, lower4, small[:, 4, 0:4 * T].rearrange("p (t e) -> p t e", t=T))
                d(dve.tensor_scalar(small[:, 5, 0:4 * T], small[:, 4, 0:4 * T], 2.0, None, ALU.is_lt))
                settle()
                d(dve.tensor_scalar(small[:, 6, 0:4 * T], small[:, 5, 0:4 * T], 1e30, -1e30, ALU.mult, ALU.add))
                pairs = lambda i: small[:, i, :].rearrange("p (a b) -> p a b", b=2)
                d(tt(pairs(7), pairs(2), bc(small[:, 5, 0:4 * T], 2), ALU.mult))
                settle()
                d(tt(pairs(7), pairs(7), bc(small[:, 6, 0:4 * T], 2), ALU.add))
                rank(sm(7), E, lower8, RANK[:, :, :])
                for k in range(2):
                    d(dve.tensor_scalar(OH[:, :, k, :], RANK[:, :, :], float(k), None, ALU.is_equal))
                settle()
                d(dve.tensor_copy(SRC[:, ds(g * 2 * T * E, 2 * T * E)], OH[:, :, :, :].rearrange("p t k e -> p (t k e)")))
                d(tt(OHT[:, :, :, :], OH[:, :, :, :], rep(sm(1), 2, 2), ALU.mult))
                d(dve.tensor_copy(X8[:, ds(g * KC * E, KC * E)].rearrange("p (c s) -> p c s", c=KC), xT[:, :, 0:E]))
                settle()
                d(dve.tensor_reduce(WV[:, ds(g * 2 * T, 2 * T)], OHT[:, :, :, :].rearrange("p t k e -> p (t k) e"), AX, ALU.add))

                def add_y(t):
                    ps, b = full(plan, turn, ("acc", "y", t))
                    tt(xg(g, t), xg(g, t), ps[:, 0:D], ALU.add).then_inc(bank_empty[b], 1)

                for i in range(T):
                    ps, b = full(plan, turn, ("up", i))
                    dve.wait_ge(sem("silu_rows"), T * g + (i + 1))
                    pair = ps[:, :].rearrange("p (a n) -> p a n", a=2)
                    tt(HB0[:, i % 3, :].rearrange("p (a n) -> p a n", a=2), pair[:, :, P:2 * P],
                       SG0[:, b, :].rearrange("p (a n) -> p a n", a=2), ALU.mult).then_inc(bank_empty[b], 1)
                    if i > 0:
                        add_y(i - 1)
                add_y(T - 1)
                for t in reversed(range(T)):
                    evacuated(plan, turn, ("acc", "y", t))
                settle()

            def routed_start():
                flat3 = lambda ap: ap.rearrange("p (a e) -> p a e", e=E)
                d(dve.memset(XE, 0.0))
                d(dve.memset(HS, 0.0))
                d(dve.memset(GT, 0.0))
                d(dve.tensor_reduce(small[:, 0, 0:E], SRC[:, :].rearrange("p (a e) -> p e a", e=E), AX, ALU.add))
                settle()
                dve.tensor_copy(SEL[:, 0, :], small[:, 0, 0:E]).then_inc(sem("choices_counted"), 1)
                for half in range(2):
                    i = dve.tensor_copy(XE.rearrange("p c (e n) -> p c e n", n=DIAG)[:, :, :, E * E * half:E * E * half + E],
                                        rep(X8[:, (GROUPS - 1) * KC * E:GROUPS * KC * E].rearrange("p (c s) -> p c s", c=KC), E, 2))
                    i.then_inc(sem("first_rows_spread"), 1)
                ps, b = full(jr0, 0, ("cnt",))
                dve.tensor_copy(small[:, 1, 0:E], ps[:, 0:E]).then_inc(bank_empty[b], 1)
                evacuated(jr0, 0, ("cnt",))
                count, begin, end = small[:, 1, 0:E], small[:, 2, 0:E], small[:, 3, 0:E]
                before = cmpa[:, 0:E * E].rearrange("p (i j) -> p i j", i=E)
                d(tt(before, lower8[:, :, :], rep(count, E), ALU.mult))
                settle()
                d(dve.tensor_reduce(begin, before, AX, ALU.add))
                settle()
                d(tt(end, begin, count, ALU.add))
                place = bc(FLAT[:, :], E)
                d(tt(flat3(EO), place, rep(begin, 2 * TILES), ALU.is_ge))
                settle()
                d(tt(flat3(cmpb[:, :]), place, rep(end, 2 * TILES), ALU.is_lt))
                settle()
                d(tt(EO, EO, cmpb[:, :], ALU.mult))
                ps, b = full(jr0, 0, ("gt",))
                d(dve.tensor_copy(GT[0:64, 0:256], ps[0:64, 0:256]))
                dve.tensor_copy(GT[64:P, 256:512], ps[64:P, 0:256]).then_inc(bank_empty[b], 1)
                settle()

            def routed(g):
                eo = EO[:, ds(g * 2 * T * E, 2 * T * E)].rearrange("p (a e) -> p a e", e=E)
                src = SRC[:, ds(g * 2 * T * E, 2 * T * E)].rearrange("p (a e) -> p a e", e=E)
                d(tt(OHS.rearrange("p a (e s) -> p a e s", e=E), bc(eo, E), rep(src, E, 2), ALU.mult))
                settle()
                tt(OWS.rearrange("p t (k n) -> p (t k) n", k=2), OHS, bc(WV[:, ds(g * 2 * T, 2 * T)], E * E), ALU.mult).then_inc(sem("pairs_built"), 1)
                for t in range(T):
                    ps, b = full(jr, g, ("gu", t))
                    dve.wait_ge(sem("routed_silu"), T * g + (t + 1))
                    tt(HR[:, 2 * t:2 * t + 2, :], ps[:, :].rearrange("p (k n) -> p k n", k=2)[:, :, HID0:2 * HID0],
                       SGR[:, t, :, :], ALU.mult).then_inc(bank_empty[b], 1)
                ps, b = full(jr, g, ("hs",))
                tt(HS, HS, ps[:, 0:64], ALU.add).then_inc(bank_empty[b], 1)
                evacuated(jr, g, ("hs",))
                alone()

            def routed_end():
                ps, b = full(jr1, 0, ("dn",))
                tt(X[0:E, FIRST * D:(FIRST + 1) * D], X[0:E, FIRST * D:(FIRST + 1) * D], ps[0:E, 0:D], ALU.add).then_inc(bank_empty[b], 1)
                evacuated(jr1, 0, ("dn",))

            def layer1_scores(g, between=None):
                dve.wait_ge(sem("norm_rows_free"), g + PRIMED)
                alone()
                norm(lambda t: xg(g, t), lambda t: NA[:, t, :], 1e-5, 2 * g + 1, "normed", stream="_l1")
                d(dve.memset(S16, 0.0))
                settle()
                dve.wait_ge(sem("ctx2_loaded"), 16 * (g + 1))
                dve.wait_ge(sem("normed_l1"), 2 * g + 1)
                both(g, score_products, score_sum, 0, (between, None))
                dve.wait_ge(sem("products_used"), 4 * g + 2)
                settle()
                sv, sbv = EXTRA[:, 0:1024].rearrange("p (t n) -> p t n", t=T), EXTRA[:, 1024:2048].rearrange("p (t n) -> p t n", t=T)
                d(dve.scalar_tensor_tensor(sbv, sv, float(HD) ** -0.5, rep(causal16[:, :, :].rearrange("p h k -> p (h k)"), T), ALU.mult, ALU.add))
                settle()
                rows = EXTRA[:, 1024:2048].rearrange("p (a k) -> p a k", k=H)
                d(dve.tensor_reduce(MX16[:, :], rows, AX, ALU.max))
                settle()
                tt(rows, rows, bc(MX16[:, :], H), ALU.subtract).then_inc(sem("shifted16"), 1)

            def score_sum(t, k, part):
                return dve.tensor_reduce(S16[:, t, 4 * k:4 * k + 4, 0:PAIRBLK[k]], part.rearrange("p (h k d) -> p h k d", h=4, d=HD), AX, ALU.add)

            def value_sum(t, k, part):
                return dve.tensor_reduce(O16[:, t, 64 * k:64 * k + 64].rearrange("p (h d) -> p h d", h=4),
                                         part.rearrange("p (h d k) -> p h d k", h=4, d=HD), AX, ALU.add)

            def both(g, product, total, first, between):
                for i in range(2):
                    for k in range(4):
                        part = PRD[:, 0:4 * PAIRBLK[k] * HD]
                        d(product(tt, part, 2 * i + 1, k))
                        settle()
                        d(total(2 * i + 1, k, part))
                        settle()
                    if between[i] is not None:
                        between[i]()
                    dve.wait_ge(sem("products"), 4 * g + (first + i + 1))
                    for k in range(4):
                        last = total(2 * i, k, PR[k])
                        if k < 3:
                            d(last)
                    last.then_inc(sem("products_used"), 1)

            def layer1_values(g, between=(None, None)):
                rows = EXTRA[:, 1024:2048].rearrange("p (a k) -> p a k", k=H)
                dve.wait_ge(sem("probs16"), g + 1)
                d(dve.tensor_reduce(MX16[:, :], rows, AX, ALU.add))
                settle()
                d(dve.reciprocal(RC16[:, :], MX16[:, :]))
                both(g, value_products, value_sum, 2, between)
                dve.wait_ge(sem("products_used"), 4 * g + 4)
                settle()
                o = EXTRA[:, 2048:3072].rearrange("p (a d) -> p a d", d=HD)
                d(tt(o, o, bc(RC16[:, :], HD), ALU.mult))
                settle()
                d(tt(X[:, ds(g * T * D, T * D)], X[:, ds(g * T * D, T * D)], EXTRA[:, 2048:3072], ALU.add))
                settle()
                alone()
                norm(lambda t: xg(g, t), lambda t: NA[:, t, :], 1e-5, 2 * g + 2, "normed", stream="_l1")

            def logits_out(plan, turn):
                ps, b = full(plan, turn, ("lg1",))
                dve.tensor_copy(sm(2), ps[:, 0:T * E].rearrange("p (t e) -> p t e", t=T)).then_inc(bank_empty[b], 1)

            def lists(plan, plan_turn, g, turn, of_probs):
                evacuated(plan, plan_turn, ("lg1",))
                d(dve.tensor_reduce(MX[:, 0:T], sm(2), AX, ALU.max))
                settle()
                tt(sm(1), sm(2), bc(MX[:, 0:T], E), ALU.subtract).then_inc(sem("router_in"), 1)
                rank(sm(2), E, lower8, RANK[:, :, :])
                dve.tensor_scalar(SEL[:, :, :], RANK[:, :, :], 2.0, None, ALU.is_lt).then_inc(sem("selected"), 1)
                d(dve.tensor_scalar(OH[:, :, 0, :], RANK[:, :, :], 0.0, None, ALU.is_equal))
                d(dve.tensor_scalar(OH[:, :, 1, :], RANK[:, :, :], 1.0, None, ALU.is_equal))
                dve.wait_ge(sem("router_exp"), 2 * turn + 1)
                v = sm(2)
                if of_probs:
                    d(dve.tensor_reduce(MX[:, T:2 * T], sm(1), AX, ALU.add))
                    settle()
                    d(dve.reciprocal(RC[:, 0:T], MX[:, T:2 * T]))
                    settle()
                    d(tt(sm(3), sm(1), bc(RC[:, 0:T], E), ALU.mult))
                    v = sm(3)
                settle()
                d(tt(OHT[:, :, :, :], OH[:, :, :, :], rep(v, 2, 2), ALU.mult))
                settle()
                d(dve.tensor_reduce(sm(4, 2), OHT[:, :, :, :], AX, ALU.add))
                settle()
                two = sm(4, 2)
                tt(small[:, 8, 0:T], two[:, :, 1], two[:, :, 0], ALU.subtract).then_inc(sem("router_in"), 1)
                dve.wait_ge(sem("router_exp"), 2 * turn + 2)
                d(dve.tensor_scalar(small[:, 5, 0:T], small[:, 8, 0:T], 1.0, None, ALU.add))
                settle()
                d(dve.reciprocal(small[:, 6, 0:T], small[:, 5, 0:T]))
                settle()
                d(tt(small[:, 7, 0:T], small[:, 6, 0:T], small[:, 8, 0:T], ALU.mult))
                cw = CW[:, ds(g * 2 * T, 2 * T)].rearrange("p (t k) -> p t k", k=2)
                d(dve.tensor_copy(cw[:, :, 0], small[:, 6, 0:T]))
                settle()
                d(dve.tensor_copy(cw[:, :, 1], small[:, 7, 0:T]))
                ps, b = full(plan, plan_turn, ("rk",))
                d(tt(sm(10), ps[:, 0:T * E].rearrange("p (t e) -> p t e", t=T), rep(base[:, :], T), ALU.add))
                settle()
                tt(base[:, :], base[:, :], ps[:, T * E:(T + 1) * E], ALU.add).then_inc(bank_empty[b], 1)
                d(tt(sm(11), sm(10), rep(region0[:, :], T), ALU.add))
                settle()
                d(tt(OHT[:, :, :, :], OH[:, :, :, :], rep(sm(11), 2, 2), ALU.mult))
                settle()
                d(dve.tensor_reduce(sm(12, 2), OHT[:, :, :, :], AX, ALU.add))
                settle()
                d(dve.tensor_copy(IDX[:, ds(g * 2 * T, 2 * T)], small[:, 12, 0:2 * T]))
                dve.tensor_copy(IDXG[:, :], small[:, 12, 0:2 * T]).then_inc(sem("slots_found"), 1)
                evacuated(plan, plan_turn, ("rk",))
                settle()

            def plan_tiles():
                J = MOE_TILES
                w = lambda i: wide[0:1, i, :].rearrange("p (j e) -> p j e", e=E)
                r = lambda i: t8[0:1, i, :]
                d(dve.tensor_scalar(r(0), base[0:1, :], float(SLOT - 1), None, ALU.add))
                settle()
                d(dve.tensor_copy(lens_i[0:1, :], r(0)))
                settle()
                d(dve.tensor_scalar(lens_i[0:1, :], lens_i[0:1, :], SLOT.bit_length() - 1, None, ALU.logical_shift_right))
                settle()
                d(dve.tensor_copy(r(1), lens_i[0:1, :]))
                settle()
                d(dve.tensor_copy(r(2), r(1)))
                for e in range(1, E):
                    settle()
                    d(tt(t8[0:1, 2, e:e + 1], t8[0:1, 2, e - 1:e], t8[0:1, 1, e:e + 1], ALU.add))
                settle()
                d(tt(r(3), r(2), r(1), ALU.subtract))
                j = jrow[0:1, :].rearrange("p (j e) -> p j e", e=E)
                d(tt(w(0), j, rep(r(2), J), ALU.is_ge))
                settle()
                d(tt(w(1), j, rep(r(3), J), ALU.is_ge))
                d(tt(w(2), j, rep(r(3), J), ALU.subtract))
                settle()
                d(tt(w(1), w(1), w(0), ALU.subtract))
                d(tt(w(2), w(2), rep(r(5), J), ALU.add))
                settle()
                d(tt(w(2), w(2), w(1), ALU.mult))
                d(dve.tensor_reduce(wide[0:1, 3, 0:J], w(0), AX, ALU.add))
                settle()
                d(dve.tensor_reduce(wide[0:1, 4, 0:J], w(2), AX, ALU.add))
                d(dve.tensor_scalar(wide[0:1, 3, 0:J], wide[0:1, 3, 0:J], float(E - 1), None, ALU.min))
                settle()
                d(dve.scalar_tensor_tensor(wide[0:1, 5, 0:J], w(0)[:, :, E - 1], float(SPARE), wide[0:1, 4, 0:J], ALU.mult, ALU.add))
                d(dve.tensor_copy(tile_e[0:1, :], wide[0:1, 3, 0:J]))
                settle()
                dve.tensor_copy(tile_r[0:1, :], wide[0:1, 5, 0:J]).then_inc(sem("tiles_planned"), 1)
                d(dve.memset(base[:, :], 0.0))
                settle()

            def experts(layer, turn, pair, steps, plan):
                hc = HIDS[layer] // P
                first = 0 if layer == 1 else MOE_TILES * (HIDS[1] // P)
                n = 0
                for s in steps:
                    if s[0] == "xsT":
                        ps, b = full(plan, turn, s)
                        dve.tensor_copy(xsT[:, s[1], :, :], ps[:, :].rearrange("p (c n) -> p c n", c=KC)).then_inc(bank_empty[b], 1)
                    elif s[0] == "up":
                        _, u, c = s
                        n += 1
                        ps, b = full(plan, turn, s)
                        dve.wait_ge(sem("silu_slots"), pair * (2 * hc) + (first + n))
                        tt(HT[:, c, :], ps[:, 256:512], SG[:, b, :], ALU.mult).then_inc(bank_empty[b], 1)
                    elif s[2] == hc - 1:
                        u = s[1]
                        ps, b = full(plan, turn, ("acc", "y", u, 1))
                        dve.wait_ge(sem(f"result_free{u}"), pair + (PRIMED + tiles_before[layer][u]))
                        dve.tensor_copy(YS[:, u, 1, :], ps[:, 0:D]).then_inc(bank_empty[b], 1)

            def all_experts(layer):
                with dve.Fori(0, LOOPS) as i:
                    experts(layer, i, i, *moe[layer][0])
                experts(layer, 0, LOOPS, *moe[layer][1])

            def combine(g, turn, u=0):
                d(dve.tensor_copy(CWP[:, :], CW[:, ds(g * 2 * T, 2 * T)]))
                dve.wait_ge(sem(f"rows_gathered{u}"), 16 * 2 * T * (turn + 1))
                settle()
                for t in range(T):
                    d(dve.scalar_tensor_tensor(xg(g, t), YA[u][:, 2 * t, :], CWP[:, 2 * t:2 * t + 1], xg(g, t), ALU.mult, ALU.add))
                settle()

            def phase3(plan, turn, g, following, front_only=False):
                streams = range(STREAMS)
                xrows, xn = (lambda t: xg(g, t)), (lambda t: XN[:, t, :])

                def norm_s(u, i, src, dst, eps, last=None):
                    norm(src, dst, eps, 7 * g + i, last, range(u * TS, (u + 1) * TS), f"_s{u}")

                def shift(u):
                    sc = tiles(SC2, u)
                    d(dve.tensor_reduce(MX[:, TS * u:TS * (u + 1)], sc, AX, ALU.max))
                    settle()
                    tt(sc, sc, bc(MX[:, TS * u:TS * (u + 1)], P), ALU.subtract).then_inc(sem(f"shifted_s{u}"), 1)

                def sum_probs(u, i):
                    dve.wait_ge(sem(f"probs_s{u}"), 3 * g + (i + 1))
                    d(dve.tensor_reduce(MX[:, T + TS * u:T + TS * (u + 1)], tiles(SC2, u), AX, ALU.add))
                    settle()
                    d(dve.reciprocal(RC[:, TS * u:TS * (u + 1)], MX[:, T + TS * u:T + TS * (u + 1)]))
                    settle()

                def weighted(u, name, dst):
                    ps, b = full(plan, turn, (name, u))
                    tt(tiles(dst, u), per_tile(ps), bc(RC[:, TS * u:TS * (u + 1)], D), ALU.mult).then_inc(bank_empty[b], 1)

                def add_to_x(u, name, n):
                    dve.wait_ge(sem(f"x_biased_s{u}"), 2 * g + n)
                    ps, b = full(plan, turn, (name, u))
                    tt(xstream(g, u), xstream(g, u), ps[:, :], ALU.add).then_inc(bank_empty[b], 1)
                    evacuated(plan, turn, (name, u))
                    alone()

                def front(g):
                    combine(g, g)
                    for t in range(T):
                        i = dve.scalar_tensor_tensor(xg(g, t), YA[0][:, 2 * t + 1, :], CWP[:, 2 * t + 1:2 * t + 2], xg(g, t), ALU.mult, ALU.add)
                        i.then_inc(sem("combined"), 1)
                    dve.wait_ge(sem("combined"), T * (g + 1))
                    alone()
                    norm_both(lambda t: xg(g, t), lambda t: N1[:, t, :], 1e-5, 7 * g + 1, "normed")

                def values_out():
                    for u in streams:
                        ps, b = full(plan, turn, ("v2", u))
                        tt(tiles(V2, u), per_tile(ps), rep(row_bias[:, BV2, :], TS), ALU.add).then_inc(bank_empty[b], 1)

                if front_only:
                    front(g)
                    values_out()
                    return
                d(dve.tensor_copy(KM, keymask8[:, ds(g * (T * P // 4), T * P // 4)].bitcast(U8)))
                settle()
                d(dve.tensor_scalar(NBG[:, :], KM, 1e9, -1e9, ALU.mult, ALU.add))
                settle()
                for u in streams:
                    ps, b = full(plan, turn, ("s2", u))
                    km = KM[:, u * TS * P:(u + 1) * TS * P]
                    half = BIG[:, TS * P * u:TS * P * (u + 1)]
                    dve.scalar_tensor_tensor(half, ps[:, 0:TS * P], float(D) ** -0.5, km, ALU.mult, ALU.mult).then_inc(bank_empty[b], 1)
                    evacuated(plan, turn, ("s2", u))
                    d(tt(half, half, NBG[:, TS * P * u:TS * P * (u + 1)], ALU.add))
                    settle()
                    shift(u)
                for u in streams:
                    ps, b = full(plan, turn, ("v4", u))
                    dve.tensor_copy(tiles(V4, u), per_tile(ps)).then_inc(bank_empty[b], 1)
                    sum_probs(u, 0)
                for u in streams:
                    weighted(u, "o2", AO)
                dve.wait_ge(sem("norm_rows_free"), g + (PRIMED + GROUPS))
                for u in streams:
                    add_to_x(u, "x2", 1)
                    norm_s(u, 2, xrows, xn, 1e-5, "normed")
                for u in streams:
                    add_to_x(u, "f2", 2)
                    norm_s(u, 3, xrows, lambda t: IN3[:, t, :], 1e-5, "normed")
                for u in streams:
                    ps, b = full(plan, turn, ("s3", u))
                    dve.scalar_tensor_tensor(tiles(SC2, u), per_tile(ps, P), float(P) ** -0.5, rep(causal[:, :], TS), ALU.mult, ALU.add).then_inc(bank_empty[b], 1)
                    evacuated(plan, turn, ("s3", u))
                    shift(u)
                for u in streams:
                    sum_probs(u, 1)
                r3 = lambda t: R3[:, t, :]
                for u in streams:
                    weighted(u, "o3", AO)
                for u in streams:
                    evacuated(plan, turn, ("o3", u))
                    d(tt(tiles(R3, u), tiles(AO, u), tiles(IN3, u), ALU.add))
                    settle()
                    norm_s(u, 4, r3, lambda t: N1[:, t, :], 1e-3, "n1_raw")
                for u in streams:
                    ps, b = full(plan, turn, ("s4", u))
                    dve.tensor_scalar(tiles(SC2, u), per_tile(ps, P), float(P) ** -0.5, None, ALU.mult).then_inc(bank_empty[b], 1)
                    evacuated(plan, turn, ("s4", u))
                    shift(u)
                for u in streams:
                    sum_probs(u, 2)
                for u in streams:
                    weighted(u, "o4", R3)
                    evacuated(plan, turn, ("o4", u))
                    dve.wait_ge(sem(f"n1_ready_s{u}"), g + 1)
                    d(tt(tiles(R3, u), tiles(R3, u), tiles(N1, u), ALU.add))
                    settle()
                    norm_s(u, 5, r3, lambda t: N2[:, t, :], 1e-3)
                    settle()
                    d(tt(tiles(N2, u), tiles(N2, u), rep(row_bias[:, GAM, :], TS), ALU.mult))
                    settle()
                    tt(tiles(N2, u), tiles(N2, u), rep(row_bias[:, BET, :], TS), ALU.add).then_inc(sem(f"normed_s{u}"), 1)
                for u in streams:
                    ps, b = full(plan, turn, ("h", u))
                    tt(cols_of(hTt, u), per_chunk(ps), bc(col_bias[:, CB1, :], TS * P), ALU.add).then_inc(bank_empty[b], 1)
                    evacuated(plan, turn, ("h", u))
                    dve.scalar_tensor_tensor(cols_of(hT3, u), cols_of(hTt, u), 0.2, cols_of(hTt, u), ALU.mult, ALU.max).then_inc(sem(f"leaky_s{u}"), 1)
                for u in streams:
                    dve.wait_ge(sem(f"n2_biased_s{u}"), g + 1)
                    ps, b = full(plan, turn, ("ff", u))
                    tt(tiles(R3, u), per_tile(ps), tiles(N2B, u), ALU.add).then_inc(bank_empty[b], 1)
                    evacuated(plan, turn, ("ff", u))
                norm_both(r3, lambda t: N1[:, t, :], 1e-3, 7 * g + 6)
                settle()
                for u in streams:
                    d(tt(tiles(N1, u), tiles(N1, u), rep(row_bias[:, GAM, :], TS), ALU.mult))
                settle()
                for u in streams:
                    d(tt(tiles(N1, u), tiles(N1, u), rep(row_bias[:, BET, :], TS), ALU.add))
                settle()
                for u in streams:
                    flat = N1.rearrange("p t n -> p (t n)")[:, u * TS * D:(u + 1) * TS * D]
                    d(dve.scalar_tensor_tensor(xstream(g, u), flat, 0.0, xstream(g, u), ALU.max, ALU.add))
                settle()
                alone()
                norm_both(xrows, xn, 1e-5, 7 * g + 7, "normed")
                if following is not None:
                    values_out()
                    front(following)
                logits_out(plan, turn)
                lists(plan, turn, g, g + GROUPS, False)

            def quantized_weight():
                d(dve.tensor_reduce(MX[:, 0:1], KER, mybir.AxisListType.XY, ALU.max, apply_absolute_value=True))
                settle()
                dve.tensor_copy(MX[:, 1:2], MX[:, 0:1]).then_inc(sem("absmax"), 1)
                dve.wait_ge(sem("absmax_all"), 1)
                d(dve.tensor_scalar(MX[:, 4:5], MX[:, 2:3], 1.0 / 7.0, None, ALU.mult))
                settle()
                d(dve.reciprocal(MX[:, 3:4], MX[:, 4:5]))
                settle()
                q = QTMP
                d(dve.tensor_scalar(q, KER, MX[:, 3:4], None, ALU.mult))
                settle()
                half = 1.5 * 2.0 ** 23
                d(dve.tensor_scalar(q, q, half, -half, ALU.add, ALU.add))
                settle()
                d(dve.tensor_scalar(q, q, -8.0, 7.0, ALU.max, ALU.min))
                settle()
                for m in range(KC):
                    dve.scalar_tensor_tensor(WEFF[:, m, :], q[:, m, :], MX[:, 4:5], LAB[:, m, :], ALU.mult, ALU.add).then_inc(sem("weff_ready"), 1)

            dve.wait_ge(sem("const_loaded"), 16 * len(consts))
            dve.wait_ge(sem("masks_built"), 1)
            d(dve.tensor_copy(mask01[:, :], maski[:, :]))
            settle()
            d(dve.tensor_scalar(mask01[:, :], mask01[:, :], 0.0, None, ALU.not_equal))
            d(dve.tensor_scalar(DIST, DIST, 0.0, None, ALU.max))
            settle()
            d(tt(DIST, DIST, mask01[:, :], ALU.mult))
            d(dve.tensor_scalar(NEG, mask01[:, :], 1e9, -1e9, ALU.mult, ALU.add))
            settle()
            for h in range(H):
                i = dve.scalar_tensor_tensor(SCORE_BIAS[:, h, :], DIST, -(0.5 ** (h + 1)), NEG, ALU.mult, ALU.add)
                if h < H - 1:
                    d(i)
            i.then_inc(sem("score_bias_ready"), 1)
            for m in range(KC):
                ps, b = full(pre, 0, ("wab", m))
                dve.tensor_copy(LAB[:, m, :], ps[:, 0:D]).then_inc(bank_empty[b], 1)
            step[0], step[2] = step[2], 0
            dve.wait_ge(sem("x0_loaded"), 16)

            def straight(body):
                step[1] = 0
                body()
                step[0], step[2] = step[0] + step[2], 0

            straight(lambda: phase1(j1, 0, 0, None))
            with dve.Fori(0, GROUPS - 1) as n:
                enter(n, STEPS["phase1"])
                phase1(jf, n, n + 1, n)
            leave(GROUPS - 1)
            straight(routed_start)
            with dve.Fori(0, GROUPS) as g:
                enter(g, STEPS["routed"])
                routed(g)
            leave(GROUPS)
            routed_end()

            def last_layer1():
                layer1_scores(GROUPS - 1)
                layer1_values(GROUPS - 1)
                logits_out(j2, 0)
                lists(j2, 0, GROUPS - 1, GROUPS - 1, True)

            straight(last_layer1)
            straight(plan_tiles)
            all_experts(1)
            dve.wait_ge(sem("w3_loaded"), 16 * len(w3loads))
            straight(quantized_weight)
            straight(lambda: phase3(j3f, 0, 0, None, True))
            with dve.Fori(0, GROUPS - 1) as g:
                enter(g, STEPS["phase3"])
                phase3(j3, g, g, g + 1)
            leave(GROUPS - 1)
            straight(lambda: phase3(j3e, 0, GROUPS - 1, None))
            straight(plan_tiles)
            all_experts(3)
            with dve.Fori(0, GROUPS // 2) as i:
                enter(i, STEPS["last"])
                for u in range(2):
                    g = 2 * i + u
                    dve.wait_ge(sem("x_final"), g + PRIMED)
                    alone()
                    combine(g, i + (0 if u else GROUPS), u)
                    for t in range(T):
                        last = dve.scalar_tensor_tensor(xg(g, t), YA[u][:, 2 * t + 1, :], CWP[:, 2 * t + 1:2 * t + 2], xg(g, t), ALU.mult, ALU.add)
                        if t < T - 1:
                            d(last)
                    last.then_inc(sem("x_final"), 1)
            leave(GROUPS // 2)

        @block.gpsimd
        def _(pool):
            def alone():
                pool.sem_inc(sem("pool_passed"), 1)

            def power(count, stream=""):
                pool.wait_ge(sem("variance" + stream), count)
                pool.tensor_tensor(RS[:, :], VE[:, :], neg_half[:, :], ALU.pow).then_inc(sem("rstd" + stream), 1)

            def powers(count):
                for u in range(STREAMS):
                    part = slice(u * TS, (u + 1) * TS)
                    pool.wait_ge(sem(f"variance_s{u}"), count)
                    pool.tensor_tensor(RS[:, part], VE[:, part], neg_half[:, part], ALU.pow).then_inc(sem(f"rstd_s{u}"), 1)

            def x_bias(g):
                pool.wait_ge(sem("normed"), 2 * g + 1)
                alone()
                xx = xgroup(g)
                pool.tensor_tensor(xx, xx, rep(row_bias[:, BO0, :], T), ALU.add).then_inc(sem("x_biased"), 1)

            def x_bias_streams(g, normed, which):
                for u in range(STREAMS):
                    pool.wait_ge(sem(f"normed_s{u}"), normed)
                    alone()
                    xx = xstream(g, u).rearrange("p (t n) -> p t n", t=TS)
                    pool.tensor_tensor(xx, xx, rep(row_bias[:, which, :], TS), ALU.add).then_inc(sem(f"x_biased_s{u}"), 1)

            def scatter(turn, rows):
                pool.wait_ge(sem("slots_found"), turn + 1)
                alone()
                for t in range(T):
                    for k in range(2):
                        pool.indirect_dma_start(out=xs_dram, out_offset=bass.IndirectOffsetOnAxis(ap=IDXG[:, 2 * t + k:2 * t + k + 1], axis=0),
                                                in_=rows[:, t, :], in_offset=None).then_inc(sem("rows_sent"), 16)

            def gather(g, turn, u=0):
                pool.tensor_copy(IDXP[:, u, :], IDX[:, ds(g * 2 * T, 2 * T)]).then_inc(sem("gather_index"), 1)
                pool.wait_ge(sem("gather_index"), turn + 1)
                alone()
                for t in range(T):
                    for k in range(2):
                        pool.indirect_dma_start(out=YA[u][:, 2 * t + k, :], out_offset=None, in_=ys_dram,
                                                in_offset=bass.IndirectOffsetOnAxis(ap=IDXP[:, u, 2 * t + k:2 * t + k + 1], axis=0)).then_inc(sem(f"rows_gathered{u}"), 16)

            def phase1(plan, turn, g, prev):
                power(2 * g + 1)
                if prev is not None:
                    power(2 * prev + 1, "_l1")
                    pool.wait_ge(sem("normed_l1"), 2 * prev + 1)
                    pool.wait_ge(sem("ctx2_loaded"), 16 * (prev + 1))
                    products(prev, 0)

                def spread(i):
                    t, m = i // 2, i % 2
                    b, n = job(plan, ("kT", m), turn)
                    if t == 0:
                        pool.wait_ge(bank_empty[b], n + 1)
                    if i >= KB:
                        b, n = job(plan, ("s", i - KB, 1), turn)
                        pool.wait_ge(bank_full[b], n + 1)
                    pool.tensor_tensor(Kb[:, i % KB, :, :], rep(kT[:, m, t * P:(t + 1) * P], 8), bc(head_of[:, :], P), ALU.mult).then_inc(sem("k_heads"), 1)

                def bias(i):
                    for j in range(2):
                        b, n = job(plan, ("s", i, j), turn)
                        pool.wait_ge(bank_empty[b], n + 1)
                    pool.tensor_tensor(SC[:, i % SB, :, :], SC[:, i % SB, :, :], SCORE_BIAS[:, 8:16, :], ALU.add).then_inc(sem("biased"), 1)

                for i in range(KB):
                    spread(i)
                if prev is not None:
                    products(prev, 1)
                x_bias(g)
                for i in range(UNITS):
                    if i % 2:
                        bias(i)
                    if i + KB < UNITS:
                        spread(i + KB)
                if prev is not None:
                    products(prev, 2)
                    products(prev, 3)
                    power(2 * prev + 2, "_l1")
                power(2 * g + 2)
                if prev is not None:
                    scatter(prev, NA)

            def products(g, n):
                if n == 2:
                    pool.wait_ge(sem("probs16"), g + 1)
                if n >= 1:
                    pool.wait_ge(sem("products_used"), 4 * g + n)
                for k in range(4):
                    last = (score_products if n < 2 else value_products)(pool.tensor_tensor, PR[k], 2 * (n % 2), k)
                last.then_inc(sem("products"), 1)

            def layer1(g):
                power(2 * g + 1, "_l1")
                pool.wait_ge(sem("normed_l1"), 2 * g + 1)
                pool.wait_ge(sem("ctx2_loaded"), 16 * (g + 1))
                for n in range(4):
                    products(g, n)
                power(2 * g + 2, "_l1")
                scatter(g, NA)

            def phase3(plan, turn, g, following, front_only=False):
                def front(g):
                    powers(7 * g + 1)
                    x_bias_streams(g, 5 * g + 1, BO2)

                if front_only:
                    front(g)
                    return
                if following is not None:
                    pool.wait_ge(sem("combined"), T * (g + 1))
                    gather(following, g + 1)
                powers(7 * g + 2)
                x_bias_streams(g, 5 * g + 2, BF2)
                powers(7 * g + 3)
                powers(7 * g + 4)
                for u in range(STREAMS):
                    n1 = tiles(N1, u)
                    pool.wait_ge(sem(f"n1_raw_s{u}"), g + 1)
                    pool.tensor_tensor(n1, n1, rep(row_bias[:, GAM, :], TS), ALU.mult).then_inc(sem("n1_scaled"), 1)
                    pool.wait_ge(sem("n1_scaled"), 2 * g + (u + 1))
                    pool.tensor_tensor(n1, n1, rep(row_bias[:, BET, :], TS), ALU.add).then_inc(sem(f"n1_ready_s{u}"), 1)
                powers(7 * g + 5)
                for u in range(STREAMS):
                    pool.wait_ge(sem(f"normed_s{u}"), 5 * g + 4)
                    pool.tensor_tensor(tiles(N2B, u), tiles(N2, u), rep(row_bias[:, BB2, :], TS), ALU.add).then_inc(sem(f"n2_biased_s{u}"), 1)
                powers(7 * g + 6)
                powers(7 * g + 7)
                if following is not None:
                    front(following)
                scatter(g + GROUPS, XN)

            c = sem("pool_const")
            cn = [0]

            def k(ins):
                ins.then_inc(c, 1)
                cn[0] += 1

            def kwait():
                pool.wait_ge(c, cn[0])

            for b in range(8):
                pool.sem_inc(bank_full[b], 1)
                pool.sem_inc(bank_empty[b], 1)
            for n in PRIMED_SEMS:
                pool.sem_inc(sem(n), PRIMED)
            pool.memset(ZERO[:, :], 0.0).then_inc(sem("zero_set"), 1)
            k(pool.memset(ident[:, :], 0.0))
            k(pool.memset(tri[:, :], 1.0))
            k(pool.memset(ones[:, :], 1.0))
            k(pool.memset(neg_half[:, :], -0.5))
            k(pool.memset(lower8[:, :, :], 1.0))
            k(pool.memset(lower4[:, :, :], 1.0))
            k(pool.memset(head_of[:, :], 1.0))
            k(pool.memset(causal[:, :], 0.0))
            k(pool.memset(causal16[:, :, :], 0.0))
            k(pool.memset(V0[:, :, :, :], 1.0))
            k(pool.memset(base[:, :], 0.0))
            for e in range(E):
                k(pool.memset(region0[:, e:e + 1], float(e * CAP)))
                k(pool.memset(t8[0:1, 5, e:e + 1], float(e * REGION)))
            k(pool.iota(jrow_i[0:1, :], [[1, MOE_TILES], [0, E]], base=0, channel_multiplier=0))
            k(pool.iota(flat_i[:, 0:2 * FIRST], [[2 * P, FIRST], [1, 2]], base=2 * P * T, channel_multiplier=2))
            k(pool.iota(flat_i[:, 2 * FIRST:2 * TILES], [[2 * P, T], [1, 2]], base=0, channel_multiplier=2))
            k(pool.iota(dist_i, [[-1, P]], base=0, channel_multiplier=1))
            kwait()
            sel = lambda o, pat, b, cm, fill, op=ALU.is_ge: k(pool.affine_select(out=o, in_=o, pattern=pat, compare_op=op, fill=fill, base=b, channel_multiplier=cm))
            sel(ident[:, :], [[-1, P]], 0, 1, 1.0, ALU.not_equal)
            sel(tri[:, :], [[1, P]], -1, -1, 0.0)
            sel(lower8[:, :, :], [[1, E], [-1, E]], -1, 0, 0.0)
            sel(lower4[:, :, :], [[1, 4], [-1, 4]], -1, 0, 0.0)
            sel(head_of[:, :], [[-HD, 8]], 0, 1, 0.0)
            sel(causal[:, :], [[-1, P]], 0, 1, -1e30)
            sel(causal16[:, :, :], [[1, H], [-1, H]], 0, 0, -1e30)
            k(pool.tensor_copy(jrow[0:1, :], jrow_i[0:1, :]))
            k(pool.tensor_copy(DIST, dist_i))
            k(pool.tensor_copy(FLAT[:, :], flat_i))
            kwait()
            pool.affine_select(out=head_of[:, :], in_=head_of[:, :], pattern=[[HD, 8]], compare_op=ALU.is_ge, fill=0.0,
                               base=HD - 1, channel_multiplier=-1).then_inc(sem("masks_built"), 1)
            pool.wait_ge(sem("masks_built"), 1)
            pool.wait_ge(sem("score_bias_ready"), 1)
            phase1(j1, 0, 0, None)
            pool.wait_ge(sem("lists_zeroed"), 16 * zrows.shape[0])
            with pool.Fori(0, GROUPS - 1) as n:
                phase1(jf, n, n + 1, n)
            layer1(GROUPS - 1)
            pool.wait_ge(sem("absmax"), 1)
            pool.partition_all_reduce(MX[:, 2:3], MX[:, 1:2], P, RMAX).then_inc(sem("absmax_all"), 1)
            for u in range(2):
                pool.wait_ge(sem(f"y_stored{u}"), 16 * (LOOPS + 1 - u))
            gather(0, 0)
            phase3(j3f, 0, 0, None, True)
            with pool.Fori(0, GROUPS - 1) as g:
                phase3(j3, g, g, g + 1)
            phase3(j3e, 0, GROUPS - 1, None)
            for u in range(2):
                pool.wait_ge(sem(f"y_stored{u}"), 32 * (LOOPS + 1 - u))
            with pool.Fori(0, GROUPS // 2) as i:
                for u in range(2):
                    pool.wait_ge(sem("x_final"), 2 * i + (PRIMED + u - 1))
                    gather(2 * i + u, 2 * i + (GROUPS + u), u)


_OUT_SHAPE = (TILES, P, D)


def kernel(**inputs):
    import numpy as np
    import concourse.bacc as bacc
    from concourse.bass_utils import run_bass_kernel_spmd

    A = {k: np.asarray(v) for k, v in inputs.items()}
    kc = lambda w: np.ascontiguousarray(w.reshape(w.shape[0] // P, P, w.shape[1]).transpose(1, 0, 2))
    L0, L1, L2, L3 = "L0_xattn_", "L1_ffn_", "L2_xattn_", "L3_xattn_"
    arrays = {
        "x": np.roll(A["x"], -T, axis=0), "ctx": np.roll(A["ctx_1024"], -T, axis=0), "mask_qk": A["mask_1x1xSxS2_ik0"].reshape(P, P),
        "mask_bk": np.roll(A["mask_BxS2_bk0"], -T, axis=0).reshape(-1),
        "ebias": A["L0_ffn_expert_bias"],
        "wr0": kc(A["L0_ffn_w_gate"].T), "wr1": kc(A["L1_ffn_router_kernel_DE"]), "wr3": kc(A["L3_ffn_gate_w"].T),
        "lora_a": A["L2_ffn_a"].T, "lora_b": A["L2_ffn_b"], "kernel": kc(A["L2_ffn_kernel"]),
        "row_bias": np.concatenate([A[L0 + "wv_b"], A[L0 + "out_b"], A[L2 + "bv"], A[L2 + "bo"], A["L2_ffn_bias"],
                                    A[L3 + "gamma"], A[L3 + "beta"], A[L3 + "b2"]]),
        "col_bias": np.stack([A[n].reshape(KC, P) for n in (L0 + "wq_b", L0 + "wk_b", L2 + "bq", L2 + "bk", L3 + "b1")]).transpose(2, 0, 1),
        "w0q": kc(A[L0 + "wq_w"].T), "w0k": kc(A[L0 + "wk_w"].T), "w0v": kc(A[L0 + "wv_w"].T), "w0o": kc(A[L0 + "out_w"].T),
        "w3q2": kc(A[L2 + "Wq"]), "w3k2": kc(A[L2 + "Wk"]), "w3v2": kc(A[L2 + "Wv"]), "w3o2": kc(A[L2 + "Wo"]),
        "w3k3": kc(A[L3 + "Wk1"]), "w3q3": kc(A[L3 + "Wq1"]), "w3v3": kc(A[L3 + "Wv1"]),
        "w3k4": kc(A[L3 + "Wk2"]), "w3q4": kc(A[L3 + "Wq2"]), "w3v4": kc(A[L3 + "Wv2"]),
        "w3h": kc(A[L3 + "W1"]), "w3ff": kc(A[L3 + "W2"]),
    }
    F = "L0_ffn_"
    gate = np.concatenate([A[F + "w1"], A[F + "sw1"].T.reshape(D, 2, HID0).transpose(1, 0, 2)])
    up = np.concatenate([A[F + "w3"], A[F + "sw3"].T.reshape(D, 2, HID0).transpose(1, 0, 2)])
    down = np.concatenate([A[F + "w2"], A[F + "sw2"].T.reshape(2, HID0, D)])
    w13 = np.stack([gate, up], axis=1).transpose(2, 0, 1, 3).reshape(D, E0 * 2 * HID0)
    arrays["w13"] = kc(w13)
    arrays["w2"] = down.transpose(1, 0, 2)

    def experts(gate, up, down):
        hid = gate.shape[2]
        gu = np.concatenate([gate, up], axis=2).reshape(E, KC, P, 2 * hid).transpose(0, 2, 1, 3).reshape(E, P, -1)
        dn = down.reshape(E, hid // P, P, D).transpose(0, 2, 1, 3).reshape(E, P, -1)
        return np.concatenate([gu, dn], axis=2)

    tr = lambda a: a.transpose(0, 2, 1)
    arrays["moe1"] = experts(A[L1 + "kernel_gating_EDF"], A[L1 + "kernel_up_EDF"], A[L1 + "kernel_down_EFD"])
    arrays["moe3"] = experts(tr(A["L3_ffn_w1"]), tr(A["L3_ffn_w3"]), tr(A["L3_ffn_w2"]))
    arrays = {n: np.ascontiguousarray(a) for n, a in arrays.items()}
    nc = bacc.Bacc("TRN2", target_bir_lowering=False, num_devices=1)
    ins = {n: nc.dram_tensor(f"in_{n}", a.shape, mybir.dt.from_np(a.dtype), kind="ExternalInput").ap() for n, a in arrays.items()}
    out = nc.dram_tensor("out_x", _OUT_SHAPE, F32, kind="ExternalOutput").ap()
    build(nc, ins, out)
    r = run_bass_kernel_spmd(nc, [{f"in_{n}": a for n, a in arrays.items()}], core_ids=[0])
    return np.roll(r.results[0]["out_x"], T, axis=0)
```
